# Optimizing a Trainium2 kernel written in Bass

```python
import numpy as np
import jax
import jax.numpy as jnp

def _softmax(x, axis=-1):
    return jax.nn.softmax(x, axis=axis)

def _gelu(x):
    return jax.nn.gelu(x, approximate=True)

def _silu(x):
    return jax.nn.silu(x)

def _sigmoid(x):
    return jax.nn.sigmoid(x)

def _layernorm(x, axis=-1, eps=1e-05):
    m = jnp.mean(x, axis=axis, keepdims=True)
    v = jnp.var(x, axis=axis, keepdims=True)
    return (x - m) / jnp.sqrt(v + eps)

def _scatter_add(tgt, idx, src, axis=0):
    return tgt.at[idx].add(src)

def _segment_sum(src, seg, n):
    return jax.ops.segment_sum(src, seg, n)
kernel_name = 'mk_seq_preln_d1_jaxref_r8_88c9b0'

def setup_inputs(seed: int=0):
    np.random.seed(seed)
    _w = jnp.asarray

    def _L0_attn_setup():
        import math
        import jax, jax.numpy as jnp
        from jax import lax
        import numpy as np
        D_MODEL = 256
        N_HEADS = 16
        HEAD_DIM = 128
        INNER = N_HEADS * HEAD_DIM
        KCONV = 4
        B, N = (2, 256)

        def _l2_normalize(t, eps=1e-12):
            nrm = jnp.sqrt(jnp.sum(t * t, axis=-1, keepdims=True))
            return t / jnp.maximum(nrm, eps)

        def _short_conv(z, conv_w):
            C, K = conv_w.shape
            zc = jnp.transpose(z, (0, 2, 1))
            kern = conv_w[:, None, :]
            out = lax.conv_general_dilated(zc, kern, window_strides=(1,), padding=[(K - 1, 0)], dimension_numbers=('NCH', 'OIH', 'NCH'), feature_group_count=C)
            return jax.nn.silu(jnp.transpose(out, (0, 2, 1)))
        key = jax.random.key(seed)
        ks = jax.random.split(key, 7)
        x = jax.random.normal(ks[0], (B, N, D_MODEL), dtype=jnp.float32)
        W_qkv = jax.random.normal(ks[1], (3 * INNER, D_MODEL), dtype=jnp.float32) * 0.02
        conv_w = jax.random.normal(ks[2], (3 * INNER, KCONV), dtype=jnp.float32) * 0.2
        W_ab = jax.random.normal(ks[3], (2 * N_HEADS, D_MODEL), dtype=jnp.float32) * 0.02
        b_ab = jnp.concatenate([jnp.full((N_HEADS,), math.log(0.98 / 0.02), dtype=jnp.float32), jnp.zeros((N_HEADS,), dtype=jnp.float32)])
        W_g = jax.random.normal(ks[4], (INNER, D_MODEL), dtype=jnp.float32) * 0.02
        W_o = jax.random.normal(ks[5], (D_MODEL, INNER), dtype=jnp.float32) * 0.02
        return {'x': x, 'W_qkv': W_qkv, 'conv_w': conv_w, 'W_ab': W_ab, 'b_ab': b_ab, 'W_g': W_g, 'W_o': W_o}
    _L0_attn_in = _L0_attn_setup()

    def _L0_ffn_setup():
        import jax, jax.numpy as jnp
        import numpy as np
        E, K = (12, 3)
        B, S, H, I = (2, 256, 256, 640)

        def _forward(x, Wr, br, w1, b1, w2, b2, Wp1, bp1, Wp2, bp2):
            logits = jnp.einsum('bsh,he->bse', x, Wr) + br
            probs = jax.nn.softmax(logits, axis=-1)
            top_vals, top_idx = jax.lax.top_k(probs, K)
            ew = jax.nn.softmax(top_vals, axis=-1)
            out = jnp.zeros_like(x)
            for e in range(E):
                sel = top_idx == e
                mask = sel.any(axis=-1)
                cnt = sel.sum()
                w_e = jnp.sum(jnp.where(sel, ew, 0.0)) / jnp.maximum(cnt, 1).astype(ew.dtype)
                h = jax.nn.relu(jnp.einsum('bsh,hi->bsi', x, w1[e]) + b1[e])
                h = jnp.einsum('bsi,ih->bsh', h, w2[e]) + b2[e]
                out = out + mask[..., None].astype(x.dtype) * (w_e * h)
            pooled = out.mean(axis=1)
            phi = jax.nn.sigmoid(jax.nn.relu(pooled @ Wp1 + bp1) @ Wp2 + bp2)
            phi_mask = (phi > 0.7).astype(out.dtype)[:, :, None]
            return out * (1.0 - phi_mask * 0.8)
        key = jax.random.key(seed)
        ks = jax.random.split(key, 8)
        sH = np.float32(1.0 / np.sqrt(H))
        sI = np.float32(1.0 / np.sqrt(I))
        sH2 = np.float32(1.0 / np.sqrt(H // 2))
        return {'hidden_states': jax.random.normal(ks[0], (B, S, H), jnp.float32), 'Wr': jax.random.normal(ks[1], (H, E), jnp.float32) * sH, 'br': jnp.zeros((E,), jnp.float32), 'w1': jax.random.normal(ks[2], (E, H, I), jnp.float32) * sH, 'b1': jnp.zeros((E, I), jnp.float32), 'w2': jax.random.normal(ks[3], (E, I, H), jnp.float32) * sI, 'b2': jnp.zeros((E, H), jnp.float32), 'Wp1': jax.random.normal(ks[4], (H, H // 2), jnp.float32) * sH, 'bp1': jnp.zeros((H // 2,), jnp.float32), 'Wp2': jax.random.normal(ks[5], (H // 2, 1), jnp.float32) * sH2, 'bp2': jnp.zeros((1,), jnp.float32)}
    _L0_ffn_in = _L0_ffn_setup()
    _d = {'L0_attn_x': _L0_attn_in['x'], 'L0_attn_W_qkv': _L0_attn_in['W_qkv'], 'L0_attn_conv_w': _L0_attn_in['conv_w'], 'L0_attn_W_ab': _L0_attn_in['W_ab'], 'L0_attn_b_ab': _L0_attn_in['b_ab'], 'L0_attn_W_g': _L0_attn_in['W_g'], 'L0_attn_W_o': _L0_attn_in['W_o'], 'L0_ffn_Wr': _L0_ffn_in['Wr'], 'L0_ffn_br': _L0_ffn_in['br'], 'L0_ffn_w1': _L0_ffn_in['w1'], 'L0_ffn_b1': _L0_ffn_in['b1'], 'L0_ffn_w2': _L0_ffn_in['w2'], 'L0_ffn_b2': _L0_ffn_in['b2'], 'L0_ffn_Wp1': _L0_ffn_in['Wp1'], 'L0_ffn_bp1': _L0_ffn_in['bp1'], 'L0_ffn_Wp2': _L0_ffn_in['Wp2'], 'L0_ffn_bp2': _L0_ffn_in['bp2']}
    _x0 = _d['L0_attn_x']
    _d['L0_attn_x'] = jax.random.normal(jax.random.fold_in(jax.random.key(seed), 1), (2, 512, 256), dtype=_x0.dtype)
    del _x0
    return _d

def reference(L0_attn_x, L0_attn_W_qkv, L0_attn_conv_w, L0_attn_W_ab, L0_attn_b_ab, L0_attn_W_g, L0_attn_W_o, L0_ffn_Wr, L0_ffn_br, L0_ffn_w1, L0_ffn_b1, L0_ffn_w2, L0_ffn_b2, L0_ffn_Wp1, L0_ffn_bp1, L0_ffn_Wp2, L0_ffn_bp2):

    def _L0_attn_ref(x, W_qkv, conv_w, W_ab, b_ab, W_g, W_o):
        import math
        import jax, jax.numpy as jnp
        from jax import lax
        import numpy as np
        D_MODEL = 256
        N_HEADS = 16
        HEAD_DIM = 128
        INNER = N_HEADS * HEAD_DIM
        KCONV = 4
        B, N = (2, 256)

        def _l2_normalize(t, eps=1e-12):
            nrm = jnp.sqrt(jnp.sum(t * t, axis=-1, keepdims=True))
            return t / jnp.maximum(nrm, eps)

        def _short_conv(z, conv_w):
            C, K = conv_w.shape
            zc = jnp.transpose(z, (0, 2, 1))
            kern = conv_w[:, None, :]
            out = lax.conv_general_dilated(zc, kern, window_strides=(1,), padding=[(K - 1, 0)], dimension_numbers=('NCH', 'OIH', 'NCH'), feature_group_count=C)
            return jax.nn.silu(jnp.transpose(out, (0, 2, 1)))
        Bq, Nq, _ = x.shape
        H = b_ab.shape[0] // 2
        inner = W_g.shape[0]
        D = inner // H
        qkv = jnp.einsum('bnd,ed->bne', x, W_qkv)
        qkv = _short_conv(qkv, conv_w)
        q, k, v = jnp.split(qkv, 3, axis=-1)
        to_heads = lambda t: t.reshape(Bq, Nq, H, D).transpose(0, 2, 1, 3)
        q, k, v = (to_heads(q), to_heads(k), to_heads(v))
        q = _l2_normalize(q)
        k = _l2_normalize(k)
        ab = jnp.einsum('bnd,ed->bne', x, W_ab) + b_ab
        alpha = jax.nn.sigmoid(ab[..., :H]).transpose(0, 2, 1)
        beta = jax.nn.sigmoid(ab[..., H:]).transpose(0, 2, 1)
        q_s = q.transpose(2, 0, 1, 3)
        k_s = k.transpose(2, 0, 1, 3)
        v_s = v.transpose(2, 0, 1, 3)
        a_s = alpha.transpose(2, 0, 1)
        b_s = beta.transpose(2, 0, 1)
        S0 = jnp.zeros((Bq, H, D, D), dtype=x.dtype)

        def step(S, inp):
            q_t, k_t, v_t, a_t, b_t = inp
            Sk = jnp.einsum('bhde,bhe->bhd', S, k_t)
            u = b_t[..., None] * (v_t - a_t[..., None] * Sk)
            S = a_t[..., None, None] * S + u[..., :, None] * k_t[..., None, :]
            o = jnp.einsum('bhde,bhe->bhd', S, q_t)
            return (S, o)
        _, o = lax.scan(step, S0, (q_s, k_s, v_s, a_s, b_s))
        out = o.transpose(1, 0, 2, 3).reshape(Bq, Nq, inner)
        g = jax.nn.silu(jnp.einsum('bnd,ed->bne', x, W_g))
        out = out * g
        y = jnp.einsum('bne,de->bnd', out, W_o)
        return y

    def _L0_ffn_ref(hidden_states, Wr, br, w1, b1, w2, b2, Wp1, bp1, Wp2, bp2):
        import jax, jax.numpy as jnp
        import numpy as np
        E, K = (12, 3)
        B, S, H, I = (2, 256, 256, 640)

        def _forward(x, Wr, br, w1, b1, w2, b2, Wp1, bp1, Wp2, bp2):
            logits = jnp.einsum('bsh,he->bse', x, Wr) + br
            probs = jax.nn.softmax(logits, axis=-1)
            top_vals, top_idx = jax.lax.top_k(probs, K)
            ew = jax.nn.softmax(top_vals, axis=-1)
            out = jnp.zeros_like(x)
            for e in range(E):
                sel = top_idx == e
                mask = sel.any(axis=-1)
                cnt = sel.sum()
                w_e = jnp.sum(jnp.where(sel, ew, 0.0)) / jnp.maximum(cnt, 1).astype(ew.dtype)
                h = jax.nn.relu(jnp.einsum('bsh,hi->bsi', x, w1[e]) + b1[e])
                h = jnp.einsum('bsi,ih->bsh', h, w2[e]) + b2[e]
                out = out + mask[..., None].astype(x.dtype) * (w_e * h)
            pooled = out.mean(axis=1)
            phi = jax.nn.sigmoid(jax.nn.relu(pooled @ Wp1 + bp1) @ Wp2 + bp2)
            phi_mask = (phi > 0.7).astype(out.dtype)[:, :, None]
            return out * (1.0 - phi_mask * 0.8)
        return _forward(hidden_states, Wr, br, w1, b1, w2, b2, Wp1, bp1, Wp2, bp2)
    x = L0_attn_x
    x = x + _L0_attn_ref(_layernorm(x, axis=-1), L0_attn_W_qkv, L0_attn_conv_w, L0_attn_W_ab, L0_attn_b_ab, L0_attn_W_g, L0_attn_W_o)
    x = x + _L0_ffn_ref(_layernorm(x, axis=-1), L0_ffn_Wr, L0_ffn_br, L0_ffn_w1, L0_ffn_b1, L0_ffn_w2, L0_ffn_b2, L0_ffn_Wp1, L0_ffn_bp1, L0_ffn_Wp2, L0_ffn_bp2)
    return x

_drawn_inputs = setup_inputs


def setup_inputs(seed=0):
    import zlib

    import numpy as np

    out = dict(_drawn_inputs(seed))
    spreads = {'L0_ffn_br': (0.0, 0.1),
     'L0_ffn_b1': (0.0, 0.1),
     'L0_ffn_b2': (0.0, 0.1),
     'L0_ffn_bp1': (0.0, 0.1)}
    factors = {'L0_attn_W_qkv': 2.726,
     'L0_attn_conv_w': 3.287,
     'L0_attn_W_ab': 6.066,
     'L0_attn_b_ab': 3.579,
     'L0_attn_W_g': 3.353}
    for name, (base, spread) in spreads.items():
        noise = np.random.default_rng([zlib.crc32(name.encode()), seed]).standard_normal(out[name].shape)
        drawn = base * np.exp(spread * noise) if base else spread * noise
        out[name] = jnp.asarray(drawn.astype(out[name].dtype))
    for name, factor in factors.items():
        out[name] = (out[name] * factor).astype(out[name].dtype)
    return out
```

```python
from contextlib import ExitStack

import numpy as np

import concourse.bass as bass
from concourse import mybir

F32 = mybir.dt.float32
U32 = mybir.dt.uint32
ALU = mybir.AluOpType
ACT = mybir.ActivationFunctionType
AX = mybir.AxisListType

P = 128
B, SEQ, D = 2, 512, 256
TOK = B * SEQ
NT = TOK // P
NC = SEQ // P
KD = D // P
HEADS = 16
TAPS = 4
HG = 4
GROUPS = HEADS // HG
M = HG * NT
BLK = 32
NB = P // BLK
E, TOPK, I = 12, 3, 640
KI = I // P
LN_EPS = 1e-5
NORM_EPS2 = 1e-24

STREAMS = HG * B
SLOTS = NC * STREAMS


def block_kernel(nc, x, wqkvg, convw, wab, bab, wo, wr, br, w1, b1, w2, b2, wp1, bp1, wp2, bp2, out):
    with ExitStack() as ctx:
        def sb(name, shape, dt=F32):
            return ctx.enter_context(nc.sbuf_tensor(name, shape, dt))

        def sem(name):
            return ctx.enter_context(nc.semaphore(name))

        bank = [ctx.enter_context(nc.psum_tensor(f"bank{i}", [P, 512], F32)) for i in range(8)]

        decay_dram = nc.dram_tensor("decay_rows", [HEADS, TOK], F32).ap()
        chunk_decay_dram = nc.dram_tensor("chunk_decay_rows", [HEADS, NT], F32).ap()
        lower_dram = nc.dram_tensor("lower_blocks", [NB, M, BLK, BLK], F32).ap()
        invT_dram = nc.dram_tensor("inverse_blocks_t", [NB, M, BLK, BLK], F32).ap()
        inv_dram = nc.dram_tensor("inverse_blocks", [NB, M, BLK, BLK], F32).ap()

        resid = sb("resid", [P, NT, D])
        normedT = sb("normedT", [P, KD, TOK])
        ident = sb("ident", [P, P])
        ones = sb("ones", [P, P])
        stats = sb("stats", [P, NT, 6])
        mean_var = sb("mean_var", [P, NT, 2])
        rstd = sb("rstd", [P, NT])
        eps_col = sb("eps_col", [P, 1])

        wab_sb = sb("wab_sb", [P, KD, 2 * HEADS])
        bab_sb = sb("bab_sb", [P, 2 * HEADS])
        alpha_beta = sb("alpha_beta", [P, NT, 2 * HEADS])
        decay_from_start = sb("decay_from_start", [P, NT, HEADS])
        neg_decay = sb("neg_decay", [P, NT, HEADS])
        chunk_decay = sb("chunk_decay", [P, HEADS, NT])

        qT = sb("qT", [P, HG, TOK])
        kT = sb("kT", [P, HG, TOK])
        gated = sb("gated", [P, HG, TOK])
        vk = sb("vk", [P, 2, HG, NT, P])
        masks = sb("masks", [P, M, 2, P])
        invT = sb("invT", [P, M, P])
        inv_low = sb("inv_low", [P, M, 64])
        inv64 = inv_low[0:64, :, :]
        inv32 = inv_low[64:96, :, 0:BLK]
        state = sb("state", [P, STREAMS, P])
        qk_scales = sb("qk_scales", [P, HG, NT, 4])
        w_sb = sb("w_sb", [P, 2, KD, 4, P])
        cw_sb = sb("cw_sb", [P, 2, 3, TAPS])
        decay_bc = sb("decay_bc", [P, B, SEQ])
        wo_sb = sb("wo_sb", [P, HG, D])
        conv = sb("conv", [P, 2, 512])
        conv_far = sb("conv_far", [P, 2, 512])
        vT = sb("vT", [P, 512])
        squares = sb("squares", [P, 512])
        decayed = sb("decayed", [P, NC, P])
        norms = sb("norms", [P, 2, 8])
        half = sb("half", [P, 8])
        rhs_sb = sb("rhs_sb", [P, 2, P])
        y_sb = sb("y_sb", [P, 2, P])
        o_sb = sb("o_sb", [P, 2, P])
        blocks = sb("blocks", [P, 2, BLK, BLK])
        sub_in, sub_inv = blocks[:, 0, :, :], blocks[:, 1, :, :]
        cross = blocks[:, :, :, :].rearrange("p a b c -> p (a b c)").rearrange("p (m t) -> p m t", m=M)
        sub_tmp = sb("sub_tmp", [P, 256])

        qT_flat = qT[:, :, :].rearrange("p a b -> p (a b)")
        kT_flat = kT[:, :, :].rearrange("p a b -> p (a b)")
        alpha_rows = qT[0:HEADS, 0, :]
        reset_rows = qT[0:HEADS, 1, :]
        impulse_rows = qT[0:HEADS, 2, :]
        decay_rows = qT[0:HEADS, 3, :]
        chunk_end_rows = kT[0:HEADS, 0, 0:NT]
        w1_sb = [v[:, 0:KD * I].rearrange("p (k i) -> p k i", k=KD) for v in (qT_flat, kT_flat)]
        w2_sb = [v[:, KD * I:KD * I + KI * D].rearrange("p (k d) -> p k d", k=KI) for v in (qT_flat, kT_flat)]
        hT = [masks[:, :, :, :].rearrange("p m a t -> p (m a t)")[:, 0:KI * TOK].rearrange("p (k t) -> p k t", k=KI),
              vk[:, :, :, :, :].rearrange("p a h n t -> p (a h n t)")[:, 0:KI * TOK].rearrange("p (k t) -> p k t", k=KI)]
        gated_flat = gated[:, :, :].rearrange("p h t -> p (h t)")
        acc = gated_flat[:, 0:NT * D].rearrange("p (n d) -> p n d", n=NT)
        normed = gated_flat[:, NT * D:2 * NT * D].rearrange("p (n d) -> p n d", n=NT)
        small = invT[:, :, :].rearrange("p m t -> p (m t)")

        def carve():
            at = [0]

            def take(*shape):
                n = int(np.prod(shape))
                v = small[:, at[0]:at[0] + n]
                at[0] += n
                if len(shape) == 2:
                    v = v.rearrange("p (a b) -> p a b", a=shape[0])
                return v
            return take

        take = carve()
        wr_sb, br_sb = take(KD, E), take(E)
        b1_sb, b2_sb = take(E, KI), take(D)
        wp1_sb, bp1_sb, wp2_sb, bp2_sb = take(KD, P), take(1), take(1), take(1)
        wp2_bc = take(P)
        expert_no = take(E)
        logits, probs = take(NT, E), take(NT, E)
        row_max, row_sum, row_inv = take(NT), take(NT), take(NT)
        top8, top_no, top_w = take(NT, 8), take(NT, 8), take(NT, TOPK)
        top_sum = take(NT)
        picked = take(NT, 2 * E)
        pick_one = take(NT, E)
        pick_sum, expert_w = take(2 * E), take(2 * E)
        token_w = take(NT, E)
        token_wT = take(TOK)
        pooled, hidden, phi = take(2 * KD), take(B), take(B)
        top_idx = ctx.enter_context(nc.sbuf_tensor("top_idx", [P, NT, 8], U32))

        def layernorm(dve, step):
            for n in range(NT):
                s = nc.vector.bn_stats(stats[:, n, :], resid[:, n, :])
            step(s)
            for n in range(NT):
                s = nc.vector.bn_aggr(mean_var[:, n, :], stats[:, n, :])
            return s

        def apply_norm(dve, step):
            step(nc.vector.reciprocal(rstd[:, :], rstd[:, :]))
            for n in range(NT):
                s = nc.vector.tensor_scalar(normed[:, n, :], resid[:, n, :], mean_var[:, n, 0:1], rstd[:, n:n + 1],
                                            ALU.subtract, ALU.mult)
            return s

        def wait_alone(eng, what, value):
            value = eng.to_reg(value)
            eng.wait_ge(consts, 9)
            eng.wait_ge(what, value)

        in_x, in_small = sem("in_x"), sem("in_small")
        consts, var_ready, std_ready, normed_ready = sem("consts"), sem("var_ready"), sem("std_ready"), sem("normed_ready")
        turned, turned_sb = sem("turned"), sem("turned_sb")
        ab_ready, ab_z, ab_exp, ab_sig = sem("ab_ready"), sem("ab_z"), sem("ab_exp"), sem("ab_sig")
        rows_ready, rows_sb, decay_cols, chunk_in = sem("rows_ready"), sem("rows_sb"), sem("decay_cols"), sem("chunk_in")
        dram_rows, decay_sb = sem("dram_rows"), sem("decay_sb")
        step1 = sem("step1")

        with nc.Block() as block:
            @block.sync
            def _(sp):
                sp.dma_start(resid[:, :, :], x.rearrange("(n p) d -> p n d", p=P)).then_inc(in_x, 16)
                sp.dma_start(wab_sb[:, :, :], wab).then_inc(in_small, 16)
                sp.dma_start(bab_sb[:, :], bab.partition_broadcast(P)).then_inc(in_small, 16)
                sp.wait_ge(rows_sb, 3)
                sp.dma_start(decay_dram, reset_rows).then_inc(dram_rows, 16)
                sp.dma_start(chunk_decay_dram, chunk_end_rows).then_inc(dram_rows, 16)
                sp.wait_ge(dram_rows, 32)
                sp.dma_start(chunk_decay[:, :, :], chunk_decay_dram.partition_broadcast(P)).then_inc(chunk_in, 16)
                sp.wait_ge(chunk_in, 16)

            @block.gpsimd
            def _(pool):
                nc.gpsimd.memset(ident[:, :], 0.0).then_inc(consts, 1)
                nc.gpsimd.memset(ones[:, :], 1.0).then_inc(consts, 1)
                nc.gpsimd.memset(eps_col[:, :], LN_EPS).then_inc(consts, 1)
                nc.gpsimd.memset(half[:, :], 0.5).then_inc(consts, 1)
                nc.gpsimd.memset(conv_far[:, :, :], 0.0).then_inc(consts, 1)
                nc.gpsimd.memset(invT[:, :, :], 0.0).then_inc(consts, 1)
                nc.gpsimd.memset(inv_low[:, :, :], 0.0).then_inc(consts, 1)
                nc.gpsimd.memset(impulse_rows, 0.0).then_inc(consts, 1)
                pool.wait_ge(consts, 8)
                nc.gpsimd.affine_select(out=ident[:, :], in_=ident[:, :], compare_op=ALU.not_equal, fill=1.0,
                                        base=0, pattern=[[-1, P]], channel_multiplier=1).then_inc(consts, 1)

            @block.vector
            def _(dve):
                count = [0]

                def step(ins):
                    count[0] += 1
                    ins.then_inc(step1, 1)
                    dve.wait_ge(step1, count[0])

                dve.wait_ge(in_x, 16)
                layernorm(dve, step).then_inc(var_ready, 1)
                dve.wait_ge(std_ready, 1)
                apply_norm(dve, step).then_inc(normed_ready, 1)
                for k in range(4):
                    dve.wait_ge(turned, k + 1)
                    nc.vector.tensor_copy(normedT[:, k // 2, (k % 2) * 512:(k % 2 + 1) * 512], bank[k][:, :]).then_inc(turned_sb, 1)
                dve.wait_ge(ab_ready, 1)
                dve.wait_ge(in_small, 32)
                nc.vector.tensor_tensor(alpha_beta[:, :, :], bank[4][:, 0:NT * 32].rearrange("p (n h) -> p n h", n=NT),
                                        bab_sb[:, :].unsqueeze(1).to_broadcast([P, NT, 32]), ALU.add).then_inc(ab_z, 1)
                dve.wait_ge(ab_exp, 1)
                step(nc.vector.tensor_scalar(alpha_beta[:, :, :], alpha_beta[:, :, :], 1.0, None, ALU.add))
                nc.vector.reciprocal(alpha_beta[:, :, :], alpha_beta[:, :, :]).then_inc(ab_sig, 1)
                dve.wait_ge(rows_ready, 1)
                for k in range(2):
                    s = nc.vector.tensor_copy(qT[0:HEADS, 0, k * 512:(k + 1) * 512], bank[5 + k][0:HEADS, :])
                step(s)
                dve.wait_ge(consts, 9)
                start = lambda v: v.rearrange("h (n t) -> h n t", n=NT)[:, :, 0:1]
                nc.vector.tensor_copy(start(impulse_rows), start(alpha_rows))
                step(nc.vector.tensor_copy(reset_rows, alpha_rows))
                s = nc.vector.memset(start(reset_rows), 0.0)
                s.then_inc(rows_sb, 1)
                dve.wait_ge(rows_sb, 1)
                nc.vector.tensor_tensor_scan(decay_rows, reset_rows, impulse_rows, 0.0, ALU.mult, ALU.add).then_inc(rows_sb, 1)
                dve.wait_ge(rows_sb, 2)
                nc.vector.tensor_copy(chunk_end_rows.unsqueeze(2),
                                      decay_rows.rearrange("h (n t) -> h n t", n=NT)[:, :, P - 1:P]).then_inc(rows_sb, 1)
                dve.wait_ge(decay_cols, 1)
                v = bank[7][:, 0:NT * HEADS].rearrange("p (n h) -> p n h", n=NT)
                nc.vector.tensor_copy(decay_from_start[:, :, :], v)
                nc.vector.tensor_scalar(neg_decay[:, :, :], v, -1.0, None, ALU.mult)

            @block.scalar
            def _(act):
                act.wait_ge(consts, 9)
                act.wait_ge(var_ready, 1)
                nc.scalar.activation(rstd[:, :].unsqueeze(2), mean_var[:, :, 1:2], ACT.Sqrt, bias=eps_col[:, :]).then_inc(std_ready, 1)
                act.wait_ge(ab_z, 1)
                nc.scalar.activation(alpha_beta[:, :, :], alpha_beta[:, :, :], ACT.Exp, scale=-1.0).then_inc(ab_exp, 1)

            @block.tensor
            def _(pe):
                pe.wait_ge(consts, 9)
                pe.wait_ge(normed_ready, 1)
                for k in range(KD):
                    for n in range(NT):
                        b_no = 2 * k + n // 4
                        s = nc.tensor.transpose(bank[b_no][:, (n % 4) * P:(n % 4 + 1) * P], normed[:, n, k * P:(k + 1) * P],
                                                ident[:, :])
                        if n % 4 == 3:
                            s.then_inc(turned, 1)
                pe.wait_ge(turned_sb, 4)
                pe.wait_ge(in_small, 32)
                for n in range(NT):
                    for k in range(KD):
                        s = nc.tensor.matmul(bank[4][:, n * 32:(n + 1) * 32], normedT[:, k, n * P:(n + 1) * P], wab_sb[:, k, :],
                                             start=k == 0, stop=k == KD - 1)
                s.then_inc(ab_ready, 1)
                pe.wait_ge(ab_sig, 1)
                for n in range(NT):
                    s = nc.tensor.transpose(bank[5 + n // 4][0:HEADS, (n % 4) * P:(n % 4 + 1) * P],
                                            alpha_beta[:, n, 0:HEADS], ident[:, :])
                s.then_inc(rows_ready, 1)
                pe.wait_ge(rows_sb, 2)
                for n in range(NT):
                    s = nc.tensor.transpose(bank[7][:, n * HEADS:(n + 1) * HEADS], decay_rows[:, n * P:(n + 1) * P],
                                            ident[0:HEADS, 0:HEADS])
                s.then_inc(decay_cols, 1)

        w_in = [sem("w_in_even"), sem("w_in_odd")]
        wo_in = sem("wo_in")
        decay_in = [sem("decay_in_b0"), sem("decay_in_b1")]
        proj_done = sem("proj_done")
        far_done = sem("far_done")
        near_done = sem("near_done")
        conv_done = sem("conv_done")
        silu_done = sem("silu_done")
        squared = sem("squared")
        sums_done = sem("sums_done")
        sums_read = sem("sums_read")
        rooted = sem("rooted")
        scaled = sem("scaled")
        impulses = sem("impulses")
        turned_v, turned_k = sem("turned_v"), sem("turned_k")
        products = sem("products")
        post_v, post_k, post_m = sem("post_v"), sem("post_k"), sem("post_m")
        blocks_out, blocks_in = sem("blocks_out"), sem("blocks_in")
        cleared = sem("cleared")
        inverted = sem("inverted")
        inverse_t = sem("inverse_t")
        inv_out, inv_in = sem("inv_out"), sem("inv_in")
        merge_mm, merge_ev = sem("merge_mm"), sem("merge_ev")
        ks_done, rhs_done, y_done, y_copied = sem("ks_done"), sem("rhs_done"), sem("y_done"), sem("y_copied")
        upd_done, intra_done, o_done, state_done = sem("upd_done"), sem("intra_done"), sem("o_done"), sem("state_done")
        o_turned, o_gated = sem("o_turned"), sem("o_gated")
        wo_done, wo_added = sem("wo_done"), sem("wo_added")
        step2 = sem("step2")

        PAIRS = HG * B
        STEP_PER = [0]

        def tokens(b, c=None):
            return slice(b * SEQ, (b + 1) * SEQ) if c is None else slice(b * SEQ + c * P, b * SEQ + (c + 1) * P)

        with nc.Block() as block:
            @block.sync
            def _(sp):

                with sp.Fori(0, GROUPS) as g:
                    for hh in range(HG):
                        sp.wait_ge(post_m, g * 2 * PAIRS + 2 * B * max(hh - 1, 0))
                        par = hh % 2
                        sp.dma_start(w_sb[:, par, :, :, :], wqkvg[bass.ds(g * HG + hh, 1)].squeeze(0)).then_inc(w_in[par], 16)
                        sp.dma_start(cw_sb[:, par, :, :], convw[bass.ds(g * HG + hh, 1)].squeeze(0)).then_inc(w_in[par], 16)
                        for b in range(B):
                            sp.wait_ge(post_k, g * PAIRS + max(2 * hh + b - 1, 0))
                            sp.dma_start(decay_bc[:, b, :], decay_dram[bass.ds(g * HG + hh, 1), b * SEQ:(b + 1) * SEQ].squeeze(0).partition_broadcast(P)).then_inc(decay_in[b], 16)
                    sp.wait_ge(wo_added, g * 4)
                    sp.dma_start(wo_sb[:, :, :], wo[bass.ds(g * HG, HG)].rearrange("h e d -> e h d")).then_inc(wo_in, 16)
                    sp.wait_ge(post_m, g * 2 * PAIRS + 2 * PAIRS)
                    for i in range(NB):
                        sp.dma_start(lower_dram[i].rearrange("m j t -> j m t"),
                                     masks[i * BLK:(i + 1) * BLK, :, 0, i * BLK:(i + 1) * BLK]).then_inc(blocks_out, 16)
                    sp.wait_ge(blocks_out, g * 64 + 64)
                    sp.dma_start(sub_in, lower_dram.rearrange("i m j t -> (i m) j t")).then_inc(blocks_in, 16)
                    sp.wait_ge(inverted, g + 1)
                    sp.dma_start(invT_dram.rearrange("i m j t -> (i m) j t"), sub_inv).then_inc(inv_out, 16)
                    sp.wait_ge(inverse_t, g + 1)
                    sp.dma_start(inv_dram.rearrange("i m j t -> (i m) j t"), sub_in).then_inc(inv_out, 16)
                    sp.wait_ge(inv_out, g * 32 + 32)
                    for i in range(NB):
                        sp.dma_start(invT[i * BLK:(i + 1) * BLK, :, i * BLK:(i + 1) * BLK],
                                     invT_dram[i].rearrange("m j t -> j m t")).then_inc(inv_in, 16)
                    for i in range(2):
                        sp.dma_start(inv64[i * BLK:(i + 1) * BLK, :, i * BLK:(i + 1) * BLK],
                                     inv_dram[i].rearrange("m j t -> j m t")).then_inc(inv_in, 16)
                    sp.dma_start(inv32, inv_dram[2].rearrange("m j t -> j m t")).then_inc(inv_in, 16)
                    wait_alone(sp, inv_in, g * 112 + 112)

            @block.tensor
            def _(pe):
                with pe.Fori(0, GROUPS) as g:
                    def project(p):
                        hh, b = divmod(p, B)
                        if b == 0:
                            pe.wait_ge(w_in[hh % 2], g * 64 + 32 * (hh // 2 + 1))
                        for typ in range(4):
                            if typ < 3:
                                pe.wait_ge(conv_done, g * 3 * PAIRS + max(3 * (p - 1) + typ + 1, 0))
                            else:
                                pe.wait_ge(silu_done, g * 4 * PAIRS + 4 * p)
                            for k in range(KD):
                                s = nc.tensor.matmul(bank[typ][:, :], w_sb[:, hh % 2, k, typ, :], normedT[:, k, tokens(b)],
                                                     start=k == 0, stop=k == KD - 1)
                            s.then_inc(proj_done, 1)

                    def finish(p):
                        hh, b = divmod(p, B)
                        pe.wait_ge(silu_done, g * 4 * PAIRS + 4 * p + 3)
                        pe.wait_ge(post_v, g * PAIRS + p)
                        for c in range(NC):
                            s = nc.tensor.transpose(bank[5][:, c * P:(c + 1) * P], vT[:, c * P:(c + 1) * P], ident[:, :])
                        s.then_inc(turned_v, 1)
                        pe.wait_ge(post_k, g * PAIRS + p)
                        for qk in range(2):
                            pe.wait_ge(squared, g * 2 * PAIRS + 2 * p + qk + 1)
                            for c in range(NC):
                                s = nc.tensor.matmul(bank[4][:, qk * NC + c:qk * NC + c + 1], squares[:, c * P:(c + 1) * P],
                                                     ones[:, 0:1], start=True, stop=True)
                            s.then_inc(sums_done, 1)
                        for c in range(NC):
                            if c % 2 == 0:
                                pe.wait_ge(post_m, g * 2 * PAIRS + max(2 * (p - 1) + c // 2 + 1, 0))
                            o = bank[6 + c // 2][:, (c % 2) * 2 * P:(c % 2 + 1) * 2 * P]
                            kk = kT[:, hh, tokens(b, c)]
                            nc.tensor.matmul(o[:, 0:P], kk, kk, start=True, stop=True)
                            s = nc.tensor.matmul(o[:, P:2 * P], kk, qT[:, hh, tokens(b, c)], start=True, stop=True)
                            if c % 2 == 1:
                                s.then_inc(products, 1)
                        pe.wait_ge(sums_read, g * PAIRS + p + 1)
                        for c in range(NC):
                            s = nc.tensor.transpose(bank[4][:, c * P:(c + 1) * P], kT[:, hh, tokens(b, c)], ident[:, :])
                        s.then_inc(turned_k, 1)

                    for p in range(PAIRS + 1):
                        if p < PAIRS:
                            project(p)
                        if p > 0:
                            finish(p - 1)

                    wait_alone(pe, inv_in, g * 112 + 112)
                    pe.wait_ge(post_m, g * 2 * PAIRS + 2 * PAIRS)
                    pe.wait_ge(post_k, g * PAIRS + PAIRS)
                    H2 = M // 2
                    for half_no in range(2):
                        for m in range(half_no * H2, (half_no + 1) * H2):
                            w = slice((m % H2) * BLK, (m % H2 + 1) * BLK)
                            s = nc.tensor.matmul(bank[half_no][32:64, w], masks[0:32, m, 0, 32:64], inv64[0:32, m, 0:32],
                                                 start=True, stop=True)
                        s.then_inc(merge_mm, 1)
                        for m in range(half_no * H2, (half_no + 1) * H2):
                            w = slice((m % H2) * BLK, (m % H2 + 1) * BLK)
                            s = nc.tensor.matmul(bank[2 + half_no][96:128, w], masks[64:96, m, 0, 96:128], inv32[:, m, :],
                                                 start=True, stop=True)
                        s.then_inc(merge_mm, 1)
                    for half_no in range(2):
                        wait_alone(pe, merge_ev, g * 18 + 2 * half_no + 1)
                        for m in range(half_no * H2, (half_no + 1) * H2):
                            w = slice((m % H2) * BLK, (m % H2 + 1) * BLK)
                            nc.tensor.matmul(bank[4 + half_no][0:32, w], cross[32:64, m, 0:32], invT[32:64, m, 32:64],
                                             start=True, stop=True)
                            s = nc.tensor.matmul(bank[6 + half_no][32:64, w], invT[32:64, m, 32:64], cross[32:64, m, 0:32],
                                                 start=True, stop=True)
                        s.then_inc(merge_mm, 1)
                        wait_alone(pe, merge_ev, g * 18 + 2 * half_no + 2)
                        for m in range(half_no * H2, (half_no + 1) * H2):
                            w = slice((m % H2) * BLK, (m % H2 + 1) * BLK)
                            s = nc.tensor.matmul(bank[2 + half_no][64:96, w], cross[96:128, m, 0:32], invT[96:128, m, 96:128],
                                                 start=True, stop=True)
                        s.then_inc(merge_mm, 1)
                    for e4 in range(4):
                        wait_alone(pe, merge_ev, g * 18 + (4 + 3 * e4 + 2 if e4 < 2 else 10))
                        for m in range(e4 * 8, e4 * 8 + 8):
                            w = slice((m % 8) * 64, (m % 8 + 1) * 64)
                            s = nc.tensor.matmul(bank[(0, 1, 4, 5)[e4]][64:128, w], masks[0:64, m, 0, 64:128], inv64[0:64, m, :],
                                                 start=True, stop=True)
                        s.then_inc(merge_mm, 1)
                    for e4 in range(4):
                        wait_alone(pe, merge_ev, g * 18 + 10 + e4 + 1)
                        for m in range(e4 * 8, e4 * 8 + 8):
                            w = slice((m % 8) * 64, (m % 8 + 1) * 64)
                            s = nc.tensor.matmul(bank[(2, 3, 6, 7)[e4]][0:64, w], cross[64:128, m, :], invT[64:128, m, 64:128],
                                                 start=True, stop=True)
                        s.then_inc(merge_mm, 1)

                    def chunk_of(i):
                        c, s_no = divmod(i, STREAMS)
                        hh, b = divmod(s_no, B)
                        return c, s_no, hh, b, hh * NT + b * NC + c

                    pe.wait_ge(merge_ev, g * 18 + 18)
                    for i in range(SLOTS + 3):
                        if STREAMS <= i < SLOTS:
                            c, s_no, hh, b, m = chunk_of(i)
                            pe.wait_ge(state_done, g * 3 * STREAMS + i - STREAMS + 1)
                            pe.wait_ge(rhs_done, g * SLOTS + i - 1)
                            nc.tensor.matmul(bank[i % 2][:, 0:P], kT[:, hh, tokens(b, c)], state[:, s_no, :],
                                             start=True, stop=True).then_inc(ks_done, 1)
                        if 1 <= i <= SLOTS:
                            j = i - 1
                            c, s_no, hh, b, m = chunk_of(j)
                            pe.wait_ge(rhs_done, g * SLOTS + j + 1)
                            pe.wait_ge(y_copied, g * SLOTS + max(j - 1, 0))
                            nc.tensor.matmul(bank[2 + j % 2][:, 0:P], invT[:, m, :], rhs_sb[:, j % 2, :],
                                             start=True, stop=True).then_inc(y_done, 1)
                        if 2 <= i <= SLOTS + 1:
                            j = i - 2
                            c, s_no, hh, b, m = chunk_of(j)
                            pe.wait_ge(y_copied, g * SLOTS + j + 1)
                            pe.wait_ge(o_done, g * SLOTS + max(j - 1, 0))
                            pe.wait_ge(state_done, g * 3 * STREAMS + min(max(j - 1, 0), 3 * STREAMS))
                            bk = bank[4 + j % 2]
                            s = nc.tensor.matmul(bk[:, 0:P], masks[:, m, 1, :], y_sb[:, j % 2, :], start=True, stop=True)
                            if c > 0:
                                s = nc.tensor.matmul(bk[:, 2 * P:3 * P], qT[:, hh, tokens(b, c)], state[:, s_no, :],
                                                     start=True, stop=True)
                            if c < NC - 1:
                                s = nc.tensor.matmul(bk[:, P:2 * P], vk[:, 1, hh, b * NC + c, :], y_sb[:, j % 2, :],
                                                     start=True, stop=True)
                            s.then_inc(upd_done, 1)
                        if 3 <= i:
                            j = i - 3
                            pe.wait_ge(o_done, g * SLOTS + j + 1)
                            if j % 4 == 0:
                                pe.wait_ge(o_gated, g * (SLOTS // 4) + max(j // 4 - 1, 0))
                            s = nc.tensor.transpose(bank[6 + (j // 4) % 2][:, (j % 4) * P:(j % 4 + 1) * P], o_sb[:, j % 2, :],
                                                    ident[:, :])
                            s.then_inc(o_turned, 1)

                    pe.wait_ge(wo_in, g * 16 + 16)
                    pe.wait_ge(o_gated, g * (SLOTS // 4) + SLOTS // 4)
                    for n in range(NT):
                        for hh in range(HG):
                            s = nc.tensor.matmul(bank[n // 2][:, (n % 2) * D:(n % 2 + 1) * D], gated[:, hh, n * P:(n + 1) * P],
                                                 wo_sb[:, hh, :], start=hh == 0, stop=hh == HG - 1)
                        if n % 2:
                            s.then_inc(wo_done, 1)
                    pe.wait_ge(wo_added, g * 4 + 4)

            def inner_output(act, g, i):
                c, s_no = divmod(i, STREAMS)
                hh, b = divmod(s_no, B)
                act.wait_ge(upd_done, g * SLOTS + i + 1)
                act.wait_ge(o_turned, g * SLOTS + max(i - 1, 0))
                nc.scalar.activation(o_sb[:, i % 2, :], bank[4 + i % 2][:, 0:P], ACT.Copy,
                                     scale=qk_scales[:, hh, b * NC + c, 1:2]).then_inc(intra_done, 1)

            @block.scalar
            def _(act):
                with act.Fori(0, GROUPS) as g:
                    def outer_taps(u):
                        p, typ = divmod(u, 3)
                        hh, b = divmod(p, B)
                        act.wait_ge(proj_done, g * 4 * PAIRS + 4 * p + typ + 1)
                        act.wait_ge(silu_done, g * 4 * PAIRS + max((u - 2) // 3 * 4 + (u - 2) % 3 + 1, 0))
                        if u == 0 or (b == 0 and typ == 0):
                            act.wait_ge(w_in[hh % 2], g * 64 + 32 * (hh // 2 + 1))
                        nc.scalar.activation(conv[:, u % 2, :], bank[typ][:, :], ACT.Copy,
                                             scale=cw_sb[:, hh % 2, typ, 3:4]).then_inc(far_done, 1)
                        if u >= 2:
                            act.wait_ge(near_done, g * 3 * PAIRS + u - 1)
                        nc.scalar.activation(conv_far[:, u % 2, 3:512], bank[typ][:, 0:509], ACT.Copy,
                                             scale=cw_sb[:, hh % 2, typ, 0:1]).then_inc(far_done, 1)

                    def silu(u):
                        p, typ = divmod(u, 3)
                        hh, b = divmod(p, B)
                        act.wait_ge(conv_done, g * 3 * PAIRS + u + 1)
                        if typ == 2:
                            act.wait_ge(turned_v, g * PAIRS + p)
                        dst = (qT[:, hh, tokens(b)], kT[:, hh, tokens(b)], vT[:, :])[typ]
                        nc.scalar.activation(dst, conv[:, u % 2, :], ACT.Silu).then_inc(silu_done, 1)
                        if typ == 2:
                            act.wait_ge(proj_done, g * 4 * PAIRS + 4 * p + 4)
                            nc.scalar.activation(gated[:, hh, tokens(b)], bank[3][:, :], ACT.Silu).then_inc(silu_done, 1)

                    for u in range(3 * PAIRS + 1):
                        if u < 3 * PAIRS:
                            outer_taps(u)
                        if u > 0:
                            silu(u - 1)
                    act.wait_ge(inverted, g + 1)
                    nc.scalar.copy(sub_in, sub_inv.rearrange("p a b -> p b a")).then_inc(inverse_t, 1)

                    for i in range(SLOTS):
                        c, s_no = divmod(i, STREAMS)
                        hh, b = divmod(s_no, B)
                        n = b * NC + c
                        act.wait_ge(y_done, g * SLOTS + i + 1)
                        act.wait_ge(upd_done, g * SLOTS + max(i - 1, 0))
                        nc.scalar.copy(y_sb[:, i % 2, :], bank[2 + i % 2][:, 0:P]).then_inc(y_copied, 1)
                        if i > 0:
                            inner_output(act, g, i - 1)
                    inner_output(act, g, SLOTS - 1)

            @block.gpsimd
            def _(pool):
                with pool.Fori(0, GROUPS) as g:
                    def add_outer(u):
                        pool.wait_ge(far_done, g * 6 * PAIRS + 2 * u + 2)
                        nc.gpsimd.tensor_tensor(conv[:, u % 2, :], conv[:, u % 2, :], conv_far[:, u % 2, :],
                                                ALU.add).then_inc(near_done, 1)

                    def square(p):
                        hh, b = divmod(p, B)
                        for qk, src in enumerate((qT, kT)):
                            pool.wait_ge(silu_done, g * 4 * PAIRS + 4 * p + qk + 1)
                            pool.wait_ge(sums_done, g * 2 * PAIRS + 2 * p + qk)
                            s = src[:, hh, tokens(b)]
                            nc.gpsimd.tensor_tensor(squares[:, :], s, s, ALU.mult).then_inc(squared, 1)

                    def roots(p):
                        pool.wait_ge(sums_read, g * PAIRS + p + 1)
                        nc.gpsimd.tensor_tensor(norms[:, 1, :], norms[:, 0, :], half[:, :], ALU.pow).then_inc(rooted, 1)
                        pool.wait_ge(scaled, g * PAIRS + p + 1)
                        pool.wait_ge(post_k, g * PAIRS + p)
                        hh, b = divmod(p, B)
                        nc.gpsimd.tensor_tensor(decayed[:, :, :], ident[:, :].unsqueeze(1).to_broadcast([P, NC, P]),
                                                qk_scales[:, hh, b * NC:(b + 1) * NC, 3:4].to_broadcast([P, NC, P]),
                                                ALU.mult).then_inc(impulses, 1)

                    for p in range(PAIRS + 1):
                        if p < PAIRS:
                            for typ in range(3):
                                add_outer(3 * p + typ)
                                if typ == 1 and p > 0:
                                    roots(p - 1)
                            square(p)
                        else:
                            roots(p - 1)
                    wait_alone(pool, inv_out, g * 32)
                    nc.gpsimd.memset(sub_inv, 0.0).then_inc(cleared, 1)
                    wait_alone(pool, cleared, 2 * g + 1)
                    nc.gpsimd.memset(sub_inv.rearrange("p a b -> p (a b)")[:, 0:BLK * BLK:BLK + 1], 1.0).then_inc(cleared, 1)

            @block.vector
            def _(dve):
                with dve.Fori(0, GROUPS) as g:
                    count = [0]

                    def step(ins):
                        count[0] += 1
                        ins.then_inc(step2, 1)
                        dve.wait_ge(step2, g * STEPS2 + count[0])

                    def inner_taps(u):
                        p, typ = divmod(u, 3)
                        hh, b = divmod(p, B)
                        dve.wait_ge(near_done, g * 3 * PAIRS + u + 1)
                        step(nc.vector.scalar_tensor_tensor(conv[:, u % 2, 1:512], bank[typ][:, 0:511],
                                                            cw_sb[:, hh % 2, typ, 2:3], conv[:, u % 2, 1:512],
                                                            ALU.mult, ALU.add))
                        nc.vector.scalar_tensor_tensor(conv[:, u % 2, 2:512], bank[typ][:, 0:510],
                                                       cw_sb[:, hh % 2, typ, 1:2], conv[:, u % 2, 2:512],
                                                       ALU.mult, ALU.add).then_inc(conv_done, 1)

                    def scales(p):
                        hh, b = divmod(p, B)
                        sc = qk_scales[:, hh, b * NC:(b + 1) * NC, :]
                        dve.wait_ge(sums_done, g * 2 * PAIRS + 2 * p + 2)
                        nc.vector.tensor_scalar(norms[:, 0, :], bank[4][:, 0:8], NORM_EPS2, None, ALU.max).then_inc(sums_read, 1)
                        dve.wait_ge(sums_read, g * PAIRS + p + 1)
                        step(nc.vector.reciprocal(sc[:, :, 3:4], norms[:, 0, NC:2 * NC].unsqueeze(2)))
                        nc.vector.tensor_tensor(sc[:, :, 3:4], sc[:, :, 3:4],
                                                alpha_beta[:, b * NC:(b + 1) * NC, bass.ds(g * HG + (HEADS + hh), 1)],
                                                ALU.mult).then_inc(scaled, 1)
                        dve.wait_ge(rooted, g * PAIRS + p + 1)
                        nc.vector.tensor_copy(sc[:, :, 0:1], norms[:, 1, NC:2 * NC].unsqueeze(2))
                        step(nc.vector.reciprocal(sc[:, :, 1:2], norms[:, 1, 0:NC].unsqueeze(2)))
                        step(nc.vector.tensor_tensor(sc[:, :, 2:3], sc[:, :, 1:2],
                                                     decay_from_start[:, b * NC:(b + 1) * NC, bass.ds(g * HG + hh, 1)], ALU.mult))

                    def chunk_mats(p):
                        hh, b = divmod(p, B)
                        sc = qk_scales[:, hh, b * NC:(b + 1) * NC, :]
                        dve.wait_ge(turned_v, g * PAIRS + p + 1)
                        nc.vector.tensor_tensor(vk[:, 0, hh, b * NC:(b + 1) * NC, :],
                                                bank[5][:, :].rearrange("p (c e) -> p c e", c=NC),
                                                sc[:, :, 0:1].to_broadcast([P, NC, P]), ALU.mult).then_inc(post_v, 1)
                        dve.wait_ge(impulses, g * PAIRS + p + 1)
                        dve.wait_ge(decay_in[b], g * 16 * HG + 16 * (hh + 1))
                        step(nc.vector.tensor_tensor_scan(decayed[:, :, :].rearrange("p c t -> p (c t)"), decay_bc[:, b, :],
                                                          decayed[:, :, :].rearrange("p c t -> p (c t)"), 0.0, ALU.mult, ALU.add))
                        for c2 in range(2):
                            dve.wait_ge(products, g * 2 * PAIRS + 2 * p + c2 + 1)
                            m = hh * NT + b * NC + 2 * c2
                            nc.vector.tensor_tensor(masks[:, m:m + 2, :, :],
                                                    bank[6 + c2][:, :].rearrange("p (c a t) -> p c a t", c=2, a=2),
                                                    decayed[:, 2 * c2:2 * c2 + 2, :].unsqueeze(2).to_broadcast([P, 2, 2, P]),
                                                    ALU.mult).then_inc(post_m, 1)
                        dve.wait_ge(turned_k, g * PAIRS + p + 1)
                        nc.vector.tensor_tensor(vk[:, 1, hh, b * NC:(b + 1) * NC, :],
                                                bank[4][:, :].rearrange("p (c e) -> p c e", c=NC),
                                                decayed[:, :, P - 1:P].to_broadcast([P, NC, P]), ALU.mult).then_inc(post_k, 1)

                    for p in range(PAIRS + 1):
                        for typ in range(3):
                            if p < PAIRS:
                                inner_taps(3 * p + typ)
                            if p > 0 and typ == 0:
                                scales(p - 1)
                            if p > 0 and typ == 1:
                                chunk_mats(p - 1)

                    dve.wait_ge(blocks_in, g * 16 + 16)
                    dve.wait_ge(cleared, 2 * g + 2)
                    for s in range(BLK - 1):
                        rows_n, cols = s + 1, BLK - 1 - s
                        tmp = sub_tmp[:, 0:rows_n * cols].rearrange("p (a b) -> p a b", a=rows_n)
                        step(nc.vector.tensor_tensor(tmp, sub_inv[:, 0:rows_n, s:s + 1].to_broadcast([P, rows_n, cols]),
                                                     sub_in[:, s:s + 1, s + 1:BLK].to_broadcast([P, rows_n, cols]), ALU.mult))
                        ins = nc.vector.tensor_tensor(sub_inv[:, 0:rows_n, s + 1:BLK], sub_inv[:, 0:rows_n, s + 1:BLK], tmp,
                                                      ALU.subtract)
                        if s < BLK - 2:
                            step(ins)
                        else:
                            ins.then_inc(inverted, 1)

                    H2 = M // 2

                    def evac(dst, src, sign, mm):
                        dve.wait_ge(merge_mm, g * 16 + mm)
                        if sign < 0:
                            nc.vector.tensor_scalar(dst, src, -1.0, None, ALU.mult).then_inc(merge_ev, 1)
                        else:
                            nc.vector.tensor_copy(dst, src).then_inc(merge_ev, 1)

                    def wide(v, cols):
                        return v.rearrange("p (m t) -> p m t", t=cols)

                    for h2 in range(2):
                        ms = slice(h2 * H2, (h2 + 1) * H2)
                        evac(cross[32:64, ms, 0:32], wide(bank[h2][32:64, :], 32), -1, 2 * h2 + 1)
                        evac(cross[96:128, ms, 0:32], wide(bank[2 + h2][96:128, :], 32), -1, 2 * h2 + 2)
                    for h2 in range(2):
                        ms = slice(h2 * H2, (h2 + 1) * H2)
                        evac(invT[0:32, ms, 32:64], wide(bank[4 + h2][0:32, :], 32), 1, 4 + 2 * h2 + 1)
                        evac(inv64[32:64, ms, 0:32], wide(bank[6 + h2][32:64, :], 32), 1, 4 + 2 * h2 + 1)
                        evac(invT[64:96, ms, 96:128], wide(bank[2 + h2][64:96, :], 32), 1, 4 + 2 * h2 + 2)
                    for e4 in range(4):
                        ms = slice(e4 * 8, e4 * 8 + 8)
                        evac(cross[64:128, ms, :], wide(bank[(0, 1, 4, 5)[e4]][64:128, :], 64), -1, 8 + e4 + 1)
                    for e4 in range(4):
                        ms = slice(e4 * 8, e4 * 8 + 8)
                        evac(invT[0:64, ms, 64:128], wide(bank[(2, 3, 6, 7)[e4]][0:64, :], 64), 1, 12 + e4 + 1)

                    def right_side(i):
                        c, s_no = divmod(i, STREAMS)
                        hh, b = divmod(s_no, B)
                        n = b * NC + c
                        dve.wait_ge(y_done, g * SLOTS + max(i - 1, 0))
                        if c == 0:
                            nc.vector.tensor_copy(rhs_sb[:, i % 2, :], vk[:, 0, hh, n, :]).then_inc(rhs_done, 1)
                        else:
                            dve.wait_ge(ks_done, g * (SLOTS - STREAMS) + i - STREAMS + 1)
                            nc.vector.scalar_tensor_tensor(rhs_sb[:, i % 2, :], bank[i % 2][:, 0:P],
                                                           neg_decay[:, n, bass.ds(g * HG + hh, 1)], vk[:, 0, hh, n, :],
                                                           ALU.mult, ALU.add).then_inc(rhs_done, 1)

                    def outputs(i):
                        c, s_no = divmod(i, STREAMS)
                        hh, b = divmod(s_no, B)
                        n = b * NC + c
                        bk = bank[4 + i % 2]
                        dve.wait_ge(intra_done, g * SLOTS + i + 1)
                        if c == 0:
                            nc.vector.tensor_copy(state[:, s_no, :], bk[:, P:2 * P]).then_inc(state_done, 1)
                        elif c < NC - 1:
                            nc.vector.scalar_tensor_tensor(state[:, s_no, :], state[:, s_no, :],
                                                           chunk_decay[:, bass.ds(g * HG + hh, 1), n], bk[:, P:2 * P],
                                                           ALU.mult, ALU.add).then_inc(state_done, 1)
                        if c == 0:
                            nc.vector.engine_nop().then_inc(o_done, 1)
                        else:
                            nc.vector.scalar_tensor_tensor(o_sb[:, i % 2, :], bk[:, 2 * P:3 * P],
                                                           qk_scales[:, hh, n, 2:3], o_sb[:, i % 2, :],
                                                           ALU.mult, ALU.add).then_inc(o_done, 1)

                    def gate(q):
                        c, half_no = divmod(q, STREAMS // 4)
                        dve.wait_ge(o_turned, g * SLOTS + 4 * q + 4)
                        v = gated[:, :, :].rearrange("p h (b t) -> p h b t", b=B)[:, 2 * half_no:2 * half_no + 2, :, c * P:(c + 1) * P]
                        nc.vector.tensor_tensor(v, v, bank[6 + q % 2][:, :].rearrange("p (h b t) -> p h b t", h=2, b=B),
                                                ALU.mult).then_inc(o_gated, 1)

                    for i in range(SLOTS + 3):
                        if i < SLOTS:
                            right_side(i)
                        if 2 <= i <= SLOTS + 1:
                            outputs(i - 2)
                        if i >= 6 and (i - 6) % 4 == 0:
                            gate((i - 6) // 4)

                    for q in range(4):
                        dve.wait_ge(wo_done, g * 4 + q + 1)
                        nc.vector.tensor_tensor(resid[:, 2 * q:2 * q + 2, :], resid[:, 2 * q:2 * q + 2, :],
                                                bank[q][:, :].rearrange("p (n d) -> p n d", n=2), ALU.add).then_inc(wo_added, 1)
                    assert count[0] == STEPS2, count[0]

        e_small, e_w = sem("e_small"), [sem("e_w_even"), sem("e_w_odd")]
        var3, std3, normed3, turned3, turned_sb3 = sem("var3"), sem("std3"), sem("normed3"), sem("turned3"), sem("turned_sb3")
        logits_ready, shifted, exped, top_shift, top_exp = sem("logits_ready"), sem("shifted"), sem("exped"), sem("top_shift"), sem("top_exp")
        picks, pick_sums, weights_ready, wT_ready, wT_sb = sem("picks"), sem("pick_sums"), sem("weights_ready"), sem("wT_ready"), sem("wT_sb")
        bias_mm, bias_sb = sem("bias_mm"), sem("bias_sb")
        expert_no_ready = sem("expert_no_ready")
        h_mm, h_sb, y_mm, y_acc = sem("h_mm"), sem("h_sb"), sem("y_mm"), sem("y_acc")
        pool_mm, pool_sb, hid_mm, hid_sb, phi_mm, phi_z, phi_exp = (sem("pool_mm"), sem("pool_sb"), sem("hid_mm"), sem("hid_sb"),
                                                                    sem("phi_mm"), sem("phi_z"), sem("phi_exp"))
        final, stored = sem("final"), sem("stored")
        step3 = sem("step3")
        H_PER, Y_PER = 2 * KI, NT

        with nc.Block() as block:
            @block.sync
            def _(sp):
                small_loads = [(wr_sb, wr), (br_sb, br.partition_broadcast(P)), (b1_sb, b1), (b2_sb[0:E, :], b2),
                               (wp1_sb, wp1), (bp1_sb, bp1), (wp2_sb, wp2), (bp2_sb, bp2.partition_broadcast(P))]
                for dst, src in small_loads:
                    sp.dma_start(dst, src).then_inc(e_small, 16)
                with sp.Fori(0, E // 2) as pair:
                    for par in range(2):
                        sp.wait_ge(y_mm, pair * 2 * Y_PER if par == 1 else pair * 2 * Y_PER)
                        sp.dma_start(w1_sb[par], w1[bass.ds(pair * 2 + par, 1)].squeeze(0).rearrange("(k p) i -> p k i", p=P)).then_inc(e_w[par], 16)
                        sp.dma_start(w2_sb[par], w2[bass.ds(pair * 2 + par, 1)].squeeze(0).rearrange("(k p) d -> p k d", p=P)).then_inc(e_w[par], 16)
                sp.wait_ge(final, NT)
                sp.dma_start(out.rearrange("(n p) d -> p n d", p=P), resid[:, :, :]).then_inc(stored, 16)
                sp.wait_ge(stored, 16)

            @block.gpsimd
            def _(pool):
                nc.gpsimd.iota(expert_no, pattern=[[1, E]], base=0, channel_multiplier=0,
                               allow_small_or_imprecise_dtypes=True).then_inc(expert_no_ready, 1)

            @block.scalar
            def _(act):
                act.wait_ge(var3, 1)
                nc.scalar.activation(rstd[:, :].unsqueeze(2), mean_var[:, :, 1:2], ACT.Sqrt, bias=eps_col[:, :]).then_inc(std3, 1)
                act.wait_ge(shifted, 1)
                nc.scalar.activation(probs, logits, ACT.Exp).then_inc(exped, 1)
                act.wait_ge(top_shift, 1)
                nc.scalar.activation(top_w, top_w, ACT.Exp).then_inc(top_exp, 1)
                with act.Fori(0, E // 2) as pair:
                    for par in range(2):
                        for r in range(H_PER):
                            k, half_no = divmod(r, 2)
                            wait_alone(act, h_mm, pair * 2 * H_PER + par * H_PER + r + 1)
                            nc.scalar.activation(hT[par][:, k, half_no * 512:(half_no + 1) * 512], bank[r % 4][:, :], ACT.Relu,
                                                 bias=b1_sb[:, bass.ds(pair * 2 + par, 1), k]).then_inc(h_sb, 1)
                act.wait_ge(phi_z, 1)
                nc.scalar.activation(phi, phi, ACT.Exp, scale=-1.0).then_inc(phi_exp, 1)

            @block.tensor
            def _(pe):
                pe.wait_ge(normed3, 1)
                for k in range(KD):
                    for n in range(NT):
                        b_no = 2 * k + n // 4
                        s = nc.tensor.transpose(bank[b_no][:, (n % 4) * P:(n % 4 + 1) * P], normed[:, n, k * P:(k + 1) * P],
                                                ident[:, :])
                        if n % 4 == 3:
                            s.then_inc(turned3, 1)
                pe.wait_ge(turned_sb3, 4)
                pe.wait_ge(e_small, 128)
                for n in range(NT):
                    for k in range(KD):
                        s = nc.tensor.matmul(bank[4][:, n * E:(n + 1) * E], normedT[:, k, n * P:(n + 1) * P], wr_sb[:, k, :],
                                             start=k == 0, stop=k == KD - 1)
                s.then_inc(logits_ready, 1)
                pe.wait_ge(picks, 1)
                nc.tensor.matmul(bank[5][:, 0:2 * E], ones[:, :], pick_sum, start=True, stop=True).then_inc(pick_sums, 1)
                pe.wait_ge(weights_ready, 1)
                for n in range(NT):
                    s = nc.tensor.transpose(bank[6 + n // 4][0:E, (n % 4) * P:(n % 4 + 1) * P], token_w[:, n, :], ident[:, :])
                s.then_inc(wT_ready, 1)
                pe.wait_ge(wT_sb, 1)
                for n in range(NT):
                    s = nc.tensor.matmul(bank[n // 2][:, (n % 2) * D:(n % 2 + 1) * D], token_wT[0:E, n * P:(n + 1) * P], b2_sb[0:E, :],
                                         start=True, stop=True)
                    if n % 2:
                        s.then_inc(bias_mm, 1)
                pe.wait_ge(bias_sb, 4)
                with pe.Fori(0, E // 2) as pair:
                    for par in range(2):
                        pe.wait_ge(e_w[par], pair * 32 + 32)
                        for r in range(H_PER):
                            k, half_no = divmod(r, 2)
                            pe.wait_ge(h_sb, pair * 2 * H_PER + max(par * H_PER + r - 3, 0))
                            for kd in range(KD):
                                s = nc.tensor.matmul(bank[r % 4][:, :], w1_sb[par][:, kd, k * P:(k + 1) * P],
                                                     normedT[:, kd, half_no * 512:(half_no + 1) * 512], start=kd == 0, stop=kd == KD - 1)
                            s.then_inc(h_mm, 1)
                        pe.wait_ge(h_sb, pair * 2 * H_PER + (par + 1) * H_PER)
                        for n in range(NT):
                            pe.wait_ge(y_acc, pair * 2 * Y_PER + max(par * Y_PER + n - 3, 0))
                            for k in range(KI):
                                s = nc.tensor.matmul(bank[4 + n % 4][:, 0:D], hT[par][:, k, n * P:(n + 1) * P], w2_sb[par][:, k, :],
                                                     start=k == 0, stop=k == KI - 1)
                            s.then_inc(y_mm, 1)
                pe.wait_ge(y_acc, E * Y_PER)
                for k in range(KD):
                    for b in range(B):
                        for c in range(NC):
                            s = nc.tensor.matmul(bank[0][:, k * B + b:k * B + b + 1], acc[:, b * NC + c, k * P:(k + 1) * P], ones[:, 0:1],
                                                 start=c == 0, stop=c == NC - 1)
                s.then_inc(pool_mm, 1)
                pe.wait_ge(pool_sb, 1)
                for k in range(KD):
                    s = nc.tensor.matmul(bank[1][:, 0:B], wp1_sb[:, k, :], pooled[:, k * B:(k + 1) * B], start=k == 0, stop=k == KD - 1)
                s.then_inc(hid_mm, 1)
                pe.wait_ge(hid_sb, 1)
                nc.tensor.matmul(bank[2][:, 0:B], wp2_bc, hidden, start=True, stop=True).then_inc(phi_mm, 1)

            @block.vector
            def _(dve):
                count = [0]

                def step(ins):
                    count[0] += 1
                    ins.then_inc(step3, 1)
                    dve.wait_ge(step3, count[0])

                layernorm(dve, step).then_inc(var3, 1)
                dve.wait_ge(std3, 1)
                apply_norm(dve, step).then_inc(normed3, 1)
                for k in range(4):
                    dve.wait_ge(turned3, k + 1)
                    nc.vector.tensor_copy(normedT[:, k // 2, (k % 2) * 512:(k % 2 + 1) * 512], bank[k][:, :]).then_inc(turned_sb3, 1)
                dve.wait_ge(e_small, 128)
                nc.vector.tensor_copy(wp2_bc, wp2_sb.to_broadcast([P, P]))
                dve.wait_ge(logits_ready, 1)
                step(nc.vector.tensor_tensor(logits, bank[4][:, 0:NT * E].rearrange("p (n e) -> p n e", n=NT),
                                             br_sb.unsqueeze(1).to_broadcast([P, NT, E]), ALU.add))
                step(nc.vector.tensor_reduce(row_max, logits, AX.X, ALU.max))
                nc.vector.tensor_tensor(logits, logits, row_max.unsqueeze(2).to_broadcast([P, NT, E]), ALU.subtract).then_inc(shifted, 1)
                dve.wait_ge(exped, 1)
                step(nc.vector.tensor_reduce(row_sum, probs, AX.X, ALU.add))
                step(nc.vector.reciprocal(row_inv, row_sum))
                step(nc.vector.tensor_tensor(probs, probs, row_inv.unsqueeze(2).to_broadcast([P, NT, E]), ALU.mult))
                for n in range(NT):
                    s = nc.vector.max(top8[:, n, :], probs[:, n, :])
                step(s)
                for n in range(NT):
                    s = nc.vector.max_index(top_idx[:, n, :], top8[:, n, :], probs[:, n, :])
                step(s)
                nc.vector.tensor_copy(top_no, top_idx[:, :, :])
                nc.vector.tensor_tensor(top_w, top8[:, :, 0:TOPK], top8[:, :, 0:1].to_broadcast([P, NT, TOPK]), ALU.subtract).then_inc(top_shift, 1)
                dve.wait_ge(top_exp, 1)
                step(nc.vector.tensor_reduce(top_sum, top_w, AX.X, ALU.add))
                step(nc.vector.reciprocal(top_sum, top_sum))
                step(nc.vector.tensor_tensor(top_w, top_w, top_sum.unsqueeze(2).to_broadcast([P, NT, TOPK]), ALU.mult))
                dve.wait_ge(expert_no_ready, 1)
                for k in range(TOPK):
                    one = pick_one if k else picked[:, :, 0:E]
                    step(nc.vector.tensor_tensor(one, expert_no.unsqueeze(1).to_broadcast([P, NT, E]),
                                                 top_no[:, :, k:k + 1].to_broadcast([P, NT, E]), ALU.is_equal))
                    if k:
                        step(nc.vector.tensor_tensor(picked[:, :, 0:E], picked[:, :, 0:E], pick_one, ALU.add))
                        step(nc.vector.tensor_tensor(pick_one, pick_one, top_w[:, :, k:k + 1].to_broadcast([P, NT, E]), ALU.mult))
                        step(nc.vector.tensor_tensor(picked[:, :, E:2 * E], picked[:, :, E:2 * E], pick_one, ALU.add))
                    else:
                        step(nc.vector.tensor_tensor(picked[:, :, E:2 * E], one, top_w[:, :, 0:1].to_broadcast([P, NT, E]), ALU.mult))
                nc.vector.tensor_reduce(pick_sum, picked.rearrange("p n e -> p e n"), AX.X, ALU.add).then_inc(picks, 1)
                dve.wait_ge(pick_sums, 1)
                step(nc.vector.tensor_scalar(expert_w[:, 0:E], bank[5][:, 0:E], 1.0, None, ALU.max))
                step(nc.vector.reciprocal(expert_w[:, 0:E], expert_w[:, 0:E]))
                step(nc.vector.tensor_tensor(expert_w[:, E:2 * E], bank[5][:, E:2 * E], expert_w[:, 0:E], ALU.mult))
                nc.vector.tensor_tensor(token_w, picked[:, :, 0:E], expert_w[:, E:2 * E].unsqueeze(1).to_broadcast([P, NT, E]),
                                        ALU.mult).then_inc(weights_ready, 1)
                dve.wait_ge(wT_ready, 1)
                for k in range(2):
                    s = nc.vector.tensor_copy(token_wT[0:E, k * 512:(k + 1) * 512], bank[6 + k][0:E, :])
                s.then_inc(wT_sb, 1)
                for q in range(4):
                    dve.wait_ge(bias_mm, q + 1)
                    nc.vector.tensor_copy(acc[:, 2 * q:2 * q + 2, :], bank[q][:, :].rearrange("p (n d) -> p n d", n=2)).then_inc(bias_sb, 1)
                dve.wait_ge(bias_sb, 4)
                with dve.Fori(0, E // 2) as pair:
                    for par in range(2):
                        for n in range(NT):
                            done = par * Y_PER + n
                            dve.wait_ge(y_mm, pair * 2 * Y_PER + done + 1)
                            dve.wait_ge(y_acc, pair * 2 * Y_PER + max(done - NT + 1, 0))
                            nc.vector.scalar_tensor_tensor(acc[:, n, :], bank[4 + n % 4][:, 0:D],
                                                           token_w[:, n, bass.ds(pair * 2 + par, 1)], acc[:, n, :],
                                                           ALU.mult, ALU.add).then_inc(y_acc, 1)
                dve.wait_ge(pool_mm, 1)
                nc.vector.tensor_scalar(pooled, bank[0][:, 0:2 * KD], 1.0 / SEQ, None, ALU.mult).then_inc(pool_sb, 1)
                dve.wait_ge(hid_mm, 1)
                nc.vector.tensor_scalar(hidden, bank[1][:, 0:B], bp1_sb, 0.0, ALU.add, ALU.max).then_inc(hid_sb, 1)
                dve.wait_ge(phi_mm, 1)
                nc.vector.tensor_scalar(phi, bank[2][:, 0:B], bp2_sb, None, ALU.add).then_inc(phi_z, 1)
                dve.wait_ge(phi_exp, 1)
                step(nc.vector.tensor_scalar(phi, phi, 1.0, None, ALU.add))
                step(nc.vector.reciprocal(phi, phi))
                step(nc.vector.tensor_scalar(phi, phi, 0.7, -0.8, ALU.is_gt, ALU.mult))
                step(nc.vector.tensor_scalar(phi, phi, 1.0, None, ALU.add))
                for n in range(NT):
                    nc.vector.scalar_tensor_tensor(resid[:, n, :], acc[:, n, :], phi[:, n // NC:n // NC + 1], resid[:, n, :],
                                                   ALU.mult, ALU.add).then_inc(final, 1)


STEPS2 = 3 * HG * B + 3 * HG * B + HG * B + 2 * (BLK - 1) - 1


def kernel(**inputs):
    import concourse.bacc as bacc
    from concourse.bass_utils import run_bass_kernel_spmd

    a = {k.replace("L0_", ""): np.asarray(v) for k, v in inputs.items()}

    def halves(w):
        return w.reshape(KD, P, -1).transpose(1, 0, 2)

    inner = HEADS * P
    wq = a["attn_W_qkv"].reshape(3, HEADS, P, D)
    wg = a["attn_W_g"].reshape(1, HEADS, P, D)
    wall = np.concatenate([wq, wg], 0)
    arrays = {
        "x": a["attn_x"].reshape(TOK, D),
        "wqkvg": wall.transpose(1, 3, 0, 2).reshape(HEADS, KD, P, 4, P).transpose(0, 2, 1, 3, 4),
        "convw": a["attn_conv_w"].reshape(3, HEADS, P, TAPS).transpose(1, 2, 0, 3),
        "wab": halves(a["attn_W_ab"].T),
        "bab": a["attn_b_ab"],
        "wo": a["attn_W_o"].T.reshape(HEADS, P, D),
        "wr": halves(a["ffn_Wr"]),
        "br": a["ffn_br"],
        "w1": a["ffn_w1"],
        "b1": a["ffn_b1"].reshape(E, KI, P).transpose(2, 0, 1),
        "w2": a["ffn_w2"],
        "b2": a["ffn_b2"],
        "wp1": halves(a["ffn_Wp1"]),
        "bp1": a["ffn_bp1"].reshape(P, 1),
        "wp2": a["ffn_Wp2"],
        "bp2": a["ffn_bp2"],
    }
    nc = bacc.Bacc("TRN2", target_bir_lowering=False, num_devices=1)
    args = []
    for name in arrays:
        arrays[name] = np.ascontiguousarray(arrays[name])
        args.append(nc.dram_tensor(f"in_{name}", arrays[name].shape, F32, kind="ExternalInput").ap())
    args.append(nc.dram_tensor("out_y", (TOK, D), F32, kind="ExternalOutput").ap())
    block_kernel(nc, *args)
    r = run_bass_kernel_spmd(nc, [{f"in_{k}": v for k, v in arrays.items()}], core_ids=[0])
    return r.results[0]["out_y"].reshape(B, SEQ, D)
```

```python
from contextlib import ExitStack

import numpy as np

import concourse.bass as bass
from concourse import mybir

F32 = mybir.dt.float32
U32 = mybir.dt.uint32
ALU = mybir.AluOpType
ACT = mybir.ActivationFunctionType
AX = mybir.AxisListType

P = 128
B, SEQ, D = 2, 512, 256
TOK = B * SEQ
NT = TOK // P
NC = SEQ // P
KD = D // P
HEADS = 16
TAPS = 4
HG = 2
GROUPS = HEADS // HG
M = HG * NT
BLK = 32
NB = P // BLK
E, TOPK, I = 12, 3, 640
KI = I // P
LN_EPS = 1e-5
NORM_EPS2 = 1e-24

STREAMS = HG * B
SLOTS = NC * STREAMS
FRONT_STEPS = 7 * HG * B
SUB_STEPS = 2 * (BLK - 1)
SUB_BACK, SUB_OUT = 32, 14
SUB_FRONT = SUB_STEPS - SUB_BACK - SUB_OUT
TURN_AT = 3


def block_kernel(nc, x, wqkvg, convw, wab, bab, wo, wr, br, w1, b1, w2, b2, wp1, bp1, wp2, bp2, out):
    with ExitStack() as ctx:
        def sb(name, shape, dt=F32):
            return ctx.enter_context(nc.sbuf_tensor(name, shape, dt))

        def sem(name):
            return ctx.enter_context(nc.semaphore(name))

        bank = [ctx.enter_context(nc.psum_tensor(f"bank{i}", [P, 512], F32)) for i in range(8)]

        decay_dram = nc.dram_tensor("decay_rows", [HEADS, TOK], F32).ap()
        chunk_decay_dram = nc.dram_tensor("chunk_decay_rows", [HEADS, NT], F32).ap()
        lower_dram = nc.dram_tensor("lower_blocks", [NB, M, BLK, BLK], F32).ap()
        invT_dram = nc.dram_tensor("inverse_blocks_t", [NB, M, BLK, BLK], F32).ap()
        inv_dram = nc.dram_tensor("inverse_blocks", [NB, M, BLK, BLK], F32).ap()

        resid = sb("resid", [P, NT, D])
        normedT = sb("normedT", [P, KD, TOK])
        ident = sb("ident", [P, P])
        ones = sb("ones", [P, P])
        stats = sb("stats", [P, NT, 6])
        mean_var = sb("mean_var", [P, NT, 2])
        rstd = sb("rstd", [P, NT])
        eps_col = sb("eps_col", [P, 1])

        wab_sb = sb("wab_sb", [P, KD, 2 * HEADS])
        bab_sb = sb("bab_sb", [P, 2 * HEADS])
        alpha_beta = sb("alpha_beta", [P, NT, 2 * HEADS])
        decay_from_start = sb("decay_from_start", [P, NT, HEADS])
        neg_decay = sb("neg_decay", [P, NT, HEADS])
        chunk_decay = sb("chunk_decay", [P, HEADS, NT])

        qT = sb("qT", [P, 2, HG, TOK])
        kT = sb("kT", [P, 2, HG, TOK])
        gated = sb("gated", [P, 2, HG, TOK])
        vk = sb("vk", [P, 2, 2, HG, NT, P])
        masks = sb("masks", [P, 2, M, 2, P])
        invT = sb("invT", [P, M, P])
        inv_low = sb("inv_low", [P, M, 64])
        inv64 = inv_low[0:64, :, :]
        inv32 = inv_low[64:96, :, 0:BLK]
        state = sb("state", [P, STREAMS, P])
        qk_scales = sb("qk_scales", [P, 2, HG, NT, 4])
        w_sb = sb("w_sb", [P, 2, KD, 4, P])
        cw_sb = sb("cw_sb", [P, 2, 3, TAPS])
        decay_bc = sb("decay_bc", [P, B, SEQ])
        wo_sb = sb("wo_sb", [P, 2, HG, D])
        conv = sb("conv", [P, 2, 512])
        conv_far = sb("conv_far", [P, 2, 512])
        vT = sb("vT", [P, 2, 512])
        squares = sb("squares", [P, 2, 512])
        decayed = sb("decayed", [P, NC, P])
        norms = sb("norms", [P, 2, 8])
        half = sb("half", [P, 8])
        rhs_sb = sb("rhs_sb", [P, 2, P])
        y_sb = sb("y_sb", [P, 2, P])
        o_sb = sb("o_sb", [P, 2, P])
        blocks = sb("blocks", [NB * M, 2, BLK, BLK])
        sub_in, sub_inv = blocks[:, 0, :, :], blocks[:, 1, :, :]
        cross = sb("cross", [P, M, 64])
        sub_tmp = sb("sub_tmp", [P, 256])

        qT_flat = qT[:, :, :, :].rearrange("p s a b -> p (s a b)")
        kT_flat = kT[:, :, :, :].rearrange("p s a b -> p (s a b)")
        alpha_rows, reset_rows, impulse_rows, decay_rows = (qT_flat[0:HEADS, k * TOK:(k + 1) * TOK] for k in range(4))
        chunk_end_rows = kT_flat[0:HEADS, 0:NT]
        w1_sb = [v[:, 0:KD * I].rearrange("p (k i) -> p k i", k=KD) for v in (qT_flat, kT_flat)]
        w2_sb = [v[:, KD * I:KD * I + KI * D].rearrange("p (k d) -> p k d", k=KI) for v in (qT_flat, kT_flat)]
        hT = [masks[:, :, :, :, :].rearrange("p s m a t -> p (s m a t)")[:, 0:KI * TOK].rearrange("p (k t) -> p k t", k=KI),
              vk[:, :, :, :, :, :].rearrange("p s a h n t -> p (s a h n t)")[:, 0:KI * TOK].rearrange("p (k t) -> p k t", k=KI)]
        gated_flat = gated[:, :, :, :].rearrange("p s h t -> p (s h t)")
        acc = gated_flat[:, 0:NT * D].rearrange("p (n d) -> p n d", n=NT)
        normed = gated_flat[:, NT * D:2 * NT * D].rearrange("p (n d) -> p n d", n=NT)
        small = vk[:, :, :, :, :, :].rearrange("p s a h n t -> p (s a h n t)")[:, KI * TOK:]

        def carve():
            at = [0]

            def take(*shape):
                n = int(np.prod(shape))
                v = small[:, at[0]:at[0] + n]
                at[0] += n
                if len(shape) == 2:
                    v = v.rearrange("p (a b) -> p a b", a=shape[0])
                return v
            return take

        take = carve()
        wr_sb, br_sb = take(KD, E), take(E)
        b1_sb, b2_sb = take(E, KI), take(D)
        wp1_sb, bp1_sb, wp2_sb, bp2_sb = take(KD, P), take(1), take(1), take(1)
        wp2_bc = take(P)
        expert_no = take(E)
        logits, probs = take(NT, E), take(NT, E)
        row_max, row_sum, row_inv = take(NT), take(NT), take(NT)
        top8, top_no, top_w = take(NT, 8), take(NT, 8), take(NT, TOPK)
        top_sum = take(NT)
        picked = take(NT, 2 * E)
        pick_one = take(NT, E)
        pick_sum, expert_w = take(2 * E), take(2 * E)
        token_w = take(NT, E)
        token_wT = take(TOK)
        pooled, hidden, phi = take(2 * KD), take(B), take(B)
        top_idx = ctx.enter_context(nc.sbuf_tensor("top_idx", [P, NT, 8], U32))

        def layernorm(dve, step):
            for n in range(NT):
                s = nc.vector.bn_stats(stats[:, n, :], resid[:, n, :])
            step(s)
            for n in range(NT):
                s = nc.vector.bn_aggr(mean_var[:, n, :], stats[:, n, :])
            return s

        def apply_norm(dve, step):
            step(nc.vector.reciprocal(rstd[:, :], rstd[:, :]))
            for n in range(NT):
                s = nc.vector.tensor_scalar(normed[:, n, :], resid[:, n, :], mean_var[:, n, 0:1], rstd[:, n:n + 1],
                                            ALU.subtract, ALU.mult)
            return s

        def wait_alone(eng, what, value):
            value = eng.to_reg(value)
            eng.wait_ge(consts, 9)
            eng.wait_ge(what, value)

        w_in = [sem("w_in_head0"), sem("w_in_head1")]
        decay_in = [sem("decay_in_b0"), sem("decay_in_b1")]
        wo_in = sem("wo_in")
        proj_done = sem("proj_done")
        far_done = sem("far_done")
        near_done = sem("near_done")
        conv_done = sem("conv_done")
        silu_done = sem("silu_done")
        squared = sem("squared")
        sums_done = sem("sums_done")
        sums_read = sem("sums_read")
        rooted = sem("rooted")
        scaled = sem("scaled")
        impulses = sem("impulses")
        turned_v, turned_k = sem("turned_v"), sem("turned_k")
        products = sem("products")
        post_v, post_k, post_m = sem("post_v"), sem("post_k"), sem("post_m")
        blocks_out, blocks_in = sem("blocks_out"), sem("blocks_in")
        cleared = sem("cleared")
        inverted = sem("inverted")
        inverse_t = sem("inverse_t")
        inv_out, inv_in = sem("inv_out"), sem("inv_in")
        merge_mm = sem("merge_mm")
        merge_v, merge_s = sem("merge_v"), sem("merge_s")
        ks_done, rhs_done, y_done, y_copied = sem("ks_done"), sem("rhs_done"), sem("y_done"), sem("y_copied")
        gain_done, inner_done, inner_scaled = sem("gain_done"), sem("inner_done"), sem("inner_scaled")
        o_done, state_done = sem("o_done"), sem("state_done")
        o_turned, o_gated = sem("o_turned"), sem("o_gated")
        wo_done, wo_added = sem("wo_done"), sem("wo_added")
        front_step, sub_step = sem("front_step"), sem("sub_step")


        by_group = (proj_done, far_done, near_done, conv_done, silu_done, squared, sums_done, sums_read, rooted, scaled, impulses,
                    turned_v, turned_k, products, post_v, post_k, post_m, cleared, inverted, inverse_t, merge_mm, merge_v, merge_s,
                    ks_done, rhs_done, y_done, y_copied, gain_done, inner_done, inner_scaled, o_done, state_done, o_turned, o_gated,
                    wo_done, wo_added, front_step, sub_step)

        in_x, in_small = sem("in_x"), sem("in_small")
        consts, var_ready, std_ready, normed_ready = sem("consts"), sem("var_ready"), sem("std_ready"), sem("normed_ready")
        turned, turned_sb = sem("turned"), sem("turned_sb")
        ab_ready, ab_z, ab_exp, ab_sig = sem("ab_ready"), sem("ab_z"), sem("ab_exp"), sem("ab_sig")
        rows_ready, rows_sb, decay_cols, chunk_in = sem("rows_ready"), sem("rows_sb"), sem("decay_cols"), sem("chunk_in")
        dram_rows, decay_sb = sem("dram_rows"), sem("decay_sb")
        step1 = sem("step1")

        with nc.Block() as block:
            @block.sync
            def _(sp):
                sp.dma_start(resid[:, :, :], x.rearrange("(n p) d -> p n d", p=P)).then_inc(in_x, 16)
                sp.dma_start(wab_sb[:, :, :], wab).then_inc(in_small, 16)
                sp.dma_start(bab_sb[:, :], bab.partition_broadcast(P)).then_inc(in_small, 16)
                sp.wait_ge(rows_sb, 3)
                sp.dma_start(decay_dram, reset_rows).then_inc(dram_rows, 16)
                sp.dma_start(chunk_decay_dram, chunk_end_rows).then_inc(dram_rows, 16)
                sp.wait_ge(dram_rows, 32)
                sp.dma_start(chunk_decay[:, :, :], chunk_decay_dram.partition_broadcast(P)).then_inc(chunk_in, 16)
                sp.wait_ge(chunk_in, 16)

            @block.gpsimd
            def _(pool):
                nc.gpsimd.memset(ident[:, :], 0.0).then_inc(consts, 1)
                nc.gpsimd.memset(ones[:, :], 1.0).then_inc(consts, 1)
                nc.gpsimd.memset(eps_col[:, :], LN_EPS).then_inc(consts, 1)
                nc.gpsimd.memset(half[:, :], 0.5).then_inc(consts, 1)
                nc.gpsimd.memset(conv_far[:, :, :], 0.0).then_inc(consts, 1)
                nc.gpsimd.memset(invT[:, :, :], 0.0).then_inc(consts, 1)
                nc.gpsimd.memset(inv_low[:, :, :], 0.0).then_inc(consts, 1)
                nc.gpsimd.memset(impulse_rows, 0.0).then_inc(consts, 1)
                pool.wait_ge(consts, 8)
                nc.gpsimd.affine_select(out=ident[:, :], in_=ident[:, :], compare_op=ALU.not_equal, fill=1.0,
                                        base=0, pattern=[[-1, P]], channel_multiplier=1).then_inc(consts, 1)
                for counted in by_group:
                    pool.sem_inc(counted, 1)

            @block.vector
            def _(dve):
                count = [0]

                def step(ins):
                    count[0] += 1
                    ins.then_inc(step1, 1)
                    dve.wait_ge(step1, count[0])

                dve.wait_ge(in_x, 16)
                layernorm(dve, step).then_inc(var_ready, 1)
                dve.wait_ge(std_ready, 1)
                apply_norm(dve, step).then_inc(normed_ready, 1)
                for k in range(4):
                    dve.wait_ge(turned, k + 1)
                    nc.vector.tensor_copy(normedT[:, k // 2, (k % 2) * 512:(k % 2 + 1) * 512], bank[k][:, :]).then_inc(turned_sb, 1)
                dve.wait_ge(ab_ready, 1)
                dve.wait_ge(in_small, 32)
                nc.vector.tensor_tensor(alpha_beta[:, :, :], bank[4][:, 0:NT * 32].rearrange("p (n h) -> p n h", n=NT),
                                        bab_sb[:, :].unsqueeze(1).to_broadcast([P, NT, 32]), ALU.add).then_inc(ab_z, 1)
                dve.wait_ge(ab_exp, 1)
                step(nc.vector.tensor_scalar(alpha_beta[:, :, :], alpha_beta[:, :, :], 1.0, None, ALU.add))
                nc.vector.reciprocal(alpha_beta[:, :, :], alpha_beta[:, :, :]).then_inc(ab_sig, 1)
                dve.wait_ge(rows_ready, 1)
                for k in range(2):
                    s = nc.vector.tensor_copy(alpha_rows[:, k * 512:(k + 1) * 512], bank[5 + k][0:HEADS, :])
                step(s)
                dve.wait_ge(consts, 9)
                start = lambda v: v.rearrange("h (n t) -> h n t", n=NT)[:, :, 0:1]
                nc.vector.tensor_copy(start(impulse_rows), start(alpha_rows))
                step(nc.vector.tensor_copy(reset_rows, alpha_rows))
                s = nc.vector.memset(start(reset_rows), 0.0)
                s.then_inc(rows_sb, 1)
                dve.wait_ge(rows_sb, 1)
                nc.vector.tensor_tensor_scan(decay_rows, reset_rows, impulse_rows, 0.0, ALU.mult, ALU.add).then_inc(rows_sb, 1)
                dve.wait_ge(rows_sb, 2)
                nc.vector.tensor_copy(chunk_end_rows.unsqueeze(2),
                                      decay_rows.rearrange("h (n t) -> h n t", n=NT)[:, :, P - 1:P]).then_inc(rows_sb, 1)
                dve.wait_ge(decay_cols, 1)
                v = bank[7][:, 0:NT * HEADS].rearrange("p (n h) -> p n h", n=NT)
                nc.vector.tensor_copy(decay_from_start[:, :, :], v)
                nc.vector.tensor_scalar(neg_decay[:, :, :], v, -1.0, None, ALU.mult)

            @block.scalar
            def _(act):
                act.wait_ge(consts, 9)
                act.wait_ge(var_ready, 1)
                nc.scalar.activation(rstd[:, :].unsqueeze(2), mean_var[:, :, 1:2], ACT.Sqrt, bias=eps_col[:, :]).then_inc(std_ready, 1)
                act.wait_ge(ab_z, 1)
                nc.scalar.activation(alpha_beta[:, :, :], alpha_beta[:, :, :], ACT.Exp, scale=-1.0).then_inc(ab_exp, 1)

            @block.tensor
            def _(pe):
                pe.wait_ge(consts, 9)
                pe.wait_ge(normed_ready, 1)
                for k in range(KD):
                    for n in range(NT):
                        b_no = 2 * k + n // 4
                        s = nc.tensor.transpose(bank[b_no][:, (n % 4) * P:(n % 4 + 1) * P], normed[:, n, k * P:(k + 1) * P],
                                                ident[:, :])
                        if n % 4 == 3:
                            s.then_inc(turned, 1)
                pe.wait_ge(turned_sb, 4)
                pe.wait_ge(in_small, 32)
                for n in range(NT):
                    for k in range(KD):
                        s = nc.tensor.matmul(bank[4][:, n * 32:(n + 1) * 32], normedT[:, k, n * P:(n + 1) * P], wab_sb[:, k, :],
                                             start=k == 0, stop=k == KD - 1)
                s.then_inc(ab_ready, 1)
                pe.wait_ge(ab_sig, 1)
                for n in range(NT):
                    s = nc.tensor.transpose(bank[5 + n // 4][0:HEADS, (n % 4) * P:(n % 4 + 1) * P],
                                            alpha_beta[:, n, 0:HEADS], ident[:, :])
                s.then_inc(rows_ready, 1)
                pe.wait_ge(rows_sb, 2)
                for n in range(NT):
                    s = nc.tensor.transpose(bank[7][:, n * HEADS:(n + 1) * HEADS], decay_rows[:, n * P:(n + 1) * P],
                                            ident[0:HEADS, 0:HEADS])
                s.then_inc(decay_cols, 1)

        PAIRS = HG * B
        KS_SLOTS = SLOTS - STREAMS
        LAST = GROUPS - 1

        def until(eng, what, per, g, k, alone=False):
            if isinstance(g, int) and g * per + k <= 0:
                return
            (wait_alone if alone else type(eng).wait_ge)(eng, what, g * per + (k + 1))

        def tokens(b, c=None):
            return slice(b * SEQ, (b + 1) * SEQ) if c is None else slice(b * SEQ + c * P, b * SEQ + (c + 1) * P)

        def slot(i):
            c, s_no = divmod(i, STREAMS)
            hh, b = divmod(s_no, B)
            return c, s_no, hh, b, hh * NT + b * NC + c

        def blocks_of(v, cols):
            return v.rearrange("p (m t) -> p m t", t=cols)

        with nc.Block() as block:
            @block.sync
            def _(sp):
                def load_w(g, hh):
                    sp.dma_start(w_sb[:, hh, :, :, :], wqkvg[bass.ds(g * HG + hh, 1)].squeeze(0)).then_inc(w_in[hh], 16)
                    sp.dma_start(cw_sb[:, hh, :, :], convw[bass.ds(g * HG + hh, 1)].squeeze(0)).then_inc(w_in[hh], 16)

                def load_decay(g, hh, b):
                    sp.dma_start(decay_bc[:, b, :], decay_dram[bass.ds(g * HG + hh, 1), b * SEQ:(b + 1) * SEQ].squeeze(0)
                                 .partition_broadcast(P)).then_inc(decay_in[b], 16)

                def during_front(g, last, sub_g, back_g):
                    for p in range(PAIRS):
                        hh, b = divmod(p, B)
                        if p == 1 and sub_g is not None:
                            after_substitution(sub_g, back_g)
                        if last and hh == HG - 1:
                            break
                        until(sp, post_k, PAIRS, g, p + 1)
                        load_decay(g + (hh + 1) // HG, (hh + 1) % HG, b)
                        if b == B - 1 and not last:
                            until(sp, post_m, 2 * PAIRS, g, 2 * p + 2)
                            load_w(g + 1, hh)
                    until(sp, post_m, 2 * PAIRS, g, 2 * PAIRS)
                    for i in range(NB):
                        sp.dma_start(lower_dram[i].rearrange("m j t -> j m t"),
                                     masks[i * BLK:(i + 1) * BLK, g % 2 if isinstance(g, int) else parity[0], :, 0, i * BLK:(i + 1) * BLK]
                                     ).then_inc(blocks_out, 16)
                    sp.wait_ge(blocks_out, g * (16 * NB) + 16 * NB)
                    sp.dma_start(sub_in, lower_dram.rearrange("i m j t -> (i m) j t")).then_inc(blocks_in, 16)

                def after_substitution(g, back_g):
                    until(sp, inverted, 1, g, 1)
                    sp.dma_start(invT_dram.rearrange("i m j t -> (i m) j t"), sub_inv).then_inc(inv_out, 16)
                    until(sp, inverse_t, 1, g, 1)
                    sp.dma_start(inv_dram.rearrange("i m j t -> (i m) j t"), sub_in).then_inc(inv_out, 16)
                    sp.wait_ge(inv_out, g * 32 + 32)
                    until(sp, y_done, SLOTS, back_g, 0)
                    for i in range(NB):
                        sp.dma_start(invT[i * BLK:(i + 1) * BLK, :, i * BLK:(i + 1) * BLK],
                                     invT_dram[i].rearrange("m j t -> j m t")).then_inc(inv_in, 16)
                    for i in range(2):
                        sp.dma_start(inv64[i * BLK:(i + 1) * BLK, :, i * BLK:(i + 1) * BLK],
                                     inv_dram[i].rearrange("m j t -> j m t")).then_inc(inv_in, 16)
                    sp.dma_start(inv32, inv_dram[2].rearrange("m j t -> j m t")).then_inc(inv_in, 16)

                def load_wo(g, par):
                    until(sp, wo_added, 4, g, 0)
                    sp.dma_start(wo_sb[:, par, :, :], wo[bass.ds(g * HG, HG)].rearrange("h e d -> e h d")).then_inc(wo_in, 16)

                parity = [0]
                load_w(0, 0)
                load_decay(0, 0, 0)
                load_decay(0, 0, 1)
                load_w(0, 1)
                during_front(0, False, None, 0)
                with sp.Fori(0, GROUPS // 2 - 1) as it:
                    for half_no in range(2):
                        g = it * 2 + half_no
                        parity[0] = 1 - half_no
                        load_wo(g, half_no)
                        during_front(g + 1, False, g, g)
                load_wo(LAST - 1, 0)
                during_front(LAST, True, LAST - 1, LAST - 1)
                after_substitution(LAST, LAST)
                load_wo(LAST, 1)
                sp.wait_ge(inv_in, GROUPS * 112)

            @block.tensor
            def _(pe):
                def front(g, par, back_g):
                    def project(p, types):
                        hh, b = divmod(p, B)
                        if b == 0 and types[0] == 0:
                            pe.wait_ge(w_in[hh], g * 32 + 32)
                        for typ in types:
                            if p == 0:
                                until(pe, wo_added, 4, back_g, 0)
                            if typ < 3:
                                until(pe, conv_done, 3 * PAIRS, g, 3 * (p - 1) + typ + 1 if p else 0)
                            else:
                                until(pe, silu_done, 4 * PAIRS, g, 4 * p)
                            for k in range(KD):
                                s = nc.tensor.matmul(bank[typ][:, :], w_sb[:, hh, k, typ, :], normedT[:, k, tokens(b)],
                                                     start=k == 0, stop=k == KD - 1)
                            s.then_inc(proj_done, 1)

                    def sums_and_v(p):
                        until(pe, post_k, PAIRS, g, p)
                        for qk in range(2):
                            until(pe, squared, 2 * PAIRS, g, 2 * p + qk + 1)
                            for c in range(NC):
                                s = nc.tensor.matmul(bank[4][:, qk * NC + c:qk * NC + c + 1], squares[:, qk, c * P:(c + 1) * P],
                                                     ones[:, 0:1], start=True, stop=True)
                            s.then_inc(sums_done, 1)
                        until(pe, silu_done, 4 * PAIRS, g, 4 * p + 3)
                        until(pe, post_v, PAIRS, g, p)
                        for c in range(NC):
                            s = nc.tensor.transpose(bank[5][:, c * P:(c + 1) * P], vT[:, p % 2, c * P:(c + 1) * P], ident[:, :])
                        s.then_inc(turned_v, 1)

                    def products_and_k(p):
                        hh, b = divmod(p, B)
                        for c in range(NC):
                            if c % 2 == 0:
                                until(pe, post_m, 2 * PAIRS, g, 2 * (p - 1) + c // 2 + 1 if p else 0)
                            o = bank[6 + c // 2][:, (c % 2) * 2 * P:(c % 2 + 1) * 2 * P]
                            kk = kT[:, par, hh, tokens(b, c)]
                            nc.tensor.matmul(o[:, 0:P], kk, kk, start=True, stop=True)
                            s = nc.tensor.matmul(o[:, P:2 * P], kk, qT[:, par, hh, tokens(b, c)], start=True, stop=True)
                            if c % 2 == 1:
                                s.then_inc(products, 1)
                        until(pe, sums_read, PAIRS, g, p + 1)
                        for c in range(NC):
                            s = nc.tensor.transpose(bank[4][:, c * P:(c + 1) * P], kT[:, par, hh, tokens(b, c)], ident[:, :])
                        s.then_inc(turned_k, 1)

                    for p in range(PAIRS + 1):
                        if p < PAIRS:
                            project(p, (0, 1))
                        if p > 0:
                            sums_and_v(p - 1)
                        if p < PAIRS:
                            project(p, (2, 3))
                        if p > 0:
                            products_and_k(p - 1)

                def merge(g, par, front_g):
                    until(pe, conv_done, 3 * PAIRS, front_g, 3 * PAIRS)
                    until(pe, silu_done, 4 * PAIRS, front_g, 4 * PAIRS)
                    until(pe, post_k, PAIRS, front_g, PAIRS)
                    until(pe, inv_in, 112, g, 112 - 1, alone=True)
                    for m in range(M):
                        s = nc.tensor.matmul(bank[0][32:64, m * BLK:(m + 1) * BLK], masks[0:32, par, m, 0, 32:64], inv64[0:32, m, 0:32],
                                             start=True, stop=True)
                    s.then_inc(merge_mm, 1)
                    for m in range(M):
                        s = nc.tensor.matmul(bank[2][96:128, m * BLK:(m + 1) * BLK], masks[64:96, par, m, 0, 96:128], inv32[:, m, :],
                                             start=True, stop=True)
                    s.then_inc(merge_mm, 1)
                    until(pe, merge_v, 5, g, 1, alone=True)
                    for m in range(M):
                        w = slice(m * BLK, (m + 1) * BLK)
                        nc.tensor.matmul(bank[6][32:64, w], invT[32:64, m, 32:64], cross[32:64, m, 0:32], start=True, stop=True)
                        s = nc.tensor.matmul(bank[4][0:32, w], cross[32:64, m, 0:32], invT[32:64, m, 32:64], start=True, stop=True)
                    s.then_inc(merge_mm, 1)
                    until(pe, merge_s, 4, g, 1, alone=True)
                    for m in range(M):
                        s = nc.tensor.matmul(bank[1][64:96, m * BLK:(m + 1) * BLK], cross[96:128, m, 0:32], invT[96:128, m, 96:128],
                                             start=True, stop=True)
                    s.then_inc(merge_mm, 1)
                    for e in range(2):
                        if e == 0:
                            until(pe, merge_s, 4, g, 2, alone=True)
                        for m in range(e * 8, e * 8 + 8):
                            s = nc.tensor.matmul(bank[3 + 2 * e][64:128, (m % 8) * 64:(m % 8 + 1) * 64], masks[0:64, par, m, 0, 64:128],
                                                 inv64[0:64, m, :], start=True, stop=True)
                        s.then_inc(merge_mm, 1)
                    for e in range(2):
                        until(pe, merge_v, 5, g, 4, alone=True)
                        if e == 1:
                            until(pe, merge_s, 4, g, 3, alone=True)
                        for m in range(e * 8, e * 8 + 8):
                            s = nc.tensor.matmul(bank[(7, 0)[e]][0:64, (m % 8) * 64:(m % 8 + 1) * 64], cross[64:128, m, :],
                                                 invT[64:128, m, 64:128], start=True, stop=True)
                        s.then_inc(merge_mm, 1)

                def back(g, par):
                    def output_read(j):
                        if j < STREAMS:
                            until(pe, inner_scaled, SLOTS, g, j + 1)
                        else:
                            until(pe, o_done, KS_SLOTS, g, j - STREAMS + 1)

                    for i in range(SLOTS + 3):
                        if STREAMS <= i < SLOTS:
                            c, s_no, hh, b, m = slot(i)
                            until(pe, state_done, KS_SLOTS, g, i - STREAMS + 1)
                            until(pe, y_copied, SLOTS, g, i - 2)
                            nc.tensor.matmul(bank[i % 3][:, 0:P], kT[:, par, hh, tokens(b, c)], state[:, s_no, :],
                                             start=True, stop=True).then_inc(ks_done, 1)
                        if 1 <= i <= SLOTS:
                            j = i - 1
                            c, s_no, hh, b, m = slot(j)
                            if j == 0:
                                until(pe, merge_v, 5, g, 5)
                                until(pe, merge_s, 4, g, 4)
                            if c == 0:
                                if j >= 3:
                                    until(pe, y_copied, SLOTS, g, j - 2)
                                rhs = vk[:, par, 0, hh, b * NC, :]
                            else:
                                until(pe, rhs_done, KS_SLOTS, g, j - STREAMS + 1)
                                rhs = rhs_sb[:, j % 2, :]
                            nc.tensor.matmul(bank[j % 3][:, 0:P], invT[:, m, :], rhs, start=True, stop=True).then_inc(y_done, 1)
                        if 2 <= i <= SLOTS + 1:
                            j = i - 2
                            c, s_no, hh, b, m = slot(j)
                            bk = bank[3 + j % 2]
                            if j >= 2:
                                output_read(j - 2)
                            if c > 0:
                                nc.tensor.matmul(bk[:, P:2 * P], qT[:, par, hh, tokens(b, c)], state[:, s_no, :],
                                                 start=True, stop=True)
                            until(pe, y_copied, SLOTS, g, j + 1)
                            if c < NC - 1:
                                until(pe, state_done, KS_SLOTS, g, j)
                                nc.tensor.matmul(bank[5][:, 0:P], vk[:, par, 1, hh, b * NC + c, :], y_sb[:, j % 2, :],
                                                 start=True, stop=True).then_inc(gain_done, 1)
                            nc.tensor.matmul(bk[:, 0:P], masks[:, par, m, 1, :], y_sb[:, j % 2, :],
                                             start=True, stop=True).then_inc(inner_done, 1)
                        if 3 <= i:
                            j = i - 3
                            output_read(j)
                            if j % 4 == 0:
                                until(pe, o_gated, NC, g, max(j // 4 - 1, 0))
                            nc.tensor.transpose(bank[6 + (j // 4) % 2][:, (j % 4) * P:(j % 4 + 1) * P], o_sb[:, j % 2, :],
                                                ident[:, :]).then_inc(o_turned, 1)

                    pe.wait_ge(wo_in, g * 16 + 16)
                    until(pe, o_gated, NC, g, NC)
                    for n in range(NT):
                        for hh in range(HG):
                            s = nc.tensor.matmul(bank[n // 2][:, (n % 2) * D:(n % 2 + 1) * D], gated[:, par, hh, n * P:(n + 1) * P],
                                                 wo_sb[:, par, hh, :], start=hh == 0, stop=hh == HG - 1)
                        if n % 2:
                            s.then_inc(wo_done, 1)

                front(0, 0, 0)
                with pe.Fori(0, GROUPS // 2 - 1) as it:
                    for half_no in range(2):
                        g = it * 2 + half_no
                        front(g + 1, 1 - half_no, g)
                        merge(g, half_no, g + 1)
                        back(g, half_no)
                front(LAST, 1, LAST - 1)
                merge(LAST - 1, 0, LAST)
                back(LAST - 1, 0)
                until(pe, wo_added, 4, LAST, 0)
                merge(LAST, 1, LAST)
                back(LAST, 1)

            @block.scalar
            def _(act):
                def turn_inverse(g):
                    until(act, inverted, 1, g, 1)
                    nc.scalar.copy(sub_in, sub_inv.rearrange("p a b -> p b a")).then_inc(inverse_t, 1)

                def front(g, par, sub_g):
                    def outer_taps(u):
                        p, typ = divmod(u, 3)
                        hh, b = divmod(p, B)
                        if b == 0 and typ == 0:
                            act.wait_ge(w_in[hh], g * 32 + 32)
                        until(act, proj_done, 4 * PAIRS, g, 4 * p + typ + 1)
                        if u >= 2:
                            until(act, silu_done, 4 * PAIRS, g, (u - 2) // 3 * 4 + (u - 2) % 3 + 1)
                        else:
                            until(act, silu_done, 4 * PAIRS, g, 0)
                        nc.scalar.activation(conv[:, u % 2, :], bank[typ][:, :], ACT.Copy,
                                             scale=cw_sb[:, hh, typ, 3:4]).then_inc(far_done, 1)
                        until(act, near_done, 3 * PAIRS, g, max(u - 1, 0))
                        nc.scalar.activation(conv_far[:, u % 2, 3:512], bank[typ][:, 0:509], ACT.Copy,
                                             scale=cw_sb[:, hh, typ, 0:1]).then_inc(far_done, 1)

                    def silu(u):
                        p, typ = divmod(u, 3)
                        hh, b = divmod(p, B)
                        until(act, conv_done, 3 * PAIRS, g, u + 1)
                        if typ == 2:
                            until(act, turned_v, PAIRS, g, max(p - 1, 0))
                        dst = (qT[:, par, hh, tokens(b)], kT[:, par, hh, tokens(b)], vT[:, p % 2, :])[typ]
                        nc.scalar.activation(dst, conv[:, u % 2, :], ACT.Silu).then_inc(silu_done, 1)
                        if typ == 2:
                            until(act, proj_done, 4 * PAIRS, g, 4 * p + 4)
                            nc.scalar.activation(gated[:, par, hh, tokens(b)], bank[3][:, :], ACT.Silu).then_inc(silu_done, 1)

                    def scaled_v(p):
                        hh, b = divmod(p, B)
                        until(act, rooted, PAIRS, g, p + 1)
                        until(act, turned_v, PAIRS, g, p + 1)
                        for c in range(NC):
                            s = nc.scalar.activation(vk[:, par, 0, hh, b * NC + c, :], bank[5][:, c * P:(c + 1) * P], ACT.Copy,
                                                     scale=norms[:, 1, NC + c:NC + c + 1])
                        s.then_inc(post_v, 1)

                    for u in range(3 * PAIRS + 3):
                        if u < 3 * PAIRS:
                            outer_taps(u)
                        if 0 < u <= 3 * PAIRS:
                            silu(u - 1)
                        if u == 3 + TURN_AT and sub_g is not None:
                            turn_inverse(sub_g)
                        if u >= 5 and u % 3 == 2:
                            scaled_v(u // 3 - 1)

                def merge(g):
                    until(act, merge_mm, 8, g, 2)
                    nc.scalar.mul(cross[96:128, :, 0:32], blocks_of(bank[2][96:128, :], 32), -1.0).then_inc(merge_s, 1)
                    until(act, merge_mm, 8, g, 3)
                    nc.scalar.copy(inv64[32:64, :, 0:32], blocks_of(bank[6][32:64, :], 32)).then_inc(merge_s, 1)
                    until(act, merge_mm, 8, g, 6)
                    nc.scalar.mul(cross[64:128, 8:16, :], blocks_of(bank[5][64:128, :], 64), -1.0).then_inc(merge_s, 1)
                    until(act, merge_mm, 8, g, 8)
                    nc.scalar.copy(invT[0:64, 8:16, 64:128], blocks_of(bank[0][0:64, :], 64)).then_inc(merge_s, 1)

                def back(g, par):
                    def inner(i):
                        c, s_no, hh, b, m = slot(i)
                        until(act, inner_done, SLOTS, g, i + 1)
                        until(act, o_turned, SLOTS, g, max(i - 1, 0))
                        nc.scalar.activation(o_sb[:, i % 2, :], bank[3 + i % 2][:, 0:P], ACT.Copy,
                                             scale=qk_scales[:, par, hh, b * NC + c, 1:2]).then_inc(inner_scaled, 1)

                    for i in range(SLOTS + 1):
                        if i < SLOTS:
                            until(act, y_done, SLOTS, g, i + 1)
                            until(act, inner_done, SLOTS, g, max(i - 1, 0))
                            nc.scalar.copy(y_sb[:, i % 2, :], bank[i % 3][:, 0:P]).then_inc(y_copied, 1)
                        if i > 0:
                            inner(i - 1)

                front(0, 0, None)
                with act.Fori(0, GROUPS // 2 - 1) as it:
                    for half_no in range(2):
                        g = it * 2 + half_no
                        front(g + 1, 1 - half_no, g)
                        merge(g)
                        back(g, half_no)
                front(LAST, 1, LAST - 1)
                merge(LAST - 1)
                back(LAST - 1, 0)
                turn_inverse(LAST)
                merge(LAST)
                back(LAST, 1)

            @block.gpsimd
            def _(pool):
                def front(g, par):
                    def add_outer(u):
                        until(pool, far_done, 6 * PAIRS, g, 2 * u + 2)
                        nc.gpsimd.tensor_tensor(conv[:, u % 2, :], conv[:, u % 2, :], conv_far[:, u % 2, :],
                                                ALU.add).then_inc(near_done, 1)

                    def square(p):
                        hh, b = divmod(p, B)
                        for qk, src in enumerate((qT, kT)):
                            until(pool, silu_done, 4 * PAIRS, g, 4 * p + qk + 1)
                            until(pool, sums_done, 2 * PAIRS, g, max(2 * (p - 1) + qk + 1, 0))
                            s = src[:, par, hh, tokens(b)]
                            nc.gpsimd.tensor_tensor(squares[:, qk, :], s, s, ALU.mult).then_inc(squared, 1)

                    def roots(p):
                        until(pool, sums_read, PAIRS, g, p + 1)
                        until(pool, post_v, PAIRS, g, p)
                        nc.gpsimd.tensor_tensor(norms[:, 1, :], norms[:, 0, :], half[:, :], ALU.pow).then_inc(rooted, 1)

                    def impulse(p):
                        hh, b = divmod(p, B)
                        until(pool, scaled, PAIRS, g, p + 1)
                        until(pool, post_k, PAIRS, g, p)
                        nc.gpsimd.tensor_tensor(decayed[:, :, :], ident[:, :].unsqueeze(1).to_broadcast([P, NC, P]),
                                                qk_scales[:, par, hh, b * NC:(b + 1) * NC, 3:4].to_broadcast([P, NC, P]),
                                                ALU.mult).then_inc(impulses, 1)

                    for p in range(PAIRS + 1):
                        if p < PAIRS:
                            add_outer(3 * p)
                        if p > 0:
                            roots(p - 1)
                        if p < PAIRS:
                            add_outer(3 * p + 1)
                        if p > 0:
                            impulse(p - 1)
                        if p < PAIRS:
                            add_outer(3 * p + 2)
                            square(p)
                    if not isinstance(g, int) or g > 0:
                        wait_alone(pool, inv_out, g * 32)
                    nc.gpsimd.memset(sub_inv, 0.0).then_inc(cleared, 1)
                    until(pool, cleared, 2, g, 1, alone=True)
                    nc.gpsimd.memset(sub_inv.rearrange("p a b -> p (a b)")[:, 0:BLK * BLK:BLK + 1], 1.0).then_inc(cleared, 1)

                front(0, 0)
                with pool.Fori(0, GROUPS // 2 - 1) as it:
                    for half_no in range(2):
                        front(it * 2 + (half_no + 1), 1 - half_no)
                front(LAST, 1)

            @block.vector
            def _(dve):
                def substitute(g, k):
                    s, part = divmod(k, 2)
                    rows_n, cols = s + 1, BLK - 1 - s
                    tmp = sub_tmp[0:NB * M, 0:rows_n * cols].rearrange("p (a b) -> p a b", a=rows_n)
                    rest = sub_inv[:, 0:rows_n, s + 1:BLK]
                    if k == 0:
                        dve.wait_ge(blocks_in, g * 16 + 16)
                        until(dve, cleared, 2, g, 2)
                    else:
                        until(dve, sub_step, SUB_STEPS - 1, g, k)
                    if part == 0:
                        ins = nc.vector.tensor_tensor(tmp, sub_inv[:, 0:rows_n, s:s + 1].to_broadcast([NB * M, rows_n, cols]),
                                                      sub_in[:, s:s + 1, s + 1:BLK].to_broadcast([NB * M, rows_n, cols]), ALU.mult)
                    else:
                        ins = nc.vector.tensor_tensor(rest, rest, tmp, ALU.subtract)
                    ins.then_inc(*((sub_step, 1) if k < SUB_STEPS - 1 else (inverted, 1)))

                def front(g, par, sub_g):
                    count = [0]

                    def step(ins):
                        count[0] += 1
                        ins.then_inc(front_step, 1)
                        until(dve, front_step, FRONT_STEPS, g, count[0])

                    def inner_taps(u):
                        p, typ = divmod(u, 3)
                        hh, b = divmod(p, B)
                        until(dve, near_done, 3 * PAIRS, g, u + 1)
                        step(nc.vector.scalar_tensor_tensor(conv[:, u % 2, 1:512], bank[typ][:, 0:511],
                                                            cw_sb[:, hh, typ, 2:3], conv[:, u % 2, 1:512],
                                                            ALU.mult, ALU.add))
                        nc.vector.scalar_tensor_tensor(conv[:, u % 2, 2:512], bank[typ][:, 0:510],
                                                       cw_sb[:, hh, typ, 1:2], conv[:, u % 2, 2:512],
                                                       ALU.mult, ALU.add).then_inc(conv_done, 1)

                    def scales(p):
                        hh, b = divmod(p, B)
                        sc = qk_scales[:, par, hh, b * NC:(b + 1) * NC, :]
                        until(dve, sums_done, 2 * PAIRS, g, 2 * p + 2)
                        nc.vector.tensor_scalar(norms[:, 0, :], bank[4][:, 0:8], NORM_EPS2, None, ALU.max).then_inc(sums_read, 1)
                        until(dve, sums_read, PAIRS, g, p + 1)
                        step(nc.vector.reciprocal(sc[:, :, 3:4], norms[:, 0, NC:2 * NC].unsqueeze(2)))
                        nc.vector.tensor_tensor(sc[:, :, 3:4], sc[:, :, 3:4],
                                                alpha_beta[:, b * NC:(b + 1) * NC, bass.ds(g * HG + (HEADS + hh), 1)],
                                                ALU.mult).then_inc(scaled, 1)

                    def over_q(p):
                        hh, b = divmod(p, B)
                        sc = qk_scales[:, par, hh, b * NC:(b + 1) * NC, :]
                        until(dve, rooted, PAIRS, g, p + 1)
                        step(nc.vector.reciprocal(sc[:, :, 1:2], norms[:, 1, 0:NC].unsqueeze(2)))
                        step(nc.vector.tensor_tensor(sc[:, :, 2:3], sc[:, :, 1:2],
                                                     decay_from_start[:, b * NC:(b + 1) * NC, bass.ds(g * HG + hh, 1)], ALU.mult))

                    def chunk_mats(p):
                        hh, b = divmod(p, B)
                        until(dve, impulses, PAIRS, g, p + 1)
                        dve.wait_ge(decay_in[b], g * (16 * HG) + 16 * (hh + 1))
                        step(nc.vector.tensor_tensor_scan(decayed[:, :, :].rearrange("p c t -> p (c t)"), decay_bc[:, b, :],
                                                          decayed[:, :, :].rearrange("p c t -> p (c t)"), 0.0, ALU.mult, ALU.add))
                        for c2 in range(2):
                            until(dve, products, 2 * PAIRS, g, 2 * p + c2 + 1)
                            m = hh * NT + b * NC + 2 * c2
                            nc.vector.tensor_tensor(masks[:, par, m:m + 2, :, :],
                                                    bank[6 + c2][:, :].rearrange("p (c a t) -> p c a t", c=2, a=2),
                                                    decayed[:, 2 * c2:2 * c2 + 2, :].unsqueeze(2).to_broadcast([P, 2, 2, P]),
                                                    ALU.mult).then_inc(post_m, 1)
                        until(dve, turned_k, PAIRS, g, p + 1)
                        nc.vector.tensor_tensor(vk[:, par, 1, hh, b * NC:(b + 1) * NC, :],
                                                bank[4][:, :].rearrange("p (c e) -> p c e", c=NC),
                                                decayed[:, :, P - 1:P].to_broadcast([P, NC, P]), ALU.mult).then_inc(post_k, 1)

                    def substitute_some(place):
                        if sub_g is not None and place < 6:
                            for k in range(SUB_STEPS - SUB_FRONT + place * SUB_FRONT // 6,
                                           SUB_STEPS - SUB_FRONT + (place + 1) * SUB_FRONT // 6):
                                substitute(sub_g, k)

                    for p in range(PAIRS + 1):
                        if p < PAIRS:
                            inner_taps(3 * p)
                            substitute_some(3 * p)
                        if p > 0:
                            scales(p - 1)
                        if p < PAIRS:
                            inner_taps(3 * p + 1)
                            substitute_some(3 * p + 1)
                        if p > 0:
                            over_q(p - 1)
                        if p < PAIRS:
                            inner_taps(3 * p + 2)
                            substitute_some(3 * p + 2)
                        if p > 0:
                            chunk_mats(p - 1)
                    assert count[0] == FRONT_STEPS, count[0]

                def merge(g):
                    until(dve, merge_mm, 8, g, 1)
                    nc.vector.tensor_scalar(cross[32:64, :, 0:32], blocks_of(bank[0][32:64, :], 32), -1.0, None, ALU.mult).then_inc(merge_v, 1)
                    until(dve, merge_mm, 8, g, 3)
                    nc.vector.tensor_copy(invT[0:32, :, 32:64], blocks_of(bank[4][0:32, :], 32)).then_inc(merge_v, 1)
                    until(dve, merge_mm, 8, g, 4)
                    nc.vector.tensor_copy(invT[64:96, :, 96:128], blocks_of(bank[1][64:96, :], 32)).then_inc(merge_v, 1)
                    until(dve, merge_mm, 8, g, 5)
                    nc.vector.tensor_scalar(cross[64:128, 0:8, :], blocks_of(bank[3][64:128, :], 64), -1.0, None, ALU.mult).then_inc(merge_v, 1)
                    until(dve, merge_mm, 8, g, 7)
                    nc.vector.tensor_copy(invT[0:64, 0:8, 64:128], blocks_of(bank[7][0:64, :], 64)).then_inc(merge_v, 1)

                def back(g, par, sub_g):
                    def right_side(i):
                        c, s_no, hh, b, m = slot(i)
                        n = b * NC + c
                        until(dve, ks_done, KS_SLOTS, g, i - STREAMS + 1)
                        until(dve, y_done, SLOTS, g, i - 1)
                        nc.vector.scalar_tensor_tensor(rhs_sb[:, i % 2, :], bank[i % 3][:, 0:P],
                                                       neg_decay[:, n, bass.ds(g * HG + hh, 1)], vk[:, par, 0, hh, n, :],
                                                       ALU.mult, ALU.add).then_inc(rhs_done, 1)

                    def gain(i):
                        c, s_no, hh, b, m = slot(i)
                        until(dve, gain_done, KS_SLOTS, g, i + 1)
                        if c == 0:
                            nc.vector.tensor_copy(state[:, s_no, :], bank[5][:, 0:P]).then_inc(state_done, 1)
                        else:
                            nc.vector.scalar_tensor_tensor(state[:, s_no, :], state[:, s_no, :],
                                                           chunk_decay[:, bass.ds(g * HG + hh, 1), b * NC + c], bank[5][:, 0:P],
                                                           ALU.mult, ALU.add).then_inc(state_done, 1)

                    def outputs(i):
                        c, s_no, hh, b, m = slot(i)
                        until(dve, inner_scaled, SLOTS, g, i + 1)
                        nc.vector.scalar_tensor_tensor(o_sb[:, i % 2, :], bank[3 + i % 2][:, P:2 * P],
                                                       qk_scales[:, par, hh, b * NC + c, 2:3], o_sb[:, i % 2, :],
                                                       ALU.mult, ALU.add).then_inc(o_done, 1)

                    def gate(c):
                        until(dve, o_turned, SLOTS, g, 4 * c + 4)
                        v = gated[:, par, :, :].rearrange("p h (b t) -> p h b t", b=B)[:, :, :, c * P:(c + 1) * P]
                        nc.vector.tensor_tensor(v, v, bank[6 + c % 2][:, :].rearrange("p (h b t) -> p h b t", h=HG, b=B),
                                                ALU.mult).then_inc(o_gated, 1)

                    for i in range(SLOTS + 3):
                        if STREAMS <= i < SLOTS:
                            right_side(i)
                        if 2 <= i < KS_SLOTS + 2:
                            gain(i - 2)
                        if STREAMS + 2 <= i <= SLOTS + 1:
                            outputs(i - 2)
                        if i >= 6 and (i - 6) % 4 == 0:
                            gate((i - 6) // 4)
                        if sub_g is not None and i < SLOTS:
                            for k in range(i * SUB_BACK // SLOTS, (i + 1) * SUB_BACK // SLOTS):
                                substitute(sub_g, k)

                    for q in range(4):
                        if sub_g is not None:
                            for k in range(SUB_BACK + q * SUB_OUT // 4, SUB_BACK + (q + 1) * SUB_OUT // 4):
                                substitute(sub_g, k)
                        until(dve, wo_done, 4, g, q + 1)
                        nc.vector.tensor_tensor(resid[:, 2 * q:2 * q + 2, :], resid[:, 2 * q:2 * q + 2, :],
                                                bank[q][:, :].rearrange("p (n d) -> p n d", n=2), ALU.add).then_inc(wo_added, 1)

                front(0, 0, None)
                for k in range(SUB_STEPS - SUB_FRONT):
                    substitute(0, k)
                with dve.Fori(0, GROUPS // 2 - 1) as it:
                    for half_no in range(2):
                        g = it * 2 + half_no
                        front(g + 1, 1 - half_no, g)
                        merge(g)
                        back(g, half_no, g + 1)
                front(LAST, 1, LAST - 1)
                merge(LAST - 1)
                back(LAST - 1, 0, LAST)
                for k in range(SUB_STEPS - SUB_FRONT, SUB_STEPS):
                    substitute(LAST, k)
                merge(LAST)
                back(LAST, 1, None)

        e_small, e_w = sem("e_small"), [sem("e_w_even"), sem("e_w_odd")]
        var3, std3, normed3, turned3, turned_sb3 = sem("var3"), sem("std3"), sem("normed3"), sem("turned3"), sem("turned_sb3")
        logits_ready, shifted, exped, top_shift, top_exp = sem("logits_ready"), sem("shifted"), sem("exped"), sem("top_shift"), sem("top_exp")
        picks, pick_sums, weights_ready, wT_ready, wT_sb = sem("picks"), sem("pick_sums"), sem("weights_ready"), sem("wT_ready"), sem("wT_sb")
        bias_mm, bias_sb = sem("bias_mm"), sem("bias_sb")
        expert_no_ready = sem("expert_no_ready")
        h_mm, h_sb, y_mm, y_acc = sem("h_mm"), sem("h_sb"), sem("y_mm"), sem("y_acc")
        pool_mm, pool_sb, hid_mm, hid_sb, phi_mm, phi_z, phi_exp = (sem("pool_mm"), sem("pool_sb"), sem("hid_mm"), sem("hid_sb"),
                                                                    sem("phi_mm"), sem("phi_z"), sem("phi_exp"))
        final, stored = sem("final"), sem("stored")
        step3 = sem("step3")
        H_PER, Y_PER = 2 * KI, NT

        with nc.Block() as block:
            @block.sync
            def _(sp):
                small_loads = [(wr_sb, wr), (br_sb, br.partition_broadcast(P)), (b1_sb, b1), (b2_sb[0:E, :], b2),
                               (wp1_sb, wp1), (bp1_sb, bp1), (wp2_sb, wp2), (bp2_sb, bp2.partition_broadcast(P))]
                for dst, src in small_loads:
                    sp.dma_start(dst, src).then_inc(e_small, 16)
                with sp.Fori(0, E // 2) as pair:
                    for par in range(2):
                        sp.wait_ge(y_mm, pair * 2 * Y_PER if par == 1 else pair * 2 * Y_PER)
                        sp.dma_start(w1_sb[par], w1[bass.ds(pair * 2 + par, 1)].squeeze(0).rearrange("(k p) i -> p k i", p=P)).then_inc(e_w[par], 16)
                        sp.dma_start(w2_sb[par], w2[bass.ds(pair * 2 + par, 1)].squeeze(0).rearrange("(k p) d -> p k d", p=P)).then_inc(e_w[par], 16)
                sp.wait_ge(final, NT)
                sp.dma_start(out.rearrange("(n p) d -> p n d", p=P), resid[:, :, :]).then_inc(stored, 16)
                sp.wait_ge(stored, 16)

            @block.gpsimd
            def _(pool):
                nc.gpsimd.iota(expert_no, pattern=[[1, E]], base=0, channel_multiplier=0,
                               allow_small_or_imprecise_dtypes=True).then_inc(expert_no_ready, 1)

            @block.scalar
            def _(act):
                act.wait_ge(var3, 1)
                nc.scalar.activation(rstd[:, :].unsqueeze(2), mean_var[:, :, 1:2], ACT.Sqrt, bias=eps_col[:, :]).then_inc(std3, 1)
                act.wait_ge(shifted, 1)
                nc.scalar.activation(probs, logits, ACT.Exp).then_inc(exped, 1)
                act.wait_ge(top_shift, 1)
                nc.scalar.activation(top_w, top_w, ACT.Exp).then_inc(top_exp, 1)
                with act.Fori(0, E // 2) as pair:
                    for par in range(2):
                        for r in range(H_PER):
                            k, half_no = divmod(r, 2)
                            wait_alone(act, h_mm, pair * 2 * H_PER + par * H_PER + r + 1)
                            nc.scalar.activation(hT[par][:, k, half_no * 512:(half_no + 1) * 512], bank[r % 4][:, :], ACT.Relu,
                                                 bias=b1_sb[:, bass.ds(pair * 2 + par, 1), k]).then_inc(h_sb, 1)
                act.wait_ge(phi_z, 1)
                nc.scalar.activation(phi, phi, ACT.Exp, scale=-1.0).then_inc(phi_exp, 1)

            @block.tensor
            def _(pe):
                pe.wait_ge(normed3, 1)
                for k in range(KD):
                    for n in range(NT):
                        b_no = 2 * k + n // 4
                        s = nc.tensor.transpose(bank[b_no][:, (n % 4) * P:(n % 4 + 1) * P], normed[:, n, k * P:(k + 1) * P],
                                                ident[:, :])
                        if n % 4 == 3:
                            s.then_inc(turned3, 1)
                pe.wait_ge(turned_sb3, 4)
                pe.wait_ge(e_small, 128)
                for n in range(NT):
                    for k in range(KD):
                        s = nc.tensor.matmul(bank[4][:, n * E:(n + 1) * E], normedT[:, k, n * P:(n + 1) * P], wr_sb[:, k, :],
                                             start=k == 0, stop=k == KD - 1)
                s.then_inc(logits_ready, 1)
                pe.wait_ge(picks, 1)
                nc.tensor.matmul(bank[5][:, 0:2 * E], ones[:, :], pick_sum, start=True, stop=True).then_inc(pick_sums, 1)
                pe.wait_ge(weights_ready, 1)
                for n in range(NT):
                    s = nc.tensor.transpose(bank[6 + n // 4][0:E, (n % 4) * P:(n % 4 + 1) * P], token_w[:, n, :], ident[:, :])
                s.then_inc(wT_ready, 1)
                pe.wait_ge(wT_sb, 1)
                for n in range(NT):
                    s = nc.tensor.matmul(bank[n // 2][:, (n % 2) * D:(n % 2 + 1) * D], token_wT[0:E, n * P:(n + 1) * P], b2_sb[0:E, :],
                                         start=True, stop=True)
                    if n % 2:
                        s.then_inc(bias_mm, 1)
                pe.wait_ge(bias_sb, 4)
                with pe.Fori(0, E // 2) as pair:
                    for par in range(2):
                        pe.wait_ge(e_w[par], pair * 32 + 32)
                        for r in range(H_PER):
                            k, half_no = divmod(r, 2)
                            pe.wait_ge(h_sb, pair * 2 * H_PER + max(par * H_PER + r - 3, 0))
                            for kd in range(KD):
                                s = nc.tensor.matmul(bank[r % 4][:, :], w1_sb[par][:, kd, k * P:(k + 1) * P],
                                                     normedT[:, kd, half_no * 512:(half_no + 1) * 512], start=kd == 0, stop=kd == KD - 1)
                            s.then_inc(h_mm, 1)
                        pe.wait_ge(h_sb, pair * 2 * H_PER + (par + 1) * H_PER)
                        for n in range(NT):
                            pe.wait_ge(y_acc, pair * 2 * Y_PER + max(par * Y_PER + n - 3, 0))
                            for k in range(KI):
                                s = nc.tensor.matmul(bank[4 + n % 4][:, 0:D], hT[par][:, k, n * P:(n + 1) * P], w2_sb[par][:, k, :],
                                                     start=k == 0, stop=k == KI - 1)
                            s.then_inc(y_mm, 1)
                pe.wait_ge(y_acc, E * Y_PER)
                for k in range(KD):
                    for b in range(B):
                        for c in range(NC):
                            s = nc.tensor.matmul(bank[0][:, k * B + b:k * B + b + 1], acc[:, b * NC + c, k * P:(k + 1) * P], ones[:, 0:1],
                                                 start=c == 0, stop=c == NC - 1)
                s.then_inc(pool_mm, 1)
                pe.wait_ge(pool_sb, 1)
                for k in range(KD):
                    s = nc.tensor.matmul(bank[1][:, 0:B], wp1_sb[:, k, :], pooled[:, k * B:(k + 1) * B], start=k == 0, stop=k == KD - 1)
                s.then_inc(hid_mm, 1)
                pe.wait_ge(hid_sb, 1)
                nc.tensor.matmul(bank[2][:, 0:B], wp2_bc, hidden, start=True, stop=True).then_inc(phi_mm, 1)

            @block.vector
            def _(dve):
                count = [0]

                def step(ins):
                    count[0] += 1
                    ins.then_inc(step3, 1)
                    dve.wait_ge(step3, count[0])

                layernorm(dve, step).then_inc(var3, 1)
                dve.wait_ge(std3, 1)
                apply_norm(dve, step).then_inc(normed3, 1)
                for k in range(4):
                    dve.wait_ge(turned3, k + 1)
                    nc.vector.tensor_copy(normedT[:, k // 2, (k % 2) * 512:(k % 2 + 1) * 512], bank[k][:, :]).then_inc(turned_sb3, 1)
                dve.wait_ge(e_small, 128)
                nc.vector.tensor_copy(wp2_bc, wp2_sb.to_broadcast([P, P]))
                dve.wait_ge(logits_ready, 1)
                step(nc.vector.tensor_tensor(logits, bank[4][:, 0:NT * E].rearrange("p (n e) -> p n e", n=NT),
                                             br_sb.unsqueeze(1).to_broadcast([P, NT, E]), ALU.add))
                step(nc.vector.tensor_reduce(row_max, logits, AX.X, ALU.max))
                nc.vector.tensor_tensor(logits, logits, row_max.unsqueeze(2).to_broadcast([P, NT, E]), ALU.subtract).then_inc(shifted, 1)
                dve.wait_ge(exped, 1)
                step(nc.vector.tensor_reduce(row_sum, probs, AX.X, ALU.add))
                step(nc.vector.reciprocal(row_inv, row_sum))
                step(nc.vector.tensor_tensor(probs, probs, row_inv.unsqueeze(2).to_broadcast([P, NT, E]), ALU.mult))
                for n in range(NT):
                    s = nc.vector.max(top8[:, n, :], probs[:, n, :])
                step(s)
                for n in range(NT):
                    s = nc.vector.max_index(top_idx[:, n, :], top8[:, n, :], probs[:, n, :])
                step(s)
                nc.vector.tensor_copy(top_no, top_idx[:, :, :])
                nc.vector.tensor_tensor(top_w, top8[:, :, 0:TOPK], top8[:, :, 0:1].to_broadcast([P, NT, TOPK]), ALU.subtract).then_inc(top_shift, 1)
                dve.wait_ge(top_exp, 1)
                step(nc.vector.tensor_reduce(top_sum, top_w, AX.X, ALU.add))
                step(nc.vector.reciprocal(top_sum, top_sum))
                step(nc.vector.tensor_tensor(top_w, top_w, top_sum.unsqueeze(2).to_broadcast([P, NT, TOPK]), ALU.mult))
                dve.wait_ge(expert_no_ready, 1)
                for k in range(TOPK):
                    one = pick_one if k else picked[:, :, 0:E]
                    step(nc.vector.tensor_tensor(one, expert_no.unsqueeze(1).to_broadcast([P, NT, E]),
                                                 top_no[:, :, k:k + 1].to_broadcast([P, NT, E]), ALU.is_equal))
                    if k:
                        step(nc.vector.tensor_tensor(picked[:, :, 0:E], picked[:, :, 0:E], pick_one, ALU.add))
                        step(nc.vector.tensor_tensor(pick_one, pick_one, top_w[:, :, k:k + 1].to_broadcast([P, NT, E]), ALU.mult))
                        step(nc.vector.tensor_tensor(picked[:, :, E:2 * E], picked[:, :, E:2 * E], pick_one, ALU.add))
                    else:
                        step(nc.vector.tensor_tensor(picked[:, :, E:2 * E], one, top_w[:, :, 0:1].to_broadcast([P, NT, E]), ALU.mult))
                nc.vector.tensor_reduce(pick_sum, picked.rearrange("p n e -> p e n"), AX.X, ALU.add).then_inc(picks, 1)
                dve.wait_ge(pick_sums, 1)
                step(nc.vector.tensor_scalar(expert_w[:, 0:E], bank[5][:, 0:E], 1.0, None, ALU.max))
                step(nc.vector.reciprocal(expert_w[:, 0:E], expert_w[:, 0:E]))
                step(nc.vector.tensor_tensor(expert_w[:, E:2 * E], bank[5][:, E:2 * E], expert_w[:, 0:E], ALU.mult))
                nc.vector.tensor_tensor(token_w, picked[:, :, 0:E], expert_w[:, E:2 * E].unsqueeze(1).to_broadcast([P, NT, E]),
                                        ALU.mult).then_inc(weights_ready, 1)
                dve.wait_ge(wT_ready, 1)
                for k in range(2):
                    s = nc.vector.tensor_copy(token_wT[0:E, k * 512:(k + 1) * 512], bank[6 + k][0:E, :])
                s.then_inc(wT_sb, 1)
                for q in range(4):
                    dve.wait_ge(bias_mm, q + 1)
                    nc.vector.tensor_copy(acc[:, 2 * q:2 * q + 2, :], bank[q][:, :].rearrange("p (n d) -> p n d", n=2)).then_inc(bias_sb, 1)
                dve.wait_ge(bias_sb, 4)
                with dve.Fori(0, E // 2) as pair:
                    for par in range(2):
                        for n in range(NT):
                            done = par * Y_PER + n
                            dve.wait_ge(y_mm, pair * 2 * Y_PER + done + 1)
                            dve.wait_ge(y_acc, pair * 2 * Y_PER + max(done - NT + 1, 0))
                            nc.vector.scalar_tensor_tensor(acc[:, n, :], bank[4 + n % 4][:, 0:D],
                                                           token_w[:, n, bass.ds(pair * 2 + par, 1)], acc[:, n, :],
                                                           ALU.mult, ALU.add).then_inc(y_acc, 1)
                dve.wait_ge(pool_mm, 1)
                nc.vector.tensor_scalar(pooled, bank[0][:, 0:2 * KD], 1.0 / SEQ, None, ALU.mult).then_inc(pool_sb, 1)
                dve.wait_ge(hid_mm, 1)
                nc.vector.tensor_scalar(hidden, bank[1][:, 0:B], bp1_sb, 0.0, ALU.add, ALU.max).then_inc(hid_sb, 1)
                dve.wait_ge(phi_mm, 1)
                nc.vector.tensor_scalar(phi, bank[2][:, 0:B], bp2_sb, None, ALU.add).then_inc(phi_z, 1)
                dve.wait_ge(phi_exp, 1)
                step(nc.vector.tensor_scalar(phi, phi, 1.0, None, ALU.add))
                step(nc.vector.reciprocal(phi, phi))
                step(nc.vector.tensor_scalar(phi, phi, 0.7, -0.8, ALU.is_gt, ALU.mult))
                step(nc.vector.tensor_scalar(phi, phi, 1.0, None, ALU.add))
                for n in range(NT):
                    nc.vector.scalar_tensor_tensor(resid[:, n, :], acc[:, n, :], phi[:, n // NC:n // NC + 1], resid[:, n, :],
                                                   ALU.mult, ALU.add).then_inc(final, 1)


def kernel(**inputs):
    import concourse.bacc as bacc
    from concourse.bass_utils import run_bass_kernel_spmd

    a = {k.replace("L0_", ""): np.asarray(v) for k, v in inputs.items()}

    def halves(w):
        return w.reshape(KD, P, -1).transpose(1, 0, 2)

    inner = HEADS * P
    wq = a["attn_W_qkv"].reshape(3, HEADS, P, D)
    wg = a["attn_W_g"].reshape(1, HEADS, P, D)
    wall = np.concatenate([wq, wg], 0)
    arrays = {
        "x": a["attn_x"].reshape(TOK, D),
        "wqkvg": wall.transpose(1, 3, 0, 2).reshape(HEADS, KD, P, 4, P).transpose(0, 2, 1, 3, 4),
        "convw": a["attn_conv_w"].reshape(3, HEADS, P, TAPS).transpose(1, 2, 0, 3),
        "wab": halves(a["attn_W_ab"].T),
        "bab": a["attn_b_ab"],
        "wo": a["attn_W_o"].T.reshape(HEADS, P, D),
        "wr": halves(a["ffn_Wr"]),
        "br": a["ffn_br"],
        "w1": a["ffn_w1"],
        "b1": a["ffn_b1"].reshape(E, KI, P).transpose(2, 0, 1),
        "w2": a["ffn_w2"],
        "b2": a["ffn_b2"],
        "wp1": halves(a["ffn_Wp1"]),
        "bp1": a["ffn_bp1"].reshape(P, 1),
        "wp2": a["ffn_Wp2"],
        "bp2": a["ffn_bp2"],
    }
    nc = bacc.Bacc("TRN2", target_bir_lowering=False, num_devices=1)
    args = []
    for name in arrays:
        arrays[name] = np.ascontiguousarray(arrays[name])
        args.append(nc.dram_tensor(f"in_{name}", arrays[name].shape, F32, kind="ExternalInput").ap())
    args.append(nc.dram_tensor("out_y", (TOK, D), F32, kind="ExternalOutput").ap())
    block_kernel(nc, *args)
    r = run_bass_kernel_spmd(nc, [{f"in_{k}": v for k, v in arrays.items()}], core_ids=[0])
    return r.results[0]["out_y"].reshape(B, SEQ, D)
```

```python
from contextlib import ExitStack

import numpy as np

import concourse.bass as bass
from concourse import mybir

F32 = mybir.dt.float32
U32 = mybir.dt.uint32
F32R = mybir.dt.float32r
ALU = mybir.AluOpType
ACT = mybir.ActivationFunctionType
AX = mybir.AxisListType

P = 128
B, SEQ, D = 2, 512, 256
TOK = B * SEQ
NT = TOK // P
NC = SEQ // P
KD = D // P
HEADS = 16
TAPS = 4
HG = 2
GROUPS = HEADS // HG
M = HG * NT
BLK = 32
NB = P // BLK
E, TOPK, I = 12, 3, 640
KI = I // P
LN_EPS = 1e-5
NORM_EPS2 = 1e-24

STREAMS = HG * B
SLOTS = NC * STREAMS
FRONT_STEPS = 7 * HG * B
SUB_STEPS = 2 * (BLK - 1)
SUB_BACK, SUB_OUT = 26, 6
SUB_FRONT = SUB_STEPS - SUB_BACK - SUB_OUT
SUB_SLOT = 4
SUB_TAPS = 7
TURN_AT = 8


def block_kernel(nc, x, wqkvg, convw, wab, bab, wo, wr, br, w1, b1, w2, b2, wp1, bp1, wp2, bp2, out):
    with ExitStack() as ctx:
        def sb(name, shape, dt=F32):
            return ctx.enter_context(nc.sbuf_tensor(name, shape, dt))

        def sem(name):
            return ctx.enter_context(nc.semaphore(name))

        bank = [ctx.enter_context(nc.psum_tensor(f"bank{i}", [P, 512], F32)) for i in range(8)]

        decay_dram = nc.dram_tensor("decay_rows", [HEADS, TOK], F32).ap()
        chunk_decay_dram = nc.dram_tensor("chunk_decay_rows", [HEADS, NT], F32).ap()
        lower_dram = nc.dram_tensor("lower_blocks", [NB, M, BLK, BLK], F32).ap()
        invT_dram = nc.dram_tensor("inverse_blocks_t", [NB, M, BLK, BLK], F32).ap()
        inv_dram = nc.dram_tensor("inverse_blocks", [NB, M, BLK, BLK], F32).ap()

        resid = sb("resid", [P, NT, D])
        normedT = sb("normedT", [P, KD, TOK])
        ident = sb("ident", [P, P])
        ones = sb("ones", [P, P])
        stats = sb("stats", [P, NT, 6])
        mean_var = sb("mean_var", [P, NT, 2])
        rstd = sb("rstd", [P, NT])
        eps_col = sb("eps_col", [P, 1])

        attention_memory = ctx.enter_context(ExitStack())

        def att_sb(name, shape, dt=F32):
            return attention_memory.enter_context(nc.sbuf_tensor(name, shape, dt))

        wab_sb = att_sb("wab_sb", [P, KD, 2 * HEADS])
        bab_sb = att_sb("bab_sb", [P, 2 * HEADS])
        alpha_beta = att_sb("alpha_beta", [P, NT, 2 * HEADS])
        decay_from_start = att_sb("decay_from_start", [P, NT, HEADS])
        neg_decay = att_sb("neg_decay", [P, NT, HEADS])
        chunk_decay = att_sb("chunk_decay", [P, HEADS, NT])

        qT = att_sb("qT", [P, 2, HG, TOK])
        kT = att_sb("kT", [P, 2, HG, TOK])
        gated = att_sb("gated", [P, 2, HG, TOK])
        vk = att_sb("vk", [P, 2, 2, HG, NT, P])
        masks = att_sb("masks", [P, 2, M, 2, P])
        invT = att_sb("invT", [P, M, P])
        inv_low = att_sb("inv_low", [P, M, 64])
        inv64 = inv_low[0:64, :, :]
        inv32 = inv_low[64:96, :, 0:BLK]
        state = att_sb("state", [P, STREAMS, P])
        qk_scales = att_sb("qk_scales", [P, 2, HG, NT, 4])
        w_sb = att_sb("w_sb", [P, 2, KD, 4, P])
        cw_sb = att_sb("cw_sb", [P, 2, 3, TAPS])
        decay_bc = att_sb("decay_bc", [P, B, SEQ])
        wo_sb = att_sb("wo_sb", [P, 2, HG, D])
        conv = att_sb("conv", [P, 3, 512])
        conv_far = att_sb("conv_far", [P, 3, 512])
        vT = att_sb("vT", [P, 2, 512])
        squares = att_sb("squares", [P, 2, 512])
        decayed = att_sb("decayed", [P, NC, P])
        norms = att_sb("norms", [P, 2, 8])
        half = att_sb("half", [P, 8])
        rhs_sb = att_sb("rhs_sb", [P, 2, P])
        y_sb = att_sb("y_sb", [P, 2, P])
        o_sb = att_sb("o_sb", [P, 2, P])
        blocks = att_sb("blocks", [NB * M, 2, BLK, BLK])
        sub_in, sub_inv = blocks[:, 0, :, :], blocks[:, 1, :, :]
        cross = att_sb("cross", [P, M, 64])
        sub_tmp = att_sb("sub_tmp", [P, 256])

        qT_flat = qT[:, :, :, :].rearrange("p s a b -> p (s a b)")
        kT_flat = kT[:, :, :, :].rearrange("p s a b -> p (s a b)")
        alpha_rows, reset_rows, impulse_rows, decay_rows = (qT_flat[0:HEADS, k * TOK:(k + 1) * TOK] for k in range(4))
        chunk_end_rows = kT_flat[0:HEADS, 0:NT]
        normed = gated[:, :, :, :].rearrange("p s h t -> p (s h t)")[:, 0:NT * D].rearrange("p (n d) -> p n d", n=NT)

        def matmul_parts(out, lhs, rhs, first, last):
            for i, (a, b) in enumerate(((0, 0), (0, 1), (1, 0))):
                s = nc.tensor.matmul(out, lhs[a], rhs[b], start=first and i == 0, stop=last and i == 2)
            return s

        def layernorm(dve, step):
            for n in range(NT):
                s = nc.vector.bn_stats(stats[:, n, :], resid[:, n, :])
            step(s)
            for n in range(NT):
                s = nc.vector.bn_aggr(mean_var[:, n, :], stats[:, n, :])
            return s

        def apply_norm(dve, step, normed):
            step(nc.vector.reciprocal(rstd[:, :], rstd[:, :]))
            for n in range(NT):
                s = nc.vector.tensor_scalar(normed[:, n, :], resid[:, n, :], mean_var[:, n, 0:1], rstd[:, n:n + 1],
                                            ALU.subtract, ALU.mult)
            return s

        def wait_alone(eng, what, value):
            value = eng.to_reg(value)
            eng.wait_ge(consts, 9)
            eng.wait_ge(what, value)

        w_in = [sem("w_in_head0"), sem("w_in_head1")]
        decay_in = [sem("decay_in_b0"), sem("decay_in_b1")]
        wo_in = sem("wo_in")
        proj_done = sem("proj_done")
        far_done = sem("far_done")
        near_done = sem("near_done")
        conv_done = sem("conv_done")
        silu_done = sem("silu_done")
        squared = sem("squared")
        sums_done = sem("sums_done")
        sums_read = sem("sums_read")
        rooted = sem("rooted")
        scaled = sem("scaled")
        impulses = sem("impulses")
        turned_v, turned_k = sem("turned_v"), sem("turned_k")
        products = sem("products")
        post_v, post_k, post_m = sem("post_v"), sem("post_k"), sem("post_m")
        blocks_out, blocks_in = sem("blocks_out"), sem("blocks_in")
        cleared = sem("cleared")
        inverted = sem("inverted")
        inverse_t = sem("inverse_t")
        inv_out, inv_in = sem("inv_out"), sem("inv_in")
        merge_mm = sem("merge_mm")
        merge_v, merge_s = sem("merge_v"), sem("merge_s")
        ks_done, rhs_done, y_done, y_copied = sem("ks_done"), sem("rhs_done"), sem("y_done"), sem("y_copied")
        gain_done, inner_done, inner_scaled = sem("gain_done"), sem("inner_done"), sem("inner_scaled")
        o_done, state_done = sem("o_done"), sem("state_done")
        o_turned, o_gated = sem("o_turned"), sem("o_gated")
        wo_done, wo_added = sem("wo_done"), sem("wo_added")
        front_step, sub_step = sem("front_step"), sem("sub_step")

        h_mm, y_mm, y_acc = sem("h_mm"), sem("y_mm"), sem("y_acc")
        w_high, w_split = sem("w_high"), sem("w_split")
        h_relu, h_split = sem("h_relu"), sem("h_split")

        by_group = (proj_done, far_done, near_done, conv_done, silu_done, squared, sums_done, sums_read, rooted, scaled, impulses,
                    turned_v, turned_k, products, post_v, post_k, post_m, cleared, inverted, inverse_t, merge_mm, merge_v, merge_s,
                    ks_done, rhs_done, y_done, y_copied, gain_done, inner_done, inner_scaled, o_done, state_done, o_turned, o_gated,
                    wo_done, wo_added, front_step, sub_step, h_mm, h_relu, h_split, y_mm, y_acc, w_high, w_split)

        def ahead(what):
            return 4 if what is wo_added else 1

        in_x, in_small = sem("in_x"), sem("in_small")
        consts, var_ready, std_ready, normed_ready = sem("consts"), sem("var_ready"), sem("std_ready"), sem("normed_ready")
        turned, turned_sb = sem("turned"), sem("turned_sb")
        ab_ready, ab_z, ab_exp, ab_sig = sem("ab_ready"), sem("ab_z"), sem("ab_exp"), sem("ab_sig")
        rows_ready, rows_sb, decay_cols, chunk_in = sem("rows_ready"), sem("rows_sb"), sem("decay_cols"), sem("chunk_in")
        dram_rows, decay_sb = sem("dram_rows"), sem("decay_sb")
        step1 = sem("step1")

        with nc.Block() as block:
            @block.sync
            def _(sp):
                sp.dma_start(resid[:, :, :], x.rearrange("(n p) d -> p n d", p=P)).then_inc(in_x, 16)
                sp.dma_start(wab_sb[:, :, :], wab).then_inc(in_small, 16)
                sp.dma_start(bab_sb[:, :], bab.partition_broadcast(P)).then_inc(in_small, 16)
                for hh in range(HG):
                    sp.dma_start(w_sb[:, hh, :, :, :], wqkvg[hh]).then_inc(w_in[hh], 16)
                    sp.dma_start(cw_sb[:, hh, :, :], convw[hh]).then_inc(w_in[hh], 16)
                sp.wait_ge(rows_sb, 3)
                sp.dma_start(decay_dram, reset_rows).then_inc(dram_rows, 16)
                sp.dma_start(chunk_decay_dram, chunk_end_rows).then_inc(dram_rows, 16)
                sp.wait_ge(dram_rows, 32)

            @block.gpsimd
            def _(pool):
                nc.gpsimd.memset(ident[:, :], 0.0).then_inc(consts, 1)
                nc.gpsimd.memset(ones[:, :], 1.0).then_inc(consts, 1)
                nc.gpsimd.memset(eps_col[:, :], LN_EPS).then_inc(consts, 1)
                nc.gpsimd.memset(half[:, :], 0.5).then_inc(consts, 1)
                nc.gpsimd.memset(conv_far[:, :, :], 0.0).then_inc(consts, 1)
                nc.gpsimd.memset(invT[:, :, :], 0.0).then_inc(consts, 1)
                nc.gpsimd.memset(inv_low[:, :, :], 0.0).then_inc(consts, 1)
                nc.gpsimd.memset(impulse_rows, 0.0).then_inc(consts, 1)
                pool.wait_ge(consts, 8)
                nc.gpsimd.affine_select(out=ident[:, :], in_=ident[:, :], compare_op=ALU.not_equal, fill=1.0,
                                        base=0, pattern=[[-1, P]], channel_multiplier=1).then_inc(consts, 1)
                for counted in by_group:
                    pool.sem_inc(counted, ahead(counted))

            @block.vector
            def _(dve):
                count = [0]

                def step(ins):
                    count[0] += 1
                    ins.then_inc(step1, 1)
                    dve.wait_ge(step1, count[0])

                dve.wait_ge(in_x, 16)
                layernorm(dve, step).then_inc(var_ready, 1)
                dve.wait_ge(std_ready, 1)
                apply_norm(dve, step, normed).then_inc(normed_ready, 1)
                for k in range(4):
                    dve.wait_ge(turned, k + 1)
                    nc.vector.tensor_copy(normedT[:, k // 2, (k % 2) * 512:(k % 2 + 1) * 512], bank[k][:, :]).then_inc(turned_sb, 1)
                dve.wait_ge(ab_ready, 1)
                dve.wait_ge(in_small, 32)
                nc.vector.tensor_tensor(alpha_beta[:, :, :], bank[4][:, 0:NT * 32].rearrange("p (n h) -> p n h", n=NT),
                                        bab_sb[:, :].unsqueeze(1).to_broadcast([P, NT, 32]), ALU.add).then_inc(ab_z, 1)
                dve.wait_ge(ab_exp, 1)
                step(nc.vector.tensor_scalar(alpha_beta[:, :, :], alpha_beta[:, :, :], 1.0, None, ALU.add))
                nc.vector.reciprocal(alpha_beta[:, :, :], alpha_beta[:, :, :]).then_inc(ab_sig, 1)
                dve.wait_ge(rows_ready, 1)
                for k in range(2):
                    s = nc.vector.tensor_copy(alpha_rows[:, k * 512:(k + 1) * 512], bank[5 + k][0:HEADS, :])
                step(s)
                dve.wait_ge(consts, 9)
                start = lambda v: v.rearrange("h (n t) -> h n t", n=NT)[:, :, 0:1]
                nc.vector.tensor_copy(start(impulse_rows), start(alpha_rows))
                step(nc.vector.tensor_copy(reset_rows, alpha_rows))
                s = nc.vector.memset(start(reset_rows), 0.0)
                s.then_inc(rows_sb, 1)
                dve.wait_ge(rows_sb, 1)
                nc.vector.tensor_tensor_scan(decay_rows, reset_rows, impulse_rows, 0.0, ALU.mult, ALU.add).then_inc(rows_sb, 1)
                dve.wait_ge(rows_sb, 2)
                nc.vector.tensor_copy(chunk_end_rows.unsqueeze(2),
                                      decay_rows.rearrange("h (n t) -> h n t", n=NT)[:, :, P - 1:P]).then_inc(rows_sb, 1)
                dve.wait_ge(decay_cols, 1)
                v = bank[7][:, 0:NT * HEADS].rearrange("p (n h) -> p n h", n=NT)
                nc.vector.tensor_copy(decay_from_start[:, :, :], v)
                nc.vector.tensor_scalar(neg_decay[:, :, :], v, -1.0, None, ALU.mult)

            @block.scalar
            def _(act):
                act.wait_ge(consts, 9)
                act.wait_ge(var_ready, 1)
                nc.scalar.activation(rstd[:, :].unsqueeze(2), mean_var[:, :, 1:2], ACT.Sqrt, bias=eps_col[:, :]).then_inc(std_ready, 1)
                act.wait_ge(ab_z, 1)
                nc.scalar.activation(alpha_beta[:, :, :], alpha_beta[:, :, :], ACT.Exp, scale=-1.0).then_inc(ab_exp, 1)

            @block.tensor
            def _(pe):
                pe.wait_ge(consts, 9)
                pe.wait_ge(normed_ready, 1)
                for k in range(KD):
                    for n in range(NT):
                        b_no = 2 * k + n // 4
                        s = nc.tensor.transpose(bank[b_no][:, (n % 4) * P:(n % 4 + 1) * P], normed[:, n, k * P:(k + 1) * P],
                                                ident[:, :])
                        if n % 4 == 3:
                            s.then_inc(turned, 1)
                pe.wait_ge(turned_sb, 4)
                pe.wait_ge(in_small, 32)
                for n in range(NT):
                    for k in range(KD):
                        s = nc.tensor.matmul(bank[4][:, n * 32:(n + 1) * 32], normedT[:, k, n * P:(n + 1) * P], wab_sb[:, k, :],
                                             start=k == 0, stop=k == KD - 1)
                s.then_inc(ab_ready, 1)
                pe.wait_ge(ab_sig, 1)
                for n in range(NT):
                    s = nc.tensor.transpose(bank[5 + n // 4][0:HEADS, (n % 4) * P:(n % 4 + 1) * P],
                                            alpha_beta[:, n, 0:HEADS], ident[:, :])
                s.then_inc(rows_ready, 1)
                pe.wait_ge(rows_sb, 2)
                for n in range(NT):
                    s = nc.tensor.transpose(bank[7][:, n * HEADS:(n + 1) * HEADS], decay_rows[:, n * P:(n + 1) * P],
                                            ident[0:HEADS, 0:HEADS])
                s.then_inc(decay_cols, 1)

        PAIRS = HG * B
        KS_SLOTS = SLOTS - STREAMS
        LAST = GROUPS - 1

        def until(eng, what, per, g, k, alone=False):
            if isinstance(g, int) and g * per + k <= 0:
                return
            (wait_alone if alone else type(eng).wait_ge)(eng, what, g * per + (k + ahead(what)))

        def tokens(b, c=None):
            return slice(b * SEQ, (b + 1) * SEQ) if c is None else slice(b * SEQ + c * P, b * SEQ + (c + 1) * P)

        def slot(i):
            c, s_no = divmod(i, STREAMS)
            hh, b = divmod(s_no, B)
            return c, s_no, hh, b, hh * NT + b * NC + c

        def blocks_of(v, cols):
            return v.rearrange("p (m t) -> p m t", t=cols)

        with nc.Block() as block:
            @block.sync
            def _(sp):
                def load_w(g, hh):
                    sp.dma_start(w_sb[:, hh, :, :, :], wqkvg[bass.ds(g * HG + hh, 1)].squeeze(0)).then_inc(w_in[hh], 16)
                    sp.dma_start(cw_sb[:, hh, :, :], convw[bass.ds(g * HG + hh, 1)].squeeze(0)).then_inc(w_in[hh], 16)

                def load_decay(g, hh, b):
                    sp.dma_start(decay_bc[:, b, :], decay_dram[bass.ds(g * HG + hh, 1), b * SEQ:(b + 1) * SEQ].squeeze(0)
                                 .partition_broadcast(P)).then_inc(decay_in[b], 16)

                def during_front(g, par, last, sub_g, back_g):
                    for p in range(PAIRS):
                        hh, b = divmod(p, B)
                        if p == 1 and sub_g is not None:
                            after_substitution(sub_g, back_g)
                        if last and hh == HG - 1:
                            break
                        until(sp, post_k, PAIRS, g, p + 1)
                        load_decay(g + (hh + 1) // HG, (hh + 1) % HG, b)
                        if b == B - 1 and not last:
                            until(sp, post_m, 2 * PAIRS, g, 2 * p + 2)
                            load_w(g + 1, hh)
                    until(sp, post_m, 2 * PAIRS, g, 2 * PAIRS)
                    for i in range(NB):
                        sp.dma_start(lower_dram[i].rearrange("m j t -> j m t"),
                                     masks[i * BLK:(i + 1) * BLK, par, :, 0, i * BLK:(i + 1) * BLK]
                                     ).then_inc(blocks_out, 16)
                    sp.wait_ge(blocks_out, g * (16 * NB) + 16 * NB)
                    sp.dma_start(sub_in, lower_dram.rearrange("i m j t -> (i m) j t")).then_inc(blocks_in, 16)

                def after_substitution(g, back_g):
                    until(sp, inverted, 1, g, 1)
                    sp.dma_start(invT_dram.rearrange("i m j t -> (i m) j t"), sub_inv).then_inc(inv_out, 16)
                    until(sp, inverse_t, 1, g, 1)
                    sp.dma_start(inv_dram.rearrange("i m j t -> (i m) j t"), sub_in).then_inc(inv_out, 16)
                    sp.wait_ge(inv_out, g * 32 + 32)
                    until(sp, y_done, SLOTS, back_g, 0)
                    for i in range(NB):
                        sp.dma_start(invT[i * BLK:(i + 1) * BLK, :, i * BLK:(i + 1) * BLK],
                                     invT_dram[i].rearrange("m j t -> j m t")).then_inc(inv_in, 16)
                    for i in range(2):
                        sp.dma_start(inv64[i * BLK:(i + 1) * BLK, :, i * BLK:(i + 1) * BLK],
                                     inv_dram[i].rearrange("m j t -> j m t")).then_inc(inv_in, 16)
                    sp.dma_start(inv32, inv_dram[2].rearrange("m j t -> j m t")).then_inc(inv_in, 16)

                def load_wo(g, par):
                    until(sp, wo_added, 4, g, 0)
                    sp.dma_start(wo_sb[:, par, :, :], wo[bass.ds(g * HG, HG)].rearrange("h e d -> e h d")).then_inc(wo_in, 16)

                load_decay(0, 0, 0)
                load_decay(0, 0, 1)
                sp.dma_start(chunk_decay[:, :, :], chunk_decay_dram.partition_broadcast(P)).then_inc(chunk_in, 16)
                during_front(0, 0, False, None, 0)
                with sp.Fori(0, GROUPS // 2 - 1) as it:
                    for half_no in range(2):
                        g = it * 2 + half_no
                        load_wo(g, half_no)
                        during_front(g + 1, 1 - half_no, False, g, g)
                load_wo(LAST - 1, 0)
                during_front(LAST, 1, True, LAST - 1, LAST - 1)
                after_substitution(LAST, LAST)
                load_wo(LAST, 1)
                sp.wait_ge(inv_in, GROUPS * 112)

            @block.tensor
            def _(pe):
                def front(g, par, back_g, merge_g):
                    def project(p, types):
                        hh, b = divmod(p, B)
                        if b == 0 and types[0] == 0:
                            pe.wait_ge(w_in[hh], g * 32 + 32)
                        for typ in types:
                            if p == 0:
                                until(pe, wo_added, 4, back_g, typ - 3)
                            if typ < 3:
                                until(pe, conv_done, 3 * PAIRS, g, 3 * (p - 1) + typ + 1 if p else 0)
                            else:
                                until(pe, silu_done, 4 * PAIRS, g, 4 * p)
                            for k in range(KD):
                                s = nc.tensor.matmul(bank[typ][:, :], w_sb[:, hh, k, typ, :], normedT[:, k, tokens(b)],
                                                     start=k == 0, stop=k == KD - 1)
                            s.then_inc(proj_done, 1)

                    def sums(p):
                        until(pe, post_k, PAIRS, g, p)
                        for qk in range(2):
                            until(pe, squared, 2 * PAIRS, g, 2 * p + qk + 1)
                            for c in range(NC):
                                s = nc.tensor.matmul(bank[4][:, qk * NC + c:qk * NC + c + 1], squares[:, qk, c * P:(c + 1) * P],
                                                     ones[:, 0:1], start=True, stop=True)
                            s.then_inc(sums_done, 1)

                    def turn_v(p):
                        until(pe, silu_done, 4 * PAIRS, g, 4 * p + 3)
                        until(pe, post_v, PAIRS, g, p)
                        for c in range(NC):
                            s = nc.tensor.transpose(bank[5][:, c * P:(c + 1) * P], vT[:, p % 2, c * P:(c + 1) * P], ident[:, :])
                        s.then_inc(turned_v, 1)

                    def chunk_products(p):
                        hh, b = divmod(p, B)
                        until(pe, silu_done, 4 * PAIRS, g, 4 * p + 2)
                        for c in range(NC):
                            if c % 2 == 0:
                                until(pe, post_m, 2 * PAIRS, g, 2 * (p - 1) + c // 2 + 1 if p else 0)
                            o = bank[6 + c // 2][:, (c % 2) * 2 * P:(c % 2 + 1) * 2 * P]
                            kk = kT[:, par, hh, tokens(b, c)]
                            nc.tensor.matmul(o[:, 0:P], kk, kk, start=True, stop=True)
                            s = nc.tensor.matmul(o[:, P:2 * P], kk, qT[:, par, hh, tokens(b, c)], start=True, stop=True)
                            if c % 2 == 1:
                                s.then_inc(products, 1)

                    def turn_k(p):
                        hh, b = divmod(p, B)
                        until(pe, sums_read, PAIRS, g, p + 1)
                        for c in range(NC):
                            s = nc.tensor.transpose(bank[4][:, c * P:(c + 1) * P], kT[:, par, hh, tokens(b, c)], ident[:, :])
                        s.then_inc(turned_k, 1)

                    for p in range(PAIRS):
                        project(p, (0, 1, 2))
                        if p > 0:
                            sums(p - 1)
                            turn_v(p - 1)
                        project(p, (3,))
                        if p > 0:
                            chunk_products(p - 1)
                            turn_k(p - 1)
                    p = PAIRS - 1
                    merging = merge_g is not None
                    if merging:
                        merge(merge_g, 1 - par, 0, g)
                        merge(merge_g, 1 - par, 1, g)
                    chunk_products(p)
                    sums(p)
                    if merging:
                        merge(merge_g, 1 - par, 2, g)
                    turn_v(p)
                    if merging:
                        merge(merge_g, 1 - par, 3, g)
                    turn_k(p)
                    if merging:
                        merge(merge_g, 1 - par, 4, g)

                def merge(g, par, stage, front_g):
                    if stage == 0:
                        until(pe, conv_done, 3 * PAIRS, front_g, 3 * PAIRS - 2)
                        until(pe, inv_in, 112, g, 112 - 1, alone=True)
                        for m in range(M):
                            s = nc.tensor.matmul(bank[0][32:64, m * BLK:(m + 1) * BLK], masks[0:32, par, m, 0, 32:64], inv64[0:32, m, 0:32],
                                                 start=True, stop=True)
                        s.then_inc(merge_mm, 1)
                    if stage == 1:
                        until(pe, conv_done, 3 * PAIRS, front_g, 3 * PAIRS, alone=True)
                        for m in range(M):
                            s = nc.tensor.matmul(bank[2][96:128, m * BLK:(m + 1) * BLK], masks[64:96, par, m, 0, 96:128], inv32[:, m, :],
                                                 start=True, stop=True)
                        s.then_inc(merge_mm, 1)
                    if stage == 2:
                        until(pe, silu_done, 4 * PAIRS, front_g, 4 * PAIRS, alone=True)
                        until(pe, merge_v, 5, g, 1, alone=True)
                        for m in range(M):
                            w = slice(m * BLK, (m + 1) * BLK)
                            nc.tensor.matmul(bank[1][32:64, w], invT[32:64, m, 32:64], cross[32:64, m, 0:32], start=True, stop=True)
                            s = nc.tensor.matmul(bank[3][0:32, w], cross[32:64, m, 0:32], invT[32:64, m, 32:64], start=True, stop=True)
                        s.then_inc(merge_mm, 1)
                        until(pe, merge_s, 4, g, 1, alone=True)
                        for m in range(M):
                            s = nc.tensor.matmul(bank[0][64:96, m * BLK:(m + 1) * BLK], cross[96:128, m, 0:32], invT[96:128, m, 96:128],
                                                 start=True, stop=True)
                        s.then_inc(merge_mm, 1)
                    if stage == 3:
                        until(pe, merge_s, 4, g, 2, alone=True)
                        for e in range(2):
                            for m in range(e * 8, e * 8 + 8):
                                s = nc.tensor.matmul(bank[1 + e][64:128, (m % 8) * 64:(m % 8 + 1) * 64], masks[0:64, par, m, 0, 64:128],
                                                     inv64[0:64, m, :], start=True, stop=True)
                            s.then_inc(merge_mm, 1)
                    if stage == 4:
                        for e in range(2):
                            until(pe, merge_v, 5, g, 4, alone=True)
                            if e == 1:
                                until(pe, merge_s, 4, g, 3, alone=True)
                            for m in range(e * 8, e * 8 + 8):
                                s = nc.tensor.matmul(bank[(3, 0)[e]][0:64, (m % 8) * 64:(m % 8 + 1) * 64], cross[64:128, m, :],
                                                     invT[64:128, m, 64:128], start=True, stop=True)
                            s.then_inc(merge_mm, 1)

                def back(g, par, front_g):
                    def output_read(j):
                        if j < STREAMS:
                            until(pe, inner_scaled, SLOTS, g, j + 1)
                        else:
                            until(pe, o_done, KS_SLOTS, g, j - STREAMS + 1)

                    for i in range(SLOTS + 3):
                        if STREAMS <= i < SLOTS:
                            c, s_no, hh, b, m = slot(i)
                            until(pe, state_done, KS_SLOTS, g, i - STREAMS + 1)
                            until(pe, y_copied, SLOTS, g, i - 2)
                            nc.tensor.matmul(bank[i % 3][:, 0:P], kT[:, par, hh, tokens(b, c)], state[:, s_no, :],
                                             start=True, stop=True).then_inc(ks_done, 1)
                        if 1 <= i <= SLOTS:
                            j = i - 1
                            c, s_no, hh, b, m = slot(j)
                            if j == 0:
                                until(pe, post_k, PAIRS, front_g, PAIRS)
                                until(pe, post_v, PAIRS, front_g, PAIRS)
                                until(pe, merge_v, 5, g, 5)
                                until(pe, merge_s, 4, g, 4)
                            if c == 0:
                                if j >= 3:
                                    until(pe, y_copied, SLOTS, g, j - 2)
                                rhs = vk[:, par, 0, hh, b * NC, :]
                            else:
                                until(pe, rhs_done, KS_SLOTS, g, j - STREAMS + 1)
                                rhs = rhs_sb[:, j % 2, :]
                            nc.tensor.matmul(bank[j % 3][:, 0:P], invT[:, m, :], rhs, start=True, stop=True).then_inc(y_done, 1)
                        if 2 <= i <= SLOTS + 1:
                            j = i - 2
                            c, s_no, hh, b, m = slot(j)
                            bk = bank[3 + j % 2]
                            if j >= 2:
                                output_read(j - 2)
                            if c > 0:
                                nc.tensor.matmul(bk[:, P:2 * P], qT[:, par, hh, tokens(b, c)], state[:, s_no, :],
                                                 start=True, stop=True)
                            until(pe, y_copied, SLOTS, g, j + 1)
                            if c < NC - 1:
                                until(pe, state_done, KS_SLOTS, g, j)
                                nc.tensor.matmul(bank[5][:, 0:P], vk[:, par, 1, hh, b * NC + c, :], y_sb[:, j % 2, :],
                                                 start=True, stop=True).then_inc(gain_done, 1)
                            nc.tensor.matmul(bk[:, 0:P], masks[:, par, m, 1, :], y_sb[:, j % 2, :],
                                             start=True, stop=True).then_inc(inner_done, 1)
                        if 3 <= i:
                            j = i - 3
                            output_read(j)
                            if j % 4 == 0:
                                until(pe, o_gated, NC, g, max(j // 4 - 1, 0))
                            nc.tensor.transpose(bank[6 + (j // 4) % 2][:, (j % 4) * P:(j % 4 + 1) * P], o_sb[:, j % 2, :],
                                                ident[:, :]).then_inc(o_turned, 1)

                    pe.wait_ge(wo_in, g * 16 + 16)
                    until(pe, o_gated, NC, g, NC)
                    for n in range(NT):
                        for hh in range(HG):
                            s = nc.tensor.matmul(bank[n // 2][:, (n % 2) * D:(n % 2 + 1) * D], gated[:, par, hh, n * P:(n + 1) * P],
                                                 wo_sb[:, par, hh, :], start=hh == 0, stop=hh == HG - 1)
                        if n % 2:
                            s.then_inc(wo_done, 1)

                front(0, 0, 0, None)
                with pe.Fori(0, GROUPS // 2 - 1) as it:
                    for half_no in range(2):
                        g = it * 2 + half_no
                        front(g + 1, 1 - half_no, g, g)
                        back(g, half_no, g + 1)
                front(LAST, 1, LAST - 1, LAST - 1)
                back(LAST - 1, 0, LAST)
                until(pe, wo_added, 4, LAST, 0)
                for stage in range(5):
                    merge(LAST, 1, stage, LAST)
                back(LAST, 1, LAST)

            @block.scalar
            def _(act):
                def turn_inverse(g):
                    until(act, inverted, 1, g, 1)
                    nc.scalar.copy(sub_in, sub_inv.rearrange("p a b -> p b a")).then_inc(inverse_t, 1)

                def merge(g, stage):
                    if stage == 0:
                        until(act, merge_mm, 8, g, 2)
                        nc.scalar.mul(cross[96:128, :, 0:32], blocks_of(bank[2][96:128, :], 32), -1.0).then_inc(merge_s, 1)
                    if stage == 1:
                        until(act, merge_mm, 8, g, 3)
                        nc.scalar.copy(inv64[32:64, :, 0:32], blocks_of(bank[1][32:64, :], 32)).then_inc(merge_s, 1)
                    if stage == 2:
                        until(act, merge_mm, 8, g, 6)
                        nc.scalar.mul(cross[64:128, 8:16, :], blocks_of(bank[2][64:128, :], 64), -1.0).then_inc(merge_s, 1)
                    if stage == 3:
                        until(act, merge_mm, 8, g, 8)
                        nc.scalar.copy(invT[0:64, 8:16, 64:128], blocks_of(bank[0][0:64, :], 64)).then_inc(merge_s, 1)

                def front(g, par, sub_g):
                    def outer_taps(u):
                        p, typ = divmod(u, 3)
                        hh, b = divmod(p, B)
                        if b == 0 and typ == 0:
                            act.wait_ge(w_in[hh], g * 32 + 32)
                        until(act, proj_done, 4 * PAIRS, g, 4 * p + typ + 1)
                        until(act, silu_done, 4 * PAIRS, g, (u - 3) // 3 * 4 + typ + 1 if u >= 3 else 0)
                        nc.scalar.activation(conv[:, typ, :], bank[typ][:, :], ACT.Copy,
                                             scale=cw_sb[:, hh, typ, 3:4]).then_inc(far_done, 1)
                        until(act, near_done, 3 * PAIRS, g, max(u - 2, 0))
                        nc.scalar.activation(conv_far[:, typ, 3:512], bank[typ][:, 0:509], ACT.Copy,
                                             scale=cw_sb[:, hh, typ, 0:1]).then_inc(far_done, 1)

                    def silu(u):
                        p, typ = divmod(u, 3)
                        hh, b = divmod(p, B)
                        until(act, conv_done, 3 * PAIRS, g, u + 1)
                        if typ == 2:
                            until(act, turned_v, PAIRS, g, max(p - 1, 0))
                        dst = (qT[:, par, hh, tokens(b)], kT[:, par, hh, tokens(b)], vT[:, p % 2, :])[typ]
                        nc.scalar.activation(dst, conv[:, typ, :], ACT.Silu).then_inc(silu_done, 1)
                        if typ == 2:
                            until(act, proj_done, 4 * PAIRS, g, 4 * p + 4)
                            nc.scalar.activation(gated[:, par, hh, tokens(b)], bank[3][:, :], ACT.Silu).then_inc(silu_done, 1)

                    def square(p, qk):
                        hh, b = divmod(p, B)
                        until(act, silu_done, 4 * PAIRS, g, 4 * p + qk + 1)
                        until(act, sums_done, 2 * PAIRS, g, max(2 * (p - 1) + qk + 1, 0))
                        nc.scalar.activation(squares[:, qk, :], (qT, kT)[qk][:, par, hh, tokens(b)], ACT.Square).then_inc(squared, 1)

                    def scaled_v(p):
                        hh, b = divmod(p, B)
                        until(act, rooted, PAIRS, g, p + 1)
                        until(act, turned_v, PAIRS, g, p + 1)
                        for c in range(NC):
                            s = nc.scalar.activation(vk[:, par, 0, hh, b * NC + c, :], bank[5][:, c * P:(c + 1) * P], ACT.Copy,
                                                     scale=norms[:, 1, NC + c:NC + c + 1])
                        s.then_inc(post_v, 1)

                    for u in range(3 * PAIRS + 2):
                        if u < 3 * PAIRS:
                            outer_taps(u)
                        if u >= 2:
                            p, typ = divmod(u - 2, 3)
                            if typ > 0:
                                square(p, typ - 1)
                            silu(u - 2)
                            if typ == 2 and p > 0:
                                scaled_v(p - 1)
                        if u == TURN_AT and sub_g is not None:
                            turn_inverse(sub_g)
                    if sub_g is not None:
                        merge(sub_g, 0)
                        merge(sub_g, 1)
                    scaled_v(PAIRS - 1)
                    if sub_g is not None:
                        merge(sub_g, 2)
                        merge(sub_g, 3)

                def back(g, par):
                    def inner(i):
                        c, s_no, hh, b, m = slot(i)
                        until(act, inner_done, SLOTS, g, i + 1)
                        until(act, o_turned, SLOTS, g, max(i - 1, 0))
                        nc.scalar.activation(o_sb[:, i % 2, :], bank[3 + i % 2][:, 0:P], ACT.Copy,
                                             scale=qk_scales[:, par, hh, b * NC + c, 1:2]).then_inc(inner_scaled, 1)

                    for i in range(SLOTS + 1):
                        if i < SLOTS:
                            until(act, y_done, SLOTS, g, i + 1)
                            until(act, inner_done, SLOTS, g, max(i - 1, 0))
                            nc.scalar.copy(y_sb[:, i % 2, :], bank[i % 3][:, 0:P]).then_inc(y_copied, 1)
                        if i > 0:
                            inner(i - 1)

                front(0, 0, None)
                with act.Fori(0, GROUPS // 2 - 1) as it:
                    for half_no in range(2):
                        g = it * 2 + half_no
                        front(g + 1, 1 - half_no, g)
                        back(g, half_no)
                front(LAST, 1, LAST - 1)
                back(LAST - 1, 0)
                turn_inverse(LAST)
                for stage in range(4):
                    merge(LAST, stage)
                back(LAST, 1)

            @block.gpsimd
            def _(pool):
                def front(g, par):
                    def add_outer(u):
                        typ = u % 3
                        until(pool, far_done, 6 * PAIRS, g, 2 * u + 2)
                        nc.gpsimd.tensor_tensor(conv[:, typ, :], conv[:, typ, :], conv_far[:, typ, :],
                                                ALU.add).then_inc(near_done, 1)

                    def roots(p):
                        until(pool, sums_read, PAIRS, g, p + 1)
                        until(pool, post_v, PAIRS, g, p)
                        nc.gpsimd.tensor_tensor(norms[:, 1, :], norms[:, 0, :], half[:, :], ALU.pow).then_inc(rooted, 1)

                    def impulse(p):
                        hh, b = divmod(p, B)
                        until(pool, scaled, PAIRS, g, p + 1)
                        until(pool, post_k, PAIRS, g, p)
                        nc.gpsimd.tensor_tensor(decayed[:, :, :], ident[:, :].unsqueeze(1).to_broadcast([P, NC, P]),
                                                qk_scales[:, par, hh, b * NC:(b + 1) * NC, 3:4].to_broadcast([P, NC, P]),
                                                ALU.mult).then_inc(impulses, 1)

                    for p in range(PAIRS):
                        add_outer(3 * p)
                        add_outer(3 * p + 1)
                        if p > 0:
                            impulse(p - 1)
                        add_outer(3 * p + 2)
                        if p > 0:
                            roots(p - 1)
                    impulse(PAIRS - 1)
                    roots(PAIRS - 1)
                    if not isinstance(g, int) or g > 0:
                        wait_alone(pool, inv_out, g * 32)
                    nc.gpsimd.memset(sub_inv, 0.0).then_inc(cleared, 1)
                    until(pool, cleared, 2, g, 1, alone=True)
                    nc.gpsimd.memset(sub_inv.rearrange("p a b -> p (a b)")[:, 0:BLK * BLK:BLK + 1], 1.0).then_inc(cleared, 1)

                front(0, 0)
                with pool.Fori(0, GROUPS // 2 - 1) as it:
                    for half_no in range(2):
                        front(it * 2 + (half_no + 1), 1 - half_no)
                front(LAST, 1)

            @block.vector
            def _(dve):
                def substitute(g, k):
                    s, part = divmod(k, 2)
                    rows_n, cols = s + 1, BLK - 1 - s
                    tmp = sub_tmp[0:NB * M, 0:rows_n * cols].rearrange("p (a b) -> p a b", a=rows_n)
                    rest = sub_inv[:, 0:rows_n, s + 1:BLK]
                    if k == 0:
                        dve.wait_ge(blocks_in, g * 16 + 16)
                        until(dve, cleared, 2, g, 2)
                    else:
                        until(dve, sub_step, SUB_STEPS - 1, g, k)
                    if part == 0:
                        ins = nc.vector.tensor_tensor(tmp, sub_inv[:, 0:rows_n, s:s + 1].to_broadcast([NB * M, rows_n, cols]),
                                                      sub_in[:, s:s + 1, s + 1:BLK].to_broadcast([NB * M, rows_n, cols]), ALU.mult)
                    else:
                        ins = nc.vector.tensor_tensor(rest, rest, tmp, ALU.subtract)
                    ins.then_inc(*((sub_step, 1) if k < SUB_STEPS - 1 else (inverted, 1)))

                def merge(g, stage):
                    if stage == 0:
                        until(dve, merge_mm, 8, g, 1)
                        nc.vector.tensor_scalar(cross[32:64, :, 0:32], blocks_of(bank[0][32:64, :], 32), -1.0, None, ALU.mult).then_inc(merge_v, 1)
                    if stage == 1:
                        until(dve, merge_mm, 8, g, 3)
                        nc.vector.tensor_copy(invT[0:32, :, 32:64], blocks_of(bank[3][0:32, :], 32)).then_inc(merge_v, 1)
                    if stage == 2:
                        until(dve, merge_mm, 8, g, 4)
                        nc.vector.tensor_copy(invT[64:96, :, 96:128], blocks_of(bank[0][64:96, :], 32)).then_inc(merge_v, 1)
                    if stage == 3:
                        until(dve, merge_mm, 8, g, 5)
                        nc.vector.tensor_scalar(cross[64:128, 0:8, :], blocks_of(bank[1][64:128, :], 64), -1.0, None, ALU.mult).then_inc(merge_v, 1)
                    if stage == 4:
                        until(dve, merge_mm, 8, g, 7)
                        nc.vector.tensor_copy(invT[0:64, 0:8, 64:128], blocks_of(bank[3][0:64, :], 64)).then_inc(merge_v, 1)

                def front(g, par, sub_g):
                    count = [0]

                    def step(ins):
                        count[0] += 1
                        ins.then_inc(front_step, 1)
                        until(dve, front_step, FRONT_STEPS, g, count[0])

                    def inner_taps(u):
                        p, typ = divmod(u, 3)
                        hh, b = divmod(p, B)
                        until(dve, near_done, 3 * PAIRS, g, u + 1)
                        step(nc.vector.scalar_tensor_tensor(conv[:, typ, 1:512], bank[typ][:, 0:511],
                                                            cw_sb[:, hh, typ, 2:3], conv[:, typ, 1:512],
                                                            ALU.mult, ALU.add))
                        nc.vector.scalar_tensor_tensor(conv[:, typ, 2:512], bank[typ][:, 0:510],
                                                       cw_sb[:, hh, typ, 1:2], conv[:, typ, 2:512],
                                                       ALU.mult, ALU.add).then_inc(conv_done, 1)

                    def scales(p):
                        hh, b = divmod(p, B)
                        sc = qk_scales[:, par, hh, b * NC:(b + 1) * NC, :]
                        until(dve, sums_done, 2 * PAIRS, g, 2 * p + 2)
                        nc.vector.tensor_scalar(norms[:, 0, :], bank[4][:, 0:8], NORM_EPS2, None, ALU.max).then_inc(sums_read, 1)
                        until(dve, sums_read, PAIRS, g, p + 1)
                        step(nc.vector.reciprocal(sc[:, :, 3:4], norms[:, 0, NC:2 * NC].unsqueeze(2)))
                        nc.vector.tensor_tensor(sc[:, :, 3:4], sc[:, :, 3:4],
                                                alpha_beta[:, b * NC:(b + 1) * NC, bass.ds(g * HG + (HEADS + hh), 1)],
                                                ALU.mult).then_inc(scaled, 1)

                    def over_q(p):
                        hh, b = divmod(p, B)
                        sc = qk_scales[:, par, hh, b * NC:(b + 1) * NC, :]
                        until(dve, rooted, PAIRS, g, p + 1)
                        step(nc.vector.reciprocal(sc[:, :, 1:2], norms[:, 1, 0:NC].unsqueeze(2)))
                        step(nc.vector.tensor_tensor(sc[:, :, 2:3], sc[:, :, 1:2],
                                                     decay_from_start[:, b * NC:(b + 1) * NC, bass.ds(g * HG + hh, 1)], ALU.mult))

                    def chunk_mats(p):
                        hh, b = divmod(p, B)
                        until(dve, impulses, PAIRS, g, p + 1)
                        dve.wait_ge(decay_in[b], g * (16 * HG) + 16 * (hh + 1))
                        step(nc.vector.tensor_tensor_scan(decayed[:, :, :].rearrange("p c t -> p (c t)"), decay_bc[:, b, :],
                                                          decayed[:, :, :].rearrange("p c t -> p (c t)"), 0.0, ALU.mult, ALU.add))
                        for c2 in range(2):
                            until(dve, products, 2 * PAIRS, g, 2 * p + c2 + 1)
                            m = hh * NT + b * NC + 2 * c2
                            nc.vector.tensor_tensor(masks[:, par, m:m + 2, :, :],
                                                    bank[6 + c2][:, :].rearrange("p (c a t) -> p c a t", c=2, a=2),
                                                    decayed[:, 2 * c2:2 * c2 + 2, :].unsqueeze(2).to_broadcast([P, 2, 2, P]),
                                                    ALU.mult).then_inc(post_m, 1)
                        until(dve, turned_k, PAIRS, g, p + 1)
                        nc.vector.tensor_tensor(vk[:, par, 1, hh, b * NC:(b + 1) * NC, :],
                                                bank[4][:, :].rearrange("p (c e) -> p c e", c=NC),
                                                decayed[:, :, P - 1:P].to_broadcast([P, NC, P]), ALU.mult).then_inc(post_k, 1)

                    def substitute_some(place):
                        if sub_g is not None and place < SUB_TAPS:
                            for k in range(SUB_STEPS - SUB_FRONT + place * SUB_FRONT // SUB_TAPS,
                                           SUB_STEPS - SUB_FRONT + (place + 1) * SUB_FRONT // SUB_TAPS):
                                substitute(sub_g, k)

                    for p in range(PAIRS):
                        inner_taps(3 * p)
                        substitute_some(3 * p)
                        if p > 0:
                            scales(p - 1)
                        inner_taps(3 * p + 1)
                        substitute_some(3 * p + 1)
                        inner_taps(3 * p + 2)
                        substitute_some(3 * p + 2)
                        if p > 0:
                            chunk_mats(p - 1)
                            over_q(p - 1)
                    p = PAIRS - 1
                    merging = sub_g is not None
                    if merging:
                        merge(sub_g, 0)
                    scales(p)
                    if merging:
                        merge(sub_g, 1)
                        merge(sub_g, 2)
                    if merging:
                        merge(sub_g, 3)
                    chunk_mats(p)
                    over_q(p)
                    if merging:
                        merge(sub_g, 4)
                    assert count[0] == FRONT_STEPS, count[0]

                def back(g, par, sub_g, among):
                    def right_side(i):
                        c, s_no, hh, b, m = slot(i)
                        n = b * NC + c
                        until(dve, ks_done, KS_SLOTS, g, i - STREAMS + 1)
                        until(dve, y_done, SLOTS, g, i - 1)
                        nc.vector.scalar_tensor_tensor(rhs_sb[:, i % 2, :], bank[i % 3][:, 0:P],
                                                       neg_decay[:, n, bass.ds(g * HG + hh, 1)], vk[:, par, 0, hh, n, :],
                                                       ALU.mult, ALU.add).then_inc(rhs_done, 1)

                    def gain(i):
                        c, s_no, hh, b, m = slot(i)
                        until(dve, gain_done, KS_SLOTS, g, i + 1)
                        if c == 0:
                            nc.vector.tensor_copy(state[:, s_no, :], bank[5][:, 0:P]).then_inc(state_done, 1)
                        else:
                            nc.vector.scalar_tensor_tensor(state[:, s_no, :], state[:, s_no, :],
                                                           chunk_decay[:, bass.ds(g * HG + hh, 1), b * NC + c], bank[5][:, 0:P],
                                                           ALU.mult, ALU.add).then_inc(state_done, 1)

                    def outputs(i):
                        c, s_no, hh, b, m = slot(i)
                        until(dve, inner_scaled, SLOTS, g, i + 1)
                        nc.vector.scalar_tensor_tensor(o_sb[:, i % 2, :], bank[3 + i % 2][:, P:2 * P],
                                                       qk_scales[:, par, hh, b * NC + c, 2:3], o_sb[:, i % 2, :],
                                                       ALU.mult, ALU.add).then_inc(o_done, 1)

                    def gate(c):
                        until(dve, o_turned, SLOTS, g, 4 * c + 4)
                        v = gated[:, par, :, :].rearrange("p h (b t) -> p h b t", b=B)[:, :, :, c * P:(c + 1) * P]
                        nc.vector.tensor_tensor(v, v, bank[6 + c % 2][:, :].rearrange("p (h b t) -> p h b t", h=HG, b=B),
                                                ALU.mult).then_inc(o_gated, 1)

                    for i in range(SLOTS + 3):
                        if STREAMS <= i < SLOTS:
                            right_side(i)
                        if 2 <= i < KS_SLOTS + 2:
                            gain(i - 2)
                        if STREAMS + 2 <= i <= SLOTS + 1:
                            outputs(i - 2)
                        if i >= 6 and (i - 6) % 4 == 0:
                            gate((i - 6) // 4)
                        if sub_g is not None and SUB_SLOT <= i < SLOTS:
                            for k in range((i - SUB_SLOT) * among // (SLOTS - SUB_SLOT),
                                           (i - SUB_SLOT + 1) * among // (SLOTS - SUB_SLOT)):
                                substitute(sub_g, k)

                    for q in range(4):
                        until(dve, wo_done, 4, g, q + 1)
                        nc.vector.tensor_tensor(resid[:, 2 * q:2 * q + 2, :], resid[:, 2 * q:2 * q + 2, :],
                                                bank[q][:, :].rearrange("p (n d) -> p n d", n=2), ALU.add).then_inc(wo_added, 1)
                    if sub_g is not None:
                        for k in range(among, min(among + SUB_OUT, SUB_STEPS)):
                            substitute(sub_g, k)

                front(0, 0, None)
                dve.wait_ge(chunk_in, 16)
                for k in range(SUB_STEPS - SUB_FRONT):
                    substitute(0, k)
                with dve.Fori(0, GROUPS // 2 - 1) as it:
                    for half_no in range(2):
                        g = it * 2 + half_no
                        front(g + 1, 1 - half_no, g)
                        back(g, half_no, g + 1, SUB_BACK)
                front(LAST, 1, LAST - 1)
                back(LAST - 1, 0, LAST, SUB_STEPS)
                for stage in range(5):
                    merge(LAST, stage)
                back(LAST, 1, None, 0)

        attention_memory.close()

        def moe_sb(name, shape, dt=F32):
            return sb(name, shape, dt)[tuple(slice(None) for _ in shape)]

        acc = moe_sb("acc", [P, NT, D])
        normed_x = moe_sb("normed_x", [P, NT, D])
        w1_raw, w2_raw = ([moe_sb(f"{w}_raw{par}", shape) for par in range(2)] for w, shape in (("w1", [P, KD, I]), ("w2", [P, KI, D])))
        w1_sb, w2_sb = ([[moe_sb(f"{w}_{part}{par}", shape, F32R) for part in ("high", "low")] for par in range(2)]
                        for w, shape in (("w1", [P, KD, I]), ("w2", [P, KI, D])))
        hT = [[moe_sb(f"hT_{part}{par}", [P, KI, SEQ], F32R) for part in ("high", "low")] for par in range(2)]
        h_raw = moe_sb("h_raw", [P, 4, SEQ])
        x_parts = [moe_sb(f"x_{part}", [P, KD, TOK], F32R) for part in ("high", "low")]
        wr_sb, br_sb = moe_sb("wr_sb", [P, KD, E]), moe_sb("br_sb", [P, E])
        b1_sb, b2_sb = moe_sb("b1_sb", [P, E, KI]), moe_sb("b2_sb", [P, D])
        wp1_sb, bp1_sb, wp2_sb, bp2_sb = moe_sb("wp1_sb", [P, KD, P]), moe_sb("bp1_sb", [P, 1]), moe_sb("wp2_sb", [P, 1]), moe_sb("bp2_sb", [P, 1])
        wp2_bc = moe_sb("wp2_bc", [P, P])
        expert_no = moe_sb("expert_no", [P, E])
        logits, probs = moe_sb("logits", [P, NT, E]), moe_sb("probs", [P, NT, E])
        row_max, row_sum, row_inv = moe_sb("row_max", [P, NT]), moe_sb("row_sum", [P, NT]), moe_sb("row_inv", [P, NT])
        top8, top_no, top_w = moe_sb("top8", [P, NT, 8]), moe_sb("top_no", [P, NT, 8]), moe_sb("top_w", [P, NT, TOPK])
        top_idx = moe_sb("top_idx", [P, NT, 8], U32)
        top_sum = moe_sb("top_sum", [P, NT])
        picked = moe_sb("picked", [P, NT, 2 * E])
        pick_one = moe_sb("pick_one", [P, NT, E])
        pick_sum, expert_w = moe_sb("pick_sum", [P, 2 * E]), moe_sb("expert_w", [P, 2 * E])
        token_w = moe_sb("token_w", [P, NT, E])
        token_wT = moe_sb("token_wT", [P, TOK])
        pooled, hidden, phi = moe_sb("pooled", [P, 2 * KD]), moe_sb("hidden", [P, B]), moe_sb("phi", [P, B])

        e_small = sem("e_small")
        w1_in, w2_in = [sem("w1_in_even"), sem("w1_in_odd")], [sem("w2_in_even"), sem("w2_in_odd")]
        var3, std3, normed3, turned3, turned_sb3 = sem("var3"), sem("std3"), sem("normed3"), sem("turned3"), sem("turned_sb3")
        logits_ready, shifted, exped, top_shift, top_exp = sem("logits_ready"), sem("shifted"), sem("exped"), sem("top_shift"), sem("top_exp")
        picks, pick_sums, weights_ready, wT_ready, wT_sb = sem("picks"), sem("pick_sums"), sem("weights_ready"), sem("wT_ready"), sem("wT_sb")
        bias_mm, bias_sb = sem("bias_mm"), sem("bias_sb")
        expert_no_ready = sem("expert_no_ready")
        x_high, x_split = sem("x_high"), sem("x_split")
        pool_mm, pool_sb, hid_mm, hid_sb, phi_mm, phi_z, phi_exp = (sem("pool_mm"), sem("pool_sb"), sem("hid_mm"), sem("hid_sb"),
                                                                    sem("phi_mm"), sem("phi_z"), sem("phi_exp"))
        final, stored = sem("final"), sem("stored")
        step3 = sem("step3")
        UNITS, PAIR_UNITS = 2 * E, 4
        H_PER, Y_PER = KI, NC
        LAST_PAIR = E // 2 - 1
        BATCH_THEN_HALF = [(b, k) for b in range(B) for k in range(KD)]

        with nc.Block() as block:
            @block.sync
            def _(sp):
                def load_expert(pair, par):
                    e = pair * 2 + par
                    until(sp, w_split, 2, e - 1, -1)
                    sp.dma_start(w1_raw[par], w1[bass.ds(e, 1)].squeeze(0).rearrange("(k p) i -> p k i", p=P)).then_inc(w1_in[par], 16)
                    until(sp, w_split, 2, e - 1, 0)
                    sp.dma_start(w2_raw[par], w2[bass.ds(e, 1)].squeeze(0).rearrange("(k p) d -> p k d", p=P)).then_inc(w2_in[par], 16)

                small_loads = [(wr_sb, wr), (br_sb, br.partition_broadcast(P)), (b1_sb, b1), (b2_sb[0:E, :], b2),
                               (wp1_sb, wp1), (bp1_sb, bp1), (wp2_sb, wp2), (bp2_sb, bp2.partition_broadcast(P))]
                for i, (dst, src) in enumerate(small_loads):
                    sp.dma_start(dst, src).then_inc(e_small, 16)
                    if i == 2:
                        load_expert(0, 0)
                load_expert(0, 1)
                with sp.Fori(1, E // 2) as pair:
                    for par in range(2):
                        load_expert(pair, par)
                sp.wait_ge(final, NT)
                sp.dma_start(out.rearrange("(n p) d -> p n d", p=P), resid[:, :, :]).then_inc(stored, 16)
                sp.wait_ge(stored, 16)

            @block.gpsimd
            def _(pool):
                def high_parts(pair, par):
                    until(pool, h_mm, 2 * H_PER, pair * 2 + par - 1, 0, alone=True)
                    wait_alone(pool, w1_in[par], pair * 16 + 16)
                    nc.gpsimd.tensor_copy(w1_sb[par][0], w1_raw[par]).then_inc(w_high, 1)
                    until(pool, y_mm, 2 * Y_PER, pair * 2 + par - 1, 0, alone=True)
                    wait_alone(pool, w2_in[par], pair * 16 + 16)
                    nc.gpsimd.tensor_copy(w2_sb[par][0], w2_raw[par]).then_inc(w_high, 1)

                nc.gpsimd.iota(expert_no, pattern=[[1, E]], base=0, channel_multiplier=0,
                               allow_small_or_imprecise_dtypes=True).then_inc(expert_no_ready, 1)
                pool.wait_ge(w1_in[0], 16)
                nc.gpsimd.tensor_copy(w1_sb[0][0], w1_raw[0]).then_inc(w_high, 1)
                for i, (b, k) in enumerate(BATCH_THEN_HALF):
                    pool.wait_ge(turned_sb3, i + 1)
                    pool.wait_ge(x_high, i + 1)
                    nc.gpsimd.tensor_tensor(x_parts[1][:, k, tokens(b)], normedT[:, k, tokens(b)], x_parts[0][:, k, tokens(b)],
                                            ALU.subtract).then_inc(x_split, 1)
                pool.wait_ge(w2_in[0], 16)
                nc.gpsimd.tensor_copy(w2_sb[0][0], w2_raw[0]).then_inc(w_high, 1)
                high_parts(0, 1)
                with pool.Fori(1, E // 2) as pair:
                    for par in range(2):
                        high_parts(pair, par)

            @block.scalar
            def _(act):
                act.wait_ge(var3, 1)
                nc.scalar.activation(rstd[:, :].unsqueeze(2), mean_var[:, :, 1:2], ACT.Sqrt, bias=eps_col[:, :]).then_inc(std3, 1)
                for i, (b, k) in enumerate(BATCH_THEN_HALF):
                    act.wait_ge(turned_sb3, i + 1)
                    nc.scalar.copy(x_parts[0][:, k, tokens(b)], bank[2 * k + b][:, :]).then_inc(x_high, 1)
                act.wait_ge(shifted, 1)
                nc.scalar.activation(probs, logits, ACT.Exp).then_inc(exped, 1)
                act.wait_ge(top_shift, 1)
                nc.scalar.activation(top_w, top_w, ACT.Exp).then_inc(top_exp, 1)
                def hidden_units(pair, q):
                    for k in range(KI):
                        until(act, h_split, PAIR_UNITS * H_PER, pair, max(q * H_PER + k - 3, 0), alone=True)
                        until(act, h_mm, PAIR_UNITS * H_PER, pair, q * H_PER + k + 1, alone=True)
                        nc.scalar.activation(h_raw[:, (q * KI + k) % 4, :], bank[(q * KI + k) % 4][:, :], ACT.Relu,
                                             bias=b1_sb[:, bass.ds(pair * 2 + q // 2, 1), k])
                        nc.scalar.activation(hT[q % 2][0][:, k, :], bank[(q * KI + k) % 4][:, :], ACT.Relu,
                                             bias=b1_sb[:, bass.ds(pair * 2 + q // 2, 1), k]).then_inc(h_relu, 1)

                act.wait_ge(e_small, 128)
                with act.Fori(0, E // 2) as pair:
                    for q in range(PAIR_UNITS):
                        hidden_units(pair, q)
                act.wait_ge(phi_z, 1)
                nc.scalar.activation(phi, phi, ACT.Exp, scale=-1.0).then_inc(phi_exp, 1)

            @block.tensor
            def _(pe):
                def first_product(pair, q):
                    until(pe, w_split, 4, pair, 2 * (q // 2) + 1)
                    for k in range(KI):
                        until(pe, h_relu, PAIR_UNITS * H_PER, pair, max(q * H_PER + k - 3, 0))
                        for kd in range(KD):
                            s = matmul_parts(bank[(q * KI + k) % 4][:, :], [w[:, kd, k * P:(k + 1) * P] for w in w1_sb[q // 2]],
                                             [x[:, kd, tokens(q % 2)] for x in x_parts], kd == 0, kd == KD - 1)
                        s.then_inc(h_mm, 1)

                def second_product(pair, q):
                    until(pe, w_split, 4, pair, 2 * (q // 2) + 2)
                    until(pe, h_split, PAIR_UNITS * H_PER, pair, (q + 1) * H_PER)
                    for n in range(NC):
                        until(pe, y_acc, PAIR_UNITS * Y_PER, pair, max(q * Y_PER + n - 3, 0))
                        for k in range(KI):
                            s = matmul_parts(bank[4 + n][:, 0:D], [h[:, k, n * P:(n + 1) * P] for h in hT[q % 2]],
                                             [w[:, k, :] for w in w2_sb[q // 2]], k == 0, k == KI - 1)
                        s.then_inc(y_mm, 1)

                pe.wait_ge(normed3, 1)
                for b, k in BATCH_THEN_HALF:
                    for n in range(b * NC, (b + 1) * NC):
                        b_no = 2 * k + b
                        s = nc.tensor.transpose(bank[b_no][:, (n % 4) * P:(n % 4 + 1) * P], normed_x[:, n, k * P:(k + 1) * P],
                                                ident[:, :])
                        if n % 4 == 3:
                            s.then_inc(turned3, 1)
                pe.wait_ge(turned_sb3, 4)
                pe.wait_ge(e_small, 128)
                for n in range(NT):
                    for k in range(KD):
                        s = nc.tensor.matmul(bank[4][:, n * E:(n + 1) * E], normedT[:, k, n * P:(n + 1) * P], wr_sb[:, k, :],
                                             start=k == 0, stop=k == KD - 1)
                s.then_inc(logits_ready, 1)
                pe.wait_ge(x_split, 2)
                pe.wait_ge(x_high, 4)
                first_product(0, 0)
                pe.wait_ge(picks, 1)
                nc.tensor.matmul(bank[5][:, 0:2 * E], ones[:, :], pick_sum, start=True, stop=True).then_inc(pick_sums, 1)
                pe.wait_ge(x_split, 4)
                first_product(0, 1)
                pe.wait_ge(weights_ready, 1)
                for n in range(NT):
                    s = nc.tensor.transpose(bank[6 + n // 4][0:E, (n % 4) * P:(n % 4 + 1) * P], token_w[:, n, :], ident[:, :])
                s.then_inc(wT_ready, 1)
                pe.wait_ge(wT_sb, 1)
                for n in range(NT):
                    s = nc.tensor.matmul(bank[4 + n // 2][:, (n % 2) * D:(n % 2 + 1) * D], token_wT[0:E, n * P:(n + 1) * P], b2_sb[0:E, :],
                                         start=True, stop=True)
                    if n % 2:
                        s.then_inc(bias_mm, 1)
                pe.wait_ge(bias_sb, 4)
                with pe.Fori(0, LAST_PAIR) as pair:
                    for q in range(PAIR_UNITS):
                        second_product(pair, q)
                        first_product(pair + (q + 2) // PAIR_UNITS, (q + 2) % PAIR_UNITS)
                for q in range(PAIR_UNITS):
                    second_product(LAST_PAIR, q)
                    if q < PAIR_UNITS - 2:
                        first_product(LAST_PAIR, q + 2)
                until(pe, y_acc, Y_PER, UNITS, 0)
                for k in range(KD):
                    for b in range(B):
                        for c in range(NC):
                            s = nc.tensor.matmul(bank[0][:, k * B + b:k * B + b + 1], acc[:, b * NC + c, k * P:(k + 1) * P], ones[:, 0:1],
                                                 start=c == 0, stop=c == NC - 1)
                s.then_inc(pool_mm, 1)
                pe.wait_ge(pool_sb, 1)
                for k in range(KD):
                    s = nc.tensor.matmul(bank[1][:, 0:B], wp1_sb[:, k, :], pooled[:, k * B:(k + 1) * B], start=k == 0, stop=k == KD - 1)
                s.then_inc(hid_mm, 1)
                pe.wait_ge(hid_sb, 1)
                nc.tensor.matmul(bank[2][:, 0:B], wp2_bc, hidden, start=True, stop=True).then_inc(phi_mm, 1)

            @block.vector
            def _(dve):
                count = [0]

                def low_part(low, whole, high):
                    return nc.vector.tensor_tensor(low, whole, high, ALU.subtract)

                def weights(pair, par, which):
                    until(dve, w_high, 4, pair, 2 * par + which + 1)
                    low_part((w1_sb, w2_sb)[which][par][1], (w1_raw, w2_raw)[which][par], (w1_sb, w2_sb)[which][par][0]).then_inc(w_split, 1)

                def hidden_units(pair, q):
                    for k in range(KI):
                        until(dve, h_relu, PAIR_UNITS * H_PER, pair, q * H_PER + k + 1)
                        low_part(hT[q % 2][1][:, k, :], h_raw[:, (q * KI + k) % 4, :], hT[q % 2][0][:, k, :]).then_inc(h_split, 1)

                def accumulate(pair, q):
                    for n in range(NC):
                        done = q * Y_PER + n
                        until(dve, y_mm, PAIR_UNITS * Y_PER, pair, done + 1)
                        until(dve, y_acc, PAIR_UNITS * Y_PER, pair, max(done - NT + 1, 0))
                        row = (q % 2) * NC + n
                        nc.vector.scalar_tensor_tensor(acc[:, row, :], bank[4 + n][:, 0:D],
                                                       token_w[:, row, bass.ds(pair * 2 + q // 2, 1)], acc[:, row, :],
                                                       ALU.mult, ALU.add).then_inc(y_acc, 1)

                def step(ins):
                    count[0] += 1
                    ins.then_inc(step3, 1)
                    dve.wait_ge(step3, count[0])

                layernorm(dve, step).then_inc(var3, 1)
                dve.wait_ge(std3, 1)
                apply_norm(dve, step, normed_x).then_inc(normed3, 1)
                for i, (b, k) in enumerate(BATCH_THEN_HALF):
                    dve.wait_ge(turned3, i + 1)
                    nc.vector.tensor_copy(normedT[:, k, tokens(b)], bank[2 * k + b][:, :]).then_inc(turned_sb3, 1)
                weights(0, 0, 0)
                dve.wait_ge(e_small, 128)
                nc.vector.tensor_copy(wp2_bc, wp2_sb.to_broadcast([P, P]))
                dve.wait_ge(logits_ready, 1)
                step(nc.vector.tensor_tensor(logits, bank[4][:, 0:NT * E].rearrange("p (n e) -> p n e", n=NT),
                                             br_sb.unsqueeze(1).to_broadcast([P, NT, E]), ALU.add))
                step(nc.vector.tensor_reduce(row_max, logits, AX.X, ALU.max))
                nc.vector.tensor_tensor(logits, logits, row_max.unsqueeze(2).to_broadcast([P, NT, E]), ALU.subtract).then_inc(shifted, 1)
                dve.wait_ge(exped, 1)
                step(nc.vector.tensor_reduce(row_sum, probs, AX.X, ALU.add))
                step(nc.vector.reciprocal(row_inv, row_sum))
                step(nc.vector.tensor_tensor(probs, probs, row_inv.unsqueeze(2).to_broadcast([P, NT, E]), ALU.mult))
                for n in range(NT):
                    s = nc.vector.max(top8[:, n, :], probs[:, n, :])
                step(s)
                for n in range(NT):
                    s = nc.vector.max_index(top_idx[:, n, :], top8[:, n, :], probs[:, n, :])
                step(s)
                nc.vector.tensor_copy(top_no, top_idx[:, :, :])
                nc.vector.tensor_tensor(top_w, top8[:, :, 0:TOPK], top8[:, :, 0:1].to_broadcast([P, NT, TOPK]), ALU.subtract).then_inc(top_shift, 1)
                dve.wait_ge(top_exp, 1)
                step(nc.vector.tensor_reduce(top_sum, top_w, AX.X, ALU.add))
                step(nc.vector.reciprocal(top_sum, top_sum))
                step(nc.vector.tensor_tensor(top_w, top_w, top_sum.unsqueeze(2).to_broadcast([P, NT, TOPK]), ALU.mult))
                dve.wait_ge(expert_no_ready, 1)
                for k in range(TOPK):
                    one = pick_one if k else picked[:, :, 0:E]
                    step(nc.vector.tensor_tensor(one, expert_no.unsqueeze(1).to_broadcast([P, NT, E]),
                                                 top_no[:, :, k:k + 1].to_broadcast([P, NT, E]), ALU.is_equal))
                    if k:
                        step(nc.vector.tensor_tensor(picked[:, :, 0:E], picked[:, :, 0:E], pick_one, ALU.add))
                        step(nc.vector.tensor_tensor(pick_one, pick_one, top_w[:, :, k:k + 1].to_broadcast([P, NT, E]), ALU.mult))
                        step(nc.vector.tensor_tensor(picked[:, :, E:2 * E], picked[:, :, E:2 * E], pick_one, ALU.add))
                    else:
                        step(nc.vector.tensor_tensor(picked[:, :, E:2 * E], one, top_w[:, :, 0:1].to_broadcast([P, NT, E]), ALU.mult))
                nc.vector.tensor_reduce(pick_sum, picked.rearrange("p n e -> p e n"), AX.X, ALU.add).then_inc(picks, 1)
                hidden_units(0, 0)
                weights(0, 0, 1)
                dve.wait_ge(pick_sums, 1)
                step(nc.vector.tensor_scalar(expert_w[:, 0:E], bank[5][:, 0:E], 1.0, None, ALU.max))
                step(nc.vector.reciprocal(expert_w[:, 0:E], expert_w[:, 0:E]))
                step(nc.vector.tensor_tensor(expert_w[:, E:2 * E], bank[5][:, E:2 * E], expert_w[:, 0:E], ALU.mult))
                nc.vector.tensor_tensor(token_w, picked[:, :, 0:E], expert_w[:, E:2 * E].unsqueeze(1).to_broadcast([P, NT, E]),
                                        ALU.mult).then_inc(weights_ready, 1)
                hidden_units(0, 1)
                dve.wait_ge(wT_ready, 1)
                for k in range(2):
                    s = nc.vector.tensor_copy(token_wT[0:E, k * 512:(k + 1) * 512], bank[6 + k][0:E, :])
                s.then_inc(wT_sb, 1)
                for q in range(4):
                    dve.wait_ge(bias_mm, q + 1)
                    nc.vector.tensor_copy(acc[:, 2 * q:2 * q + 2, :], bank[4 + q][:, :].rearrange("p (n d) -> p n d", n=2)).then_inc(bias_sb, 1)
                dve.wait_ge(bias_sb, 4)
                with dve.Fori(0, LAST_PAIR) as pair:
                    for q in range(PAIR_UNITS):
                        weights(pair + (q // 2 + 1) // 2, (q // 2 + 1) % 2, q % 2)
                        accumulate(pair, q)
                        hidden_units(pair + (q + 2) // PAIR_UNITS, (q + 2) % PAIR_UNITS)
                for q in range(PAIR_UNITS):
                    if q < 2:
                        weights(LAST_PAIR, 1, q)
                    accumulate(LAST_PAIR, q)
                    if q < PAIR_UNITS - 2:
                        hidden_units(LAST_PAIR, q + 2)
                dve.wait_ge(pool_mm, 1)
                nc.vector.tensor_scalar(pooled, bank[0][:, 0:2 * KD], 1.0 / SEQ, None, ALU.mult).then_inc(pool_sb, 1)
                dve.wait_ge(hid_mm, 1)
                nc.vector.tensor_scalar(hidden, bank[1][:, 0:B], bp1_sb, 0.0, ALU.add, ALU.max).then_inc(hid_sb, 1)
                dve.wait_ge(phi_mm, 1)
                nc.vector.tensor_scalar(phi, bank[2][:, 0:B], bp2_sb, None, ALU.add).then_inc(phi_z, 1)
                dve.wait_ge(phi_exp, 1)
                step(nc.vector.tensor_scalar(phi, phi, 1.0, None, ALU.add))
                step(nc.vector.reciprocal(phi, phi))
                step(nc.vector.tensor_scalar(phi, phi, 0.7, -0.8, ALU.is_gt, ALU.mult))
                step(nc.vector.tensor_scalar(phi, phi, 1.0, None, ALU.add))
                for n in range(NT):
                    nc.vector.scalar_tensor_tensor(resid[:, n, :], acc[:, n, :], phi[:, n // NC:n // NC + 1], resid[:, n, :],
                                                   ALU.mult, ALU.add).then_inc(final, 1)


def kernel(**inputs):
    import concourse.bacc as bacc
    from concourse.bass_utils import run_bass_kernel_spmd

    a = {k.replace("L0_", ""): np.asarray(v) for k, v in inputs.items()}

    def halves(w):
        return w.reshape(KD, P, -1).transpose(1, 0, 2)

    inner = HEADS * P
    wq = a["attn_W_qkv"].reshape(3, HEADS, P, D)
    wg = a["attn_W_g"].reshape(1, HEADS, P, D)
    wall = np.concatenate([wq, wg], 0)
    arrays = {
        "x": a["attn_x"].reshape(TOK, D),
        "wqkvg": wall.transpose(1, 3, 0, 2).reshape(HEADS, KD, P, 4, P).transpose(0, 2, 1, 3, 4),
        "convw": a["attn_conv_w"].reshape(3, HEADS, P, TAPS).transpose(1, 2, 0, 3),
        "wab": halves(a["attn_W_ab"].T),
        "bab": a["attn_b_ab"],
        "wo": a["attn_W_o"].T.reshape(HEADS, P, D),
        "wr": halves(a["ffn_Wr"]),
        "br": a["ffn_br"],
        "w1": a["ffn_w1"],
        "b1": a["ffn_b1"].reshape(E, KI, P).transpose(2, 0, 1),
        "w2": a["ffn_w2"],
        "b2": a["ffn_b2"],
        "wp1": halves(a["ffn_Wp1"]),
        "bp1": a["ffn_bp1"].reshape(P, 1),
        "wp2": a["ffn_Wp2"],
        "bp2": a["ffn_bp2"],
    }
    nc = bacc.Bacc("TRN2", target_bir_lowering=False, num_devices=1)
    args = []
    for name in arrays:
        arrays[name] = np.ascontiguousarray(arrays[name])
        args.append(nc.dram_tensor(f"in_{name}", arrays[name].shape, F32, kind="ExternalInput").ap())
    args.append(nc.dram_tensor("out_y", (TOK, D), F32, kind="ExternalOutput").ap())
    block_kernel(nc, *args)
    r = run_bass_kernel_spmd(nc, [{f"in_{k}": v for k, v in arrays.items()}], core_ids=[0])
    return r.results[0]["out_y"].reshape(B, SEQ, D)
```
